# Optimizing a Trainium2 kernel written in Bass

```python
import numpy as np
import jax
import jax.numpy as jnp

def _softmax(x, axis=-1):
    return jax.nn.softmax(x, axis=axis)

def _gelu(x):
    return jax.nn.gelu(x, approximate=True)

def _silu(x):
    return jax.nn.silu(x)

def _sigmoid(x):
    return jax.nn.sigmoid(x)

def _layernorm(x, axis=-1, eps=1e-05):
    m = jnp.mean(x, axis=axis, keepdims=True)
    v = jnp.var(x, axis=axis, keepdims=True)
    return (x - m) / jnp.sqrt(v + eps)

def _scatter_add(tgt, idx, src, axis=0):
    return tgt.at[idx].add(src)

def _segment_sum(src, seg, n):
    return jax.ops.segment_sum(src, seg, n)
kernel_name = 'mk_adaln_d1_jaxref_r8_361d2b'

def setup_inputs(seed: int=0):
    np.random.seed(seed)
    _w = jnp.asarray

    def _L0_attn_setup():
        import jax, jax.numpy as jnp
        import numpy as np
        import math
        B, T, E = (2, 256, 256)
        G, QPG, D = (4, 4, 128)

        def sinusoidal_pe(t, d, dtype):
            pos = jnp.arange(t, dtype=jnp.float32)[:, None]
            i = jnp.arange(0, d, 2, dtype=jnp.float32)
            inv_freq = jnp.exp(-(jnp.log(10000.0) * i / d))
            ang = pos * inv_freq
            pe = jnp.zeros((t, d), dtype=jnp.float32)
            pe = pe.at[:, 0::2].set(jnp.sin(ang)).at[:, 1::2].set(jnp.cos(ang))
            return pe.astype(dtype)
        key = jax.random.key(seed)
        ks = jax.random.split(key, 6)
        s = lambda fan_in: 1.0 / math.sqrt(fan_in)
        return {'x': jax.random.normal(ks[0], (B, T, E), dtype=jnp.float32), 'wq': jax.random.uniform(ks[1], (E, G * QPG * D), jnp.float32, -s(E), s(E)), 'bq': jax.random.uniform(ks[2], (G * QPG * D,), jnp.float32, -s(E), s(E)), 'wkv': jax.random.uniform(ks[3], (E, 2 * G * D), jnp.float32, -s(E), s(E)), 'bkv': jax.random.uniform(ks[4], (2 * G * D,), jnp.float32, -s(E), s(E)), 'wo': jax.random.uniform(ks[5], (G * QPG * D, E), jnp.float32, -s(G * QPG * D), s(G * QPG * D))}
    _L0_attn_in = _L0_attn_setup()

    def _L0_ffn_setup():
        import jax, jax.numpy as jnp
        import numpy as np
        NUM_EXPERTS_PER_TOK = 2
        key = jax.random.key(seed)
        k1, k2, k3, k4 = jax.random.split(key, 4)
        B, S, D, O, E = (4, 256, 256, 256, 8)
        x = jax.random.normal(k1, (B, S, D), dtype=jnp.float32)
        gate_w = jax.random.normal(k2, (E, D), dtype=jnp.float32) * (1.0 / np.sqrt(D))
        expert_w = jax.random.normal(k3, (E, O, D), dtype=jnp.float32) * (1.0 / np.sqrt(D))
        expert_b = jax.random.normal(k4, (E, O), dtype=jnp.float32) * 0.01
        return {'x': x, 'gate_w': gate_w, 'expert_w': expert_w, 'expert_b': expert_b}
    _L0_ffn_in = _L0_ffn_setup()
    _L0_c = _w((lambda *s: np.random.randn(*s).astype(np.float32) * 0.05)(2, 256))
    _L0_wmod = _w((lambda *s: np.random.randn(*s).astype(np.float32) * 0.05)(256, 6 * 256) * 256 ** (-0.5))
    _d = {'L0_attn_x': _L0_attn_in['x'], 'L0_attn_wq': _L0_attn_in['wq'], 'L0_attn_bq': _L0_attn_in['bq'], 'L0_attn_wkv': _L0_attn_in['wkv'], 'L0_attn_bkv': _L0_attn_in['bkv'], 'L0_attn_wo': _L0_attn_in['wo'], 'L0_ffn_gate_w': _L0_ffn_in['gate_w'], 'L0_ffn_expert_w': _L0_ffn_in['expert_w'], 'L0_ffn_expert_b': _L0_ffn_in['expert_b'], 'L0_c': _L0_c, 'L0_wmod': _L0_wmod}
    _x0 = _d['L0_attn_x']
    _d['L0_attn_x'] = jax.random.normal(jax.random.fold_in(jax.random.key(seed), 1), (2, 1024, 256), dtype=_x0.dtype)
    del _x0
    return _d

def reference(L0_attn_x, L0_attn_wq, L0_attn_bq, L0_attn_wkv, L0_attn_bkv, L0_attn_wo, L0_ffn_gate_w, L0_ffn_expert_w, L0_ffn_expert_b, L0_c, L0_wmod):

    def _L0_attn_ref(x, wq, bq, wkv, bkv, wo):
        import jax, jax.numpy as jnp
        import numpy as np
        import math
        B, T, E = (2, 256, 256)
        G, QPG, D = (4, 4, 128)

        def sinusoidal_pe(t, d, dtype):
            pos = jnp.arange(t, dtype=jnp.float32)[:, None]
            i = jnp.arange(0, d, 2, dtype=jnp.float32)
            inv_freq = jnp.exp(-(jnp.log(10000.0) * i / d))
            ang = pos * inv_freq
            pe = jnp.zeros((t, d), dtype=jnp.float32)
            pe = pe.at[:, 0::2].set(jnp.sin(ang)).at[:, 1::2].set(jnp.cos(ang))
            return pe.astype(dtype)
        b, t, e = x.shape
        q = (x @ wq + bq).reshape(b, t, G, QPG, D).transpose(0, 2, 3, 1, 4)
        kv = (x @ wkv + bkv).reshape(b, t, G, 1, 2 * D).transpose(0, 2, 3, 1, 4)
        k, v = (kv[..., :D], kv[..., D:])
        pe = sinusoidal_pe(t, D, x.dtype)
        q = q + pe
        k = k + pe
        scores = jnp.einsum('bgqtd,bgksd->bgqts', q, k) / math.sqrt(D)
        causal = jnp.tril(jnp.ones((t, t), dtype=bool))
        scores = jnp.where(causal, scores, -jnp.inf)
        probs = jax.nn.softmax(scores, axis=-1)
        out = jnp.einsum('bgqts,bgksd->btgqd', probs, v).reshape(b, t, G * QPG * D)
        return out @ wo

    def _L0_ffn_ref(x, gate_w, expert_w, expert_b):
        import jax, jax.numpy as jnp
        import numpy as np
        NUM_EXPERTS_PER_TOK = 2
        B, S, D = x.shape
        xf = x.reshape(B * S, D)
        gate_logits = xf @ gate_w.T
        top_vals, top_idx = jax.lax.top_k(gate_logits, NUM_EXPERTS_PER_TOK)
        w = jax.nn.softmax(top_vals.astype(jnp.float32), axis=-1).astype(x.dtype)
        y_all = jnp.einsum('td,eod->teo', xf, expert_w) + expert_b[None, :, :]
        y_sel = jnp.take_along_axis(y_all, top_idx[:, :, None], axis=1)
        out = jnp.sum(y_sel * w[:, :, None], axis=1)
        return out.reshape(B, S, -1)
    x = L0_attn_x
    mod = (_silu(L0_c) @ L0_wmod).reshape(L0_c.shape[0], 6, 1, -1)
    sa, ca, ga, sb, cb, gb = (mod[:, 0], mod[:, 1], mod[:, 2], mod[:, 3], mod[:, 4], mod[:, 5])
    ga = (2 * (ga >= 0) - 1) * jnp.maximum(jnp.abs(ga), 0.25)
    gb = (2 * (gb >= 0) - 1) * jnp.maximum(jnp.abs(gb), 0.25)
    h = _layernorm(x, axis=-1) * (1 + ca) + sa
    x = x + ga * _L0_attn_ref(h, L0_attn_wq, L0_attn_bq, L0_attn_wkv, L0_attn_bkv, L0_attn_wo)
    h = _layernorm(x, axis=-1) * (1 + cb) + sb
    x = x + gb * _L0_ffn_ref(h, L0_ffn_gate_w, L0_ffn_expert_w, L0_ffn_expert_b)
    return x

_drawn_inputs = setup_inputs


def setup_inputs(seed=0):
    import zlib

    import numpy as np

    out = dict(_drawn_inputs(seed))
    spreads = {}
    factors = {'L0_attn_wq': 6.173,
     'L0_attn_bq': 8.0,
     'L0_attn_wkv': 3.393,
     'L0_attn_bkv': 5.693,
     'L0_attn_wo': 3.031,
     'L0_ffn_expert_b': 38.134}
    for name, (base, spread) in spreads.items():
        noise = np.random.default_rng([zlib.crc32(name.encode()), seed]).standard_normal(out[name].shape)
        drawn = base * np.exp(spread * noise) if base else spread * noise
        out[name] = jnp.asarray(drawn.astype(out[name].dtype))
    for name, factor in factors.items():
        out[name] = (out[name] * factor).astype(out[name].dtype)
    return out
```

```python
from contextlib import ExitStack

import numpy as np

import concourse.bass as bass
from concourse import mybir

F32 = mybir.dt.float32
F32R = mybir.dt.float32r
BF16 = mybir.dt.bfloat16
U32 = mybir.dt.uint32
ALU = mybir.AluOpType
ACT = mybir.ActivationFunctionType
AXIS_X = mybir.AxisListType.X

P = 128
B, T, E = 2, 1024, 256
G, QPG, D = 4, 4, 128
HEADS = G * QPG
KE = E // P
NT = T // P
CH = 512
NC = T // CH
TPC = CH // P
EXPERTS, O = 8, 256
EPS = 1e-5
SCALE = float(1.0 / np.sqrt(np.float32(D)))
MASKED = -3.0e38
FREE = 2
SA, CA, GA, SB, CB, GB = range(6)

STEPS = [(c, j) for c in range(NC) for j in range((c + 1) * TPC)]
NS = len(STEPS)
PT = 3
LAG = 2
LAST_STEP = [max(q for q in range(NS) if STEPS[q][0] == c) for c in range(NC)]
PIECES = []
for _i in range(NT):
    _w = (_i + 1) * P
    if _w <= CH:
        PIECES.append((_i, 0, max(_w, 2 * P), True))
    else:
        _a = CH if _w - CH >= 2 * P else _w - 2 * P
        PIECES += [(_i, 0, _a, False), (_i, _a, _w - _a, True)]
assert len(PIECES) == NS
FIRST_PIECE = [next(q for q in range(NS) if PIECES[q][0] == i) for i in range(NT)]


def score_offset(i):
    w = (i + 1) * P
    return CH - PIECES[FIRST_PIECE[i]][2] if w > CH else 0


def prob_offset(i):
    return P * i * (i + 1) // 2


PROBS = prob_offset(NT)


def position_table():
    f = np.float32
    pos = np.arange(T, dtype=f)[:, None]
    i = np.arange(0, D, 2, dtype=f)
    inv_freq = np.exp(-(np.log(f(10000.0)) * i / f(D))).astype(f)
    ang = (pos * inv_freq).astype(f)
    pe = np.zeros((T, D), f)
    pe[:, 0::2] = np.sin(ang)
    pe[:, 1::2] = np.cos(ang)
    return np.ascontiguousarray(pe.T)


def adaln_block(nc, x, wq, bq, wkv, bkv, wo, gate_w, expert_w, expert_b, c_in, wmod, out):
    ctx = ExitStack()
    with ctx:
        def sem(name):
            return ctx.enter_context(nc.semaphore(name))

        top = [-(-nc.sbuf_base // 64) * 64]

        def at(name, shape, dt, offset):
            return nc.alloc_sbuf_tensor_at(name, shape, dt, offset=offset)

        def sb(name, shape, dt=F32):
            size = int(np.prod(shape[1:])) * (2 if dt == BF16 else 4)
            offset = top[0]
            top[0] = -(-(offset + size) // 32) * 32
            assert top[0] <= nc.sbuf_usable_end, (name, top[0], nc.sbuf_usable_end)
            return at(name, shape, dt, offset)

        def here():
            return top[0]

        h_hi = sb("h_hi", [P, KE, B * T], F32R)
        h_lo = sb("h_lo", [P, KE, B * T], F32R)
        kv_at = here()
        k_hi = sb("k_hi", [P, G, T], F32R)
        k_lo = sb("k_lo", [P, G, T], F32R)
        v_hi = sb("v_hi", [P, NT, G, D], F32R)
        v_lo = sb("v_lo", [P, NT, G, D], F32R)
        acc_at = here()
        acc = sb("acc", [P, B * NT, E])
        p_at = here()
        probs = [sb(f"probs{i}", [P, PROBS]) for i in range(2)]
        pt_hi = sb("pt_hi", [P, PT, CH], F32R)
        pt_lo = sb("pt_lo", [P, PT, CH], F32R)
        pz_hi = sb("pz_hi", [P, 2 * P], F32R)
        pz_lo = sb("pz_lo", [P, 2 * P], F32R)
        q_hi = [sb(f"q_hi{i}", [P, T], F32R) for i in range(2)]
        q_lo = [sb(f"q_lo{i}", [P, T], F32R) for i in range(2)]
        raw = sb("raw", [P, 2, CH])
        o_hi = [sb(f"o_hi{c}", [P, CH], F32R) for c in range(NC)]
        o_lo = [sb(f"o_lo{c}", [P, CH], F32R) for c in range(NC)]
        wq_raw = sb("wq_raw", [P, KE, D])
        wq_hi = [sb(f"wq_hi{i}", [P, KE, D], F32R) for i in range(2)]
        wq_lo = [sb(f"wq_lo{i}", [P, KE, D], F32R) for i in range(2)]
        wo_raw = sb("wo_raw", [P, E])
        wo_hi = [sb(f"wo_hi{i}", [P, E], F32R) for i in range(2)]
        wo_lo = [sb(f"wo_lo{i}", [P, E], F32R) for i in range(2)]
        pos = sb("pos", [P, T])
        v_bias = sb("v_bias", [P, CH])
        ident = sb("ident", [P, P])
        ident_bf = sb("ident_bf", [P, P], BF16)
        mask_bf = sb("mask_bf", [P, P], BF16)
        qk_bias = sb("qk_bias", [P, HEADS + G])
        silu_c = sb("silu_c", [P, KE, B])
        modt = sb("modt", [P, 4, KE, B])
        gate_t = sb("gate_t", [P, KE, EXPERTS])
        neg_half = sb("neg_half", [P, B * NT])
        neg_max = sb("neg_max", [P, 2, NT])
        sums = sb("sums", [P, 2, NT])
        rsum = sb("rsum", [P, 2, NT])
        iota8 = sb("iota8", [P, EXPERTS])

        xs = acc
        wmod_sb = at("wmod_sb", [P, KE, 6 * E], F32, kv_at)
        bias_rows = at("bias_rows", [HEADS + G, D], F32, kv_at + 16384)
        c_rows = at("c_rows", [B, E], F32, kv_at + 17408)
        gate_rows = at("gate_rows", [EXPERTS, E], F32, kv_at + 18432)
        vb_row = at("vb_row", [1, CH], F32, kv_at + 20480)
        stats = at("stats", [P, B * NT, 6], F32, kv_at + 22528)
        mv = at("mv", [P, B * NT, 2], F32, kv_at + 23040)
        var_eps = at("var_eps", [P, B * NT], F32, kv_at + 23296)
        rstd = at("rstd", [P, B * NT], F32, kv_at + 23424)
        ones_row = at("ones_row", [1, P], F32, kv_at + 23616)
        sig_tmp = at("sig_tmp", [P, 3, KE * B], F32, kv_at + 23552)
        wkv_hi = at("wkv_hi", [P, KE, 2 * G * D], F32R, p_at)
        wkv_lo = at("wkv_lo", [P, KE, 2 * G * D], F32R, p_at + 8192)
        wkv_raw = [at("wkv_raw0", [P, KE, 2 * G * D], F32, p_at + 4 * PROBS),
                   at("wkv_raw1", [P, KE, 2 * G * D], F32, acc_at + 8192)]
        moe_top = [kv_at]

        def moe(name, shape, dt=F32):
            offset = moe_top[0]
            moe_top[0] += -(-int(np.prod(shape[1:])) * 4 // 32) * 32
            assert moe_top[0] <= acc_at
            return at(name, shape, dt, offset)

        we_raw = moe("we_raw", [P, EXPERTS, KE, E])
        we_hi = moe("we_hi", [P, KE, EXPERTS, O], F32R)
        we_lo = moe("we_lo", [P, KE, EXPERTS, O], F32R)
        ebias = moe("ebias", [EXPERTS, O])
        gmod_w = moe("gmod_w", [P, KE, 2, E])
        moe_top2 = [p_at]

        def moe2(name, shape, dt=F32):
            offset = moe_top2[0]
            moe_top2[0] += -(-int(np.prod(shape[1:])) * 4 // 32) * 32
            assert moe_top2[0] <= p_at + 8 * PROBS
            return at(name, shape, dt, offset)

        silu_b = moe("silu_b", [P, KE, B, P])
        g_sign = moe("g_sign", [P, B, 2, E])
        g_size = moe("g_size", [P, B, 2, E])
        gmod = moe2("gmod", [P, B, 2, E])
        xin = moe2("xin", [P, 2, E])
        xn2 = moe2("xn2", [P, 2, E])
        h2 = moe2("h2", [P, 2, KE, P])
        h2_hi = [moe2(f"h2_hi{i}", [P, KE, P], F32R) for i in range(2)]
        h2_lo = [moe2(f"h2_lo{i}", [P, KE, P], F32R) for i in range(2)]
        y_bias = moe2("y_bias", [P, 2, O])
        y_even = moe2("y_even", [P, 2, O])
        y_odd = moe2("y_odd", [P, 2, O])
        y_sum = moe2("y_sum", [P, 2, O])
        y_out = moe2("y_out", [P, 2, O])
        st2 = moe2("st2", [P, 2, 6])
        mv2 = moe2("mv2", [P, 2, 2])
        ve2 = moe2("ve2", [P, 2, 1])
        rs2 = moe2("rs2", [P, 2, 1])
        logits = moe2("logits", [P, 2, EXPERTS])
        top_v = moe2("top_v", [P, 2, 8])
        top_i = moe2("top_i", [P, 2, 8], U32)
        top_f = moe2("top_f", [P, 2, 2])
        gap = moe2("gap", [P, 2, 1])
        egap = moe2("egap", [P, 2, 1])
        wsum = moe2("wsum", [P, 2, 1])
        wtop = moe2("wtop", [P, 2, 2])
        coef1 = moe2("coef1", [P, 2, EXPERTS])
        coef2 = moe2("coef2", [P, 2, EXPERTS])
        coef = moe2("coef", [P, 2, EXPERTS])
        coef_t = moe2("coef_t", [EXPERTS, 2, P])

        ps_s = ctx.enter_context(nc.psum_tensor("ps_s", [P, 2, T], F32))
        ps_t = ctx.enter_context(nc.psum_tensor("ps_t", [P, 2, CH], F32))
        ps_o = ctx.enter_context(nc.psum_tensor("ps_o", [P, CH], F32))
        ps_m = ctx.enter_context(nc.psum_tensor("ps_m", [P, CH], F32))

        def kv_bank(u):
            return ps_s[:, (u % 4) // 2, (u % 2) * CH:(u % 2 + 1) * CH]

        x_in = [sem(f"x_in{i}") for i in range(4)]
        small_in, wmod_in, pos_in, wkv_in = sem("small_in"), sem("wmod_in"), sem("pos_in"), sem("wkv_in")
        const_set, pool_step, dve_step = sem("const_set"), sem("pool_step"), sem("dve_step")
        rows_t, rows_used, sig_exp, silu_set = sem("rows_t"), sem("rows_used"), sem("sig_exp"), sem("silu_set")
        modt_mm, modt_set, vb_mm, vb_set = sem("modt_mm"), sem("modt_set"), sem("vb_mm"), sem("vb_set")
        var_set, rstd_set, xn_set = sem("var_set"), sem("rstd_set"), sem("xn_set")
        ht_mm, ht_raw, ht_hi, ht_lo = sem("ht_mm"), sem("ht_raw"), sem("ht_hi"), sem("ht_lo")
        wkv_hi_set, wkv_lo_set = sem("wkv_hi_set"), sem("wkv_lo_set")
        kv_mm, kv_raw, kv_hi, kv_lo = sem("kv_mm"), sem("kv_raw"), sem("kv_hi"), sem("kv_lo")
        acc_zero = sem("acc_zero")
        wq_in, wo_in = sem("wq_in"), sem("wo_in")
        wq_cut, wo_cut, w_step = sem("wq_cut"), sem("wo_cut"), sem("w_step")
        q_mm, q_raw, q_hi_set, q_lo_set = sem("q_mm"), sem("q_raw"), sem("q_hi_set"), sem("q_lo_set")
        s_mm, max_set, exp_set = sem("s_mm"), sem("max_set"), sem("exp_set")
        t_mm, pt_hi_set, pt_lo_set, pv_mm = sem("t_mm"), sem("pt_hi_set"), sem("pt_lo_set"), sem("pv_mm")
        o_hi_set, o_lo_set = sem("o_hi_set"), sem("o_lo_set")
        rsum_set, y_mm, y_add = sem("rsum_set"), sem("y_mm"), sem("y_add")
        we_in, gmod_in = sem("we_in"), sem("gmod_in")
        we_t, we_hi_set, we_lo_set = sem("we_t"), sem("we_hi_set"), sem("we_lo_set")
        silu_b_set, gmod_mm, gmod_set = sem("silu_b_set"), sem("gmod_mm"), sem("gmod_set")
        xin_in = [sem(f"xin_in{i}") for i in range(2)]
        xga_set, x1_set, ln_step, ve2_set, rs2_set = (sem("xga_set"), sem("x1_set"), sem("ln_step"),
                                                      sem("ve2_set"), sem("rs2_set"))
        xn2_set, h2_t, h2_set, h2_hi_set, h2_lo_set = (
            sem("xn2_set"), sem("h2_t"), sem("h2_set"), sem("h2_hi_set"), sem("h2_lo_set"))
        gate_mm, logits_set, gate_step, gap_set, egap_set = (
            sem("gate_mm"), sem("logits_set"), sem("gate_step"), sem("gap_set"), sem("egap_set"))
        coef_set, coef_mm, coef_t_set, yb_mm, yb_set = (
            sem("coef_set"), sem("coef_mm"), sem("coef_t_set"), sem("yb_mm"), sem("yb_set"))
        moe_mm, mixed, ysum_set, ysc_set, yout_set = (
            sem("moe_mm"), sem("mixed"), sem("ysum_set"), sem("ysc_set"), sem("yout_set"))
        seen, seen_pool = sem("seen"), sem("seen_pool")
        out_done = [sem(f"out_done{i}") for i in range(2)]

        pos_dram = nc.inline_tensor(position_table(), "position_table").ap()
        x_tiles = x.rearrange("b (n p) e -> p (b n) e", p=P)
        out_tiles = out.rearrange("b (n p) e -> p (b n) e", p=P)
        wq_h = wq.rearrange("(k p) (h d) -> p k h d", p=P, d=D)
        wo_h = wo.rearrange("(h d) e -> d h e", d=D)
        wkv_v = wkv.rearrange("(k p) n -> p k n", p=P)
        bkv_v = bkv.rearrange("(g two d) -> two g d", g=G, two=2)
        wmod_v = wmod.rearrange("(k p) (m e) -> p k m e", p=P, e=E)
        we_v = expert_w.rearrange("x (h p) d -> p x h d", p=P)

        block = ctx.enter_context(nc.Block())

        @block.sync
        def _(sp):
            for i in range(4):
                sp.dma_start(xs[:, 4 * i:4 * i + 4, :], x_tiles[:, 4 * i:4 * i + 4, :]).then_inc(x_in[i], 16)
            sp.dma_start(c_rows[:, :], c_in).then_inc(small_in, 16)
            sp.dma_start(bias_rows[0:HEADS, :], bq.rearrange("(h d) -> h d", d=D)).then_inc(small_in, 16)
            sp.dma_start(bias_rows[HEADS:HEADS + G, :], bkv_v[0, :, :]).then_inc(small_in, 16)
            sp.dma_start(vb_row[0:1, :].rearrange("o (g d) -> o g d", d=D), bkv_v[1:2, :, :]).then_inc(small_in, 16)
            sp.dma_start(gate_rows[:, :], gate_w).then_inc(small_in, 16)
            sp.dma_start(wmod_sb[:, :, :].rearrange("p k (m e) -> p k m e", e=E), wmod_v).then_inc(wmod_in, 16)
            sp.dma_start(wkv_raw[0][:, :, :], wkv_v).then_inc(wkv_in, 16)
            sp.dma_start(pos[:, :], pos_dram).then_inc(pos_in, 16)

            def load_head(n, r, g):
                if not (isinstance(n, int) and n == 0):
                    sp.wait_ge(wq_cut, n)
                sp.dma_start(wq_raw[:, :, :], wq_h[:, :, bass.ds(r + g * QPG, 1), :]
                             .rearrange("p k h d -> p k (h d)")).then_inc(wq_in, 16)
                if not (isinstance(n, int) and n == 0):
                    sp.wait_ge(wo_cut, n)
                sp.dma_start(wo_raw[:, :], wo_h[:, bass.ds(r + g * QPG, 1), :]
                             .rearrange("d h e -> d (h e)")).then_inc(wo_in, 16)

            for b in range(B):
                for g in range(G):
                    load_head(b * HEADS + g, 0, g)
                with sp.Fori(1, QPG) as r:
                    for g in range(G):
                        load_head(r * G + (b * HEADS + g), r, g)
                if b + 1 < B:
                    sp.wait_ge(ht_lo, B * NC * KE)
                    sp.dma_start(wkv_raw[1][:, :, :], wkv_v).then_inc(wkv_in, 16)

            sp.wait_ge(pv_mm, NS * B * HEADS)
            sp.wait_ge(s_mm, NT * B * HEADS)
            for i in range(2):
                sp.dma_start(we_raw[:, 4 * i:4 * i + 4, :, :], we_v[:, 4 * i:4 * i + 4, :, :]).then_inc(we_in, 16)
            sp.dma_start(ebias[:, :], expert_b).then_inc(gmod_in, 16)
            for i, m in enumerate((GA, GB)):
                sp.dma_start(gmod_w[:, :, i, :], wmod_v[:, :, m, :]).then_inc(gmod_in, 16)

            def load(n, par):
                sp.wait_ge(x1_set, n + 1)
                sp.dma_start(xin[:, par, :], x_tiles[:, bass.ds(n, 1), :]
                             .rearrange("p n e -> p (n e)")).then_inc(xin_in[par], 16)

            def store(n, par):
                sp.wait_ge(yout_set, n + 1)
                sp.dma_start(out_tiles[:, bass.ds(n, 1), :].rearrange("p n e -> p (n e)"),
                             y_out[:, par, :]).then_inc(out_done[par], 16)

            for i in range(2):
                sp.sem_inc(out_done[i], 16)
                load(i, i)
            with sp.Fori(0, B * NT // 2 - 1) as it:
                for par in range(2):
                    load(it * 2 + (2 + par), par)
                    store(it * 2 + par, par)
            for par in range(2):
                store(B * NT - 2 + par, par)
            for i in range(2):
                sp.wait_ge(out_done[i], 16 * (B * NT // 2 + 1))

        @block.gpsimd
        def _(pool):
            pool.memset(ident[:, :], 0.0).then_inc(pool_step, 1)
            pool.memset(ident_bf[:, :], 0.0).then_inc(pool_step, 1)
            pool.memset(mask_bf[:, :], 0.0).then_inc(pool_step, 1)
            pool.wait_ge(pool_step, 3)
            pool.affine_select(out=ident[:, :], in_=ident[:, :], compare_op=ALU.not_equal, fill=1.0, base=0,
                               pattern=[[-1, P]], channel_multiplier=1).then_inc(const_set, 1)
            pool.affine_select(out=ident_bf[:, :], in_=ident_bf[:, :], compare_op=ALU.not_equal, fill=1.0, base=0,
                               pattern=[[-1, P]], channel_multiplier=1).then_inc(const_set, 1)
            pool.affine_select(out=mask_bf[:, :], in_=mask_bf[:, :], compare_op=ALU.is_ge, fill=MASKED, base=0,
                               pattern=[[-1, P]], channel_multiplier=1).then_inc(const_set, 1)
            pool.memset(ones_row[:, :], 1.0).then_inc(const_set, 1)
            pool.memset(neg_half[:, :], -0.5).then_inc(const_set, 1)
            pool.iota(iota8[:, :], pattern=[[1, EXPERTS]], base=0, channel_multiplier=0,
                      allow_small_or_imprecise_dtypes=True).then_inc(const_set, 1)
            for z in (pz_hi, pz_lo):
                pool.memset(z[:, :].bitcast(F32), 0.0).then_inc(const_set, 1)
            pool.wait_ge(const_set, 5)
            pool.wait_ge(var_set, 1)
            pool.tensor_tensor(rstd[:, :], var_eps[:, :], neg_half[:, :], ALU.pow).then_inc(rstd_set, 1)

            def cut_wkv(b):
                for k in range(KE):
                    for i in range(2 * G * D // CH):
                        part = slice(i * CH, (i + 1) * CH)
                        pool.wait_ge(wkv_hi_set, 4 * b + 2 * k + i + 1)
                        pool.tensor_tensor(wkv_lo[:, k, part], wkv_raw[b][:, k, part],
                                           wkv_hi[:, k, part].bitcast(F32), ALU.subtract).then_inc(wkv_lo_set, 1)

            def cut_head(n, par):
                pool.wait_ge(wq_in, (n + 1) * 16)
                if not (isinstance(n, int) and n < 2):
                    pool.wait_ge(q_mm, n * NC - 2)
                pool.sem_inc(seen_pool, 1)
                pool.tensor_scalar(wq_hi[par][:, :, :], wq_raw[:, :, :], 1.0, 1.0, ALU.mult, ALU.mult).then_inc(w_step, 1)
                pool.wait_ge(w_step, n * 2 + 1)
                pool.tensor_tensor(wq_lo[par][:, :, :], wq_raw[:, :, :], wq_hi[par][:, :, :].bitcast(F32),
                                   ALU.subtract).then_inc(wq_cut, 1)
                pool.wait_ge(wo_in, (n + 1) * 16)
                if not (isinstance(n, int) and n < 2):
                    pool.wait_ge(y_mm, n * 4 - 4)
                pool.sem_inc(seen_pool, 1)
                pool.tensor_scalar(wo_hi[par][:, :], wo_raw[:, :], 1.0, 1.0, ALU.mult, ALU.mult).then_inc(w_step, 1)
                pool.wait_ge(w_step, n * 2 + 2)
                pool.tensor_tensor(wo_lo[par][:, :], wo_raw[:, :], wo_hi[par][:, :].bitcast(F32),
                                   ALU.subtract).then_inc(wo_cut, 1)

            for b in range(B):
                cut_wkv(b)
                for g in range(G):
                    cut_head(b * HEADS + g, g % 2)
                with pool.Fori(1, QPG) as r:
                    for g in range(G):
                        cut_head(r * G + (b * HEADS + g), g % 2)

            def row(n):
                return acc[:, bass.ds(n, 1), :].rearrange("p n e -> p (n e)")

            def residual(n, b, par, use):
                pool.tensor_tensor(row(n), row(n), gmod[:, b, 0, :], ALU.mult).then_inc(xga_set, 1)
                pool.wait_ge(xga_set, n + 1)
                pool.wait_ge(xin_in[par], use * 16 + 16)
                pool.sem_inc(seen_pool, 1)
                pool.tensor_tensor(row(n), row(n), xin[:, par, :], ALU.add).then_inc(x1_set, 1)
                pool.wait_ge(ve2_set, n + 1)
                pool.tensor_tensor(rs2[:, par, :], ve2[:, par, :], neg_half[:, 0:1], ALU.pow).then_inc(rs2_set, 1)

            def hidden_lo(n, par):
                pool.wait_ge(h2_hi_set, n + 1)
                pool.tensor_tensor(h2_lo[par][:, :, :], h2[:, par, :, :], h2_hi[par][:, :, :].bitcast(F32),
                                   ALU.subtract).then_inc(h2_lo_set, 1)

            def finish(n, b, par, use):
                pool.wait_ge(out_done[par], use * 16 + 16)
                pool.wait_ge(mixed, (n + 2) * EXPERTS)
                pool.tensor_tensor(y_sum[:, par, :], y_even[:, par, :], y_odd[:, par, :], ALU.add).then_inc(ysum_set, 1)
                pool.wait_ge(ysum_set, n + (FREE + 1))
                pool.tensor_tensor(y_sum[:, par, :], y_sum[:, par, :], gmod[:, b, 1, :], ALU.mult).then_inc(ysc_set, 1)
                pool.wait_ge(ysc_set, n + 1)
                pool.sem_inc(seen_pool, 1)
                pool.tensor_tensor(y_out[:, par, :], y_sum[:, par, :], row(n), ALU.add).then_inc(yout_set, 1)

            def slot(n, l, b, use):
                par = l % 2
                last = b + 1 == B
                if l > 0:
                    finish(n - 1, b, 1 - par, use - 1 if par == 0 else use)
                elif b > 0:
                    finish(n - 1, b - 1, 1, use - 1)
                if not (last and l + 1 >= NT):
                    hidden_lo(n + 1, 1 - par)
                if not (last and l + 2 >= NT):
                    residual(n + 2, b if l + 2 < NT else b + 1, par, use + 1)

            pool.sem_inc(x1_set, FREE)
            pool.sem_inc(ysum_set, FREE)
            pool.wait_ge(gmod_set, 1)
            pool.wait_ge(y_add, 4 * B * HEADS)
            residual(0, 0, 0, 0)
            residual(1, 0, 1, 0)
            hidden_lo(0, 0)
            for b in range(B):
                n0, u0 = b * NT, b * NT // 2
                slot(n0, 0, b, u0)
                slot(n0 + 1, 1, b, u0)
                with pool.Fori(1, NT // 2 - 1) as it:
                    slot(it * 2 + n0, 2, b, it + u0)
                    slot(it * 2 + (n0 + 1), 3, b, it + u0)
                slot(n0 + NT - 2, NT - 2, b, u0 + NT // 2 - 1)
                slot(n0 + NT - 1, NT - 1, b, u0 + NT // 2 - 1)
            finish(B * NT - 1, B - 1, 1, B * NT // 2 - 1)

        @block.tensor
        def _(pe):
            def product(out_ap, a, b, start, stop):
                nc.tensor.matmul(out_ap, a[1], b[0], start=start, stop=False)
                nc.tensor.matmul(out_ap, a[0], b[1], start=False, stop=False)
                return nc.tensor.matmul(out_ap, a[0], b[0], start=False, stop=stop)

            pe.wait_ge(const_set, 5)
            pe.wait_ge(small_in, 5 * 16)
            nb = HEADS + G
            pe.transpose(ps_m[:, 0:nb], bias_rows[:, :], ident[0:nb, 0:nb])
            for k in range(KE):
                pe.transpose(ps_m[:, 32 + B * k:32 + B * (k + 1)], c_rows[:, k * P:(k + 1) * P], ident[0:B, 0:B])
            for k in range(KE):
                last = pe.transpose(ps_m[:, 64 + EXPERTS * k:64 + EXPERTS * (k + 1)],
                                    gate_rows[:, k * P:(k + 1) * P], ident[0:EXPERTS, 0:EXPERTS])
            last.then_inc(rows_t, 1)
            pe.matmul(ps_o[:, :], ones_row[0:1, :], vb_row[0:1, :], start=True, stop=True).then_inc(vb_mm, 1)
            pe.wait_ge(silu_set, 1)
            pe.wait_ge(wmod_in, 16)
            pe.wait_ge(rows_used, 1)
            for i, m in enumerate((SA, CA, SB, CB)):
                for et in range(KE):
                    at_col = (i * KE + et) * B
                    for k in range(KE):
                        last = pe.matmul(ps_m[:, at_col:at_col + B],
                                         wmod_sb[:, k, m * E + et * P:m * E + (et + 1) * P], silu_c[:, k, :],
                                         start=k == 0, stop=k == KE - 1)
            last.then_inc(modt_mm, 1)
            for u in range(B * NC * KE):
                c, k = divmod(u, KE)
                pe.wait_ge(xn_set, TPC * (c + 1))
                if u >= 2:
                    pe.wait_ge(ht_raw, u - 1)
                for i in range(TPC):
                    last = pe.transpose(ps_t[:, u % 2, i * P:(i + 1) * P],
                                        xs[:, c * TPC + i, k * P:(k + 1) * P], ident[:, :])
                last.then_inc(ht_mm, 1)

            def queries(n, par, b, c):
                pe.wait_ge(wq_cut, n + 1)
                tokens = slice(b * T + c * CH, b * T + (c + 1) * CH)
                for k in range(KE):
                    last = product(ps_m[:, :], (wq_hi[par][:, k, :], wq_lo[par][:, k, :]),
                                   (h_hi[:, k, tokens], h_lo[:, k, tokens]), k == 0, k == KE - 1)
                last.then_inc(q_mm, 1)

            def score_piece(n, par, g, q, first):
                i, c0, w, ends = PIECES[q]
                if i % TPC == 0 and q == FIRST_PIECE[i]:
                    pe.wait_ge(q_lo_set, n * NC + (i // TPC + 1))
                if q == FIRST_PIECE[i] and not (first and i < 2):
                    pe.wait_ge(exp_set, n * NT + (i - 1))
                rows = slice(i * P, (i + 1) * P)
                col = score_offset(i) + c0
                keys = slice(c0, c0 + w)
                last = product(ps_s[:, i % 2, col:col + w], (q_hi[par][:, rows], q_lo[par][:, rows]),
                               (k_hi[:, g, keys], k_lo[:, g, keys]), True, not ends)
                if ends:
                    diag = score_offset(i) + i * P
                    pe.matmul(ps_s[:, i % 2, diag:diag + P], ident_bf[:, :], mask_bf[:, :],
                              start=False, stop=True).then_inc(s_mm, 1)

            def turn_probs(n, par, q, first):
                c, j = STEPS[q]
                if j == 0:
                    pe.wait_ge(exp_set, n * NT + (c + 1) * TPC)
                if not (first and q < 2):
                    pe.wait_ge(pt_lo_set, n * NS + (q - 1))
                for i in range(max(j, c * TPC), (c + 1) * TPC):
                    p0 = prob_offset(i) + j * P
                    col = (i - c * TPC) * P
                    last = pe.transpose(ps_t[:, q % 2, col:col + P], probs[par][:, p0:p0 + P], ident[:, :])
                last.then_inc(t_mm, 1)

            def weigh_values(n, g, q, first):
                c, j = STEPS[q]
                pe.wait_ge(pt_lo_set, n * NS + (q + 1))
                if j == 0 and not (first and c == 0):
                    pe.wait_ge(o_lo_set, n * NC + c)
                v = (v_hi[:, j, g, :], v_lo[:, j, g, :])
                if q in LAST_STEP:
                    last = product(ps_o[:, CH - 2 * P:CH], v, (pz_hi[:, :], pz_lo[:, :]), False, True)
                else:
                    lo = (max(j, c * TPC) - c * TPC) * P
                    last = product(ps_o[:, lo:CH], v, (pt_hi[:, q % PT, lo:CH], pt_lo[:, q % PT, lo:CH]),
                                   j == 0, False)
                last.then_inc(pv_mm, 1)

            def project(n, par, c, pair):
                if pair == 0:
                    pe.wait_ge(o_lo_set, n * NC + (c + 1))
                    if c == 0:
                        pe.wait_ge(wo_cut, n + 1)
                for i in range(2):
                    rows = slice((2 * pair + i) * P, (2 * pair + i + 1) * P)
                    last = product(ps_m[:, i * E:(i + 1) * E], (o_hi[c][:, rows], o_lo[c][:, rows]),
                                   (wo_hi[par][:, :], wo_lo[par][:, :]), True, True)
                last.then_inc(y_mm, 1)

            def frame(n, l, b):
                par, g = l % 2, l % G
                prev, nxt, nxt2 = l > 0, l + 1 < HEADS, l + 2 < HEADS
                first = isinstance(n, int) and n == 0
                for q in range(NS):
                    turn_probs(n, par, q, first)
                    if nxt:
                        score_piece(n + 1, 1 - par, (l + 1) % G, q, False)
                    if q == 0 and nxt:
                        pe.wait_ge(q_raw, n * NC + 3)
                        queries(n + 1, 1 - par, b, 1)
                    if q == 3 and prev:
                        if nxt:
                            pe.wait_ge(q_raw, n * NC + 4)
                        else:
                            pe.wait_ge(y_add, n * 4 - 2)
                        project(n - 1, 1 - par, 1, 0)
                    if q == 5 and prev:
                        pe.wait_ge(y_add, n * 4 - 1)
                        project(n - 1, 1 - par, 1, 1)
                    if q == 7:
                        if prev:
                            pe.wait_ge(y_add, n * 4)
                        else:
                            pe.wait_ge(q_raw, n * NC + 4)
                        project(n, par, 0, 0)
                    if q == 9:
                        pe.wait_ge(y_add, n * 4 + 1)
                        project(n, par, 0, 1)
                    if q == 10 and nxt2:
                        pe.wait_ge(y_add, n * 4 + 2)
                        queries(n + 2, par, b, 0)
                    if q < LAG and prev:
                        weigh_values(n - 1, (l - 1) % G, NS - LAG + q, False)
                    if q >= LAG:
                        weigh_values(n, g, q - LAG, first)

            for b in range(B):
                n0 = b * HEADS
                pe.wait_ge(wkv_lo_set, 4 * (b + 1))
                if b == 0:
                    pe.wait_ge(ht_lo, B * NC * KE)
                else:
                    pe.wait_ge(exp_set, n0 * NT)
                for u in range(G * NC + NT):
                    if u >= 4:
                        pe.wait_ge(kv_raw, 16 * b + u - 3)
                    for k in range(KE):
                        if u < G * NC:
                            g, c = divmod(u, NC)
                            wcols = slice(2 * g * D, (2 * g + 1) * D)
                            tokens = slice(b * T + c * CH, b * T + (c + 1) * CH)
                            last = product(kv_bank(u), (wkv_hi[:, k, wcols], wkv_lo[:, k, wcols]),
                                           (h_hi[:, k, tokens], h_lo[:, k, tokens]), k == 0, k == KE - 1)
                        else:
                            s = b * T + (u - G * NC) * P
                            wv = [w[:, k, :].rearrange("p (g two d) -> p g two d", g=G, two=2)[:, :, 1, :]
                                  for w in (wkv_hi, wkv_lo)]
                            last = product(kv_bank(u), (h_hi[:, k, s:s + P], h_lo[:, k, s:s + P]), wv,
                                           k == 0, k == KE - 1)
                    last.then_inc(kv_mm, 1)
                if b == 0:
                    pe.wait_ge(modt_set, 1)
                else:
                    pe.wait_ge(y_add, n0 * 4)
                queries(n0, 0, b, 0)
                pe.wait_ge(q_raw, n0 * NC + 1)
                queries(n0, 0, b, 1)
                pe.wait_ge(q_raw, n0 * NC + 2)
                queries(n0 + 1, 1, b, 0)
                pe.wait_ge(kv_lo, 16 * (b + 1))
                for q in range(NS):
                    score_piece(n0, 0, 0, q, b == 0)
                frame(n0, 0, b)
                with pe.Fori(0, (HEADS - 4) // G) as it:
                    for s in range(G):
                        frame(it * G + (n0 + 1 + s), 1 + s, b)
                for l in range(HEADS - 3, HEADS):
                    frame(n0 + l, l, b)
                n = n0 + HEADS - 1
                for q in range(NS - LAG, NS):
                    weigh_values(n, G - 1, q, False)
                for pair in range(2):
                    pe.wait_ge(y_add, n * 4 + 2 + pair)
                    project(n, 1, 1, pair)

            for u in range(EXPERTS // 2 * KE):
                e2, k = divmod(u, KE)
                pe.wait_ge(we_in, 32)
                if u < 2:
                    pe.wait_ge(pt_lo_set, NS * B * HEADS)
                else:
                    pe.wait_ge(we_lo_set, u - 1)
                for i in range(2):
                    for h in range(KE):
                        col = (i * KE + h) * P
                        last = pe.transpose(ps_t[:, u % 2, col:col + P],
                                            we_raw[:, 2 * e2 + i, h, k * P:(k + 1) * P], ident[:, :])
                last.then_inc(we_t, 1)
            pe.wait_ge(silu_b_set, 1)
            pe.wait_ge(gmod_in, 48)
            for b in range(B):
                for m in range(2):
                    for k in range(KE):
                        last = pe.matmul(ps_s[:, 0, (b * 2 + m) * E:(b * 2 + m + 1) * E], silu_b[:, k, b, :],
                                         gmod_w[:, k, m, :], start=k == 0, stop=k == KE - 1)
            last.then_inc(gmod_mm, 1)

            def turn_hidden(n, par):
                pe.wait_ge(xn2_set, n + 1)
                for k in range(KE):
                    last = pe.transpose(ps_t[:, par, k * P:(k + 1) * P], xn2[:, par, k * P:(k + 1) * P], ident[:, :])
                last.then_inc(h2_t, 1)

            def gate(n, par):
                pe.wait_ge(h2_set, n * KE + KE)
                if not (isinstance(n, int) and n == 0):
                    pe.wait_ge(yb_set, n)
                for k in range(KE):
                    last = pe.matmul(ps_m[:, 0:EXPERTS], h2[:, par, k, :], gate_t[:, k, :],
                                     start=k == 0, stop=k == KE - 1)
                last.then_inc(gate_mm, 1)

            def mix_bias(n, par):
                pe.wait_ge(coef_set, n + 1)
                pe.transpose(ps_m[0:EXPERTS, 0:P], coef[:, par, :], ident[:, :]).then_inc(coef_mm, 1)
                pe.wait_ge(coef_t_set, n + 1)
                pe.matmul(ps_m[:, 0:O], coef_t[:, par, :], ebias[:, :], start=True, stop=True).then_inc(yb_mm, 1)

            def experts(n, par, e2):
                if e2 == 0:
                    pe.wait_ge(h2_lo_set, n + 1)
                pe.wait_ge(mixed, n * EXPERTS + 2 * (e2 + 1))
                for k in range(KE):
                    w = [t[:, k, 2 * e2:2 * e2 + 2, :].rearrange("p x o -> p (x o)") for t in (we_hi, we_lo)]
                    last = product(kv_bank(e2), (h2_hi[par][:, k, :], h2_lo[par][:, k, :]), w, k == 0, k == KE - 1)
                last.then_inc(moe_mm, 1)

            def slot(n, par, more):
                if more:
                    turn_hidden(n + 1, 1 - par)
                experts(n, par, 0)
                experts(n, par, 1)
                if more:
                    gate(n + 1, 1 - par)
                experts(n, par, 2)
                experts(n, par, 3)
                if more:
                    mix_bias(n + 1, 1 - par)

            pe.sem_inc(moe_mm, FREE * EXPERTS // 2)
            pe.wait_ge(we_lo_set, 8)
            pe.wait_ge(gmod_set, 1)
            turn_hidden(0, 0)
            gate(0, 0)
            mix_bias(0, 0)
            with pe.Fori(0, B * NT // 2 - 1) as it:
                slot(it * 2, 0, True)
                slot(it * 2 + 1, 1, True)
            slot(B * NT - 2, 0, True)
            slot(B * NT - 1, 1, False)

        @block.scalar
        def _(act):
            def keep_hi(dst, src, scale=1.0):
                return nc.scalar.activation(dst, src, ACT.Copy, scale=scale)

            act.wait_ge(rows_used, 1)
            nc.scalar.activation(sig_tmp[:, 0, :], silu_c[:, :, :].rearrange("p k b -> p (k b)"), ACT.Exp,
                                 scale=-1.0).then_inc(sig_exp, 1)

            def cut_wkv(b):
                act.wait_ge(wkv_in, 16 * (b + 1))
                for k in range(KE):
                    for i in range(2 * G * D // CH):
                        part = slice(i * CH, (i + 1) * CH)
                        keep_hi(wkv_hi[:, k, part], wkv_raw[b][:, k, part]).then_inc(wkv_hi_set, 1)

            cut_wkv(0)
            for u in range(B * NC * KE):
                c, k = divmod(u, KE)
                act.wait_ge(ht_raw, u + 1)
                keep_hi(h_hi[:, k, c * CH:(c + 1) * CH], raw[:, u % 2, :]).then_inc(ht_hi, 1)

            def exponentials(n, par, i):
                w = (i + 1) * P
                act.wait_ge(max_set, n * NT + (i + 1))
                col = score_offset(i)
                nc.scalar.activation(probs[par][:, prob_offset(i):prob_offset(i) + w], ps_s[:, i % 2, col:col + w],
                                     ACT.Exp, bias=neg_max[:, par, i:i + 1],
                                     accum_out=sums[:, par, i:i + 1]).then_inc(exp_set, 1)

            def probs_hi(n, q, first):
                c, j = STEPS[q]
                act.wait_ge(t_mm, n * NS + (q + 1))
                if not (first and q < PT):
                    act.wait_ge(pv_mm, n * NS + (q - PT + 1))
                lo = (max(j, c * TPC) - c * TPC) * P
                dst = pz_hi[:, P:2 * P] if q in LAST_STEP else pt_hi[:, q % PT, lo:CH]
                keep_hi(dst, ps_t[:, q % 2, lo:CH]).then_inc(pt_hi_set, 1)

            def output_hi(n, c, first):
                act.wait_ge(pv_mm, n * NS + (LAST_STEP[c] + 1))
                if not first:
                    act.wait_ge(y_mm, n * 4 + (2 * c - 2))
                keep_hi(o_hi[c][:, :], ps_o[:, :]).then_inc(o_hi_set, 1)

            def queries_hi(n, par, c):
                act.wait_ge(q_raw, n * NC + (c + 1))
                keep_hi(q_hi[par][:, c * CH:(c + 1) * CH], raw[:, c, :], SCALE).then_inc(q_hi_set, 1)

            def frame(n, l, b):
                par = l % 2
                prev, nxt, nxt2 = l > 0, l + 1 < HEADS, l + 2 < HEADS
                first = isinstance(n, int) and n == 0
                for q in range(NS):
                    probs_hi(n, q, first)
                    if q == LAG - 1 and prev:
                        output_hi(n - 1, 1, isinstance(n, int) and n == 1)
                    if q == LAST_STEP[0] + LAG:
                        output_hi(n, 0, first)
                    if q == 0 and prev:
                        exponentials(n, par, NT - 1)
                    if q > 0 and nxt and PIECES[q - 1][3]:
                        exponentials(n + 1, 1 - par, PIECES[q - 1][0])
                    if q == 0 and nxt:
                        queries_hi(n + 1, 1 - par, 1)
                    if q == 10 and nxt2:
                        queries_hi(n + 2, par, 0)

            for b in range(B):
                n0 = b * HEADS
                for u in range(G * NC + NT):
                    act.wait_ge(kv_raw, 16 * b + u + 1)
                    if u < G * NC:
                        g, c = divmod(u, NC)
                        dst = k_hi[:, g, c * CH:(c + 1) * CH]
                    else:
                        dst = v_hi[:, u - G * NC, :, :].rearrange("p g d -> p (g d)")
                    keep_hi(dst, raw[:, u % 2, :]).then_inc(kv_hi, 1)
                queries_hi(n0, 0, 0)
                queries_hi(n0, 0, 1)
                queries_hi(n0 + 1, 1, 0)
                for i in range(NT):
                    exponentials(n0, 0, i)
                frame(n0, 0, b)
                with act.Fori(0, (HEADS - 4) // G) as it:
                    for s in range(G):
                        frame(it * G + (n0 + 1 + s), 1 + s, b)
                for l in range(HEADS - 3, HEADS):
                    frame(n0 + l, l, b)
                if b + 1 < B:
                    act.wait_ge(t_mm, (n0 + HEADS - 1) * NS)
                    cut_wkv(1)
                output_hi(n0 + HEADS - 1, 1, False)

            for u in range(EXPERTS // 2 * KE):
                e2, k = divmod(u, KE)
                act.wait_ge(we_t, u + 1)
                keep_hi(we_hi[:, k, 2 * e2:2 * e2 + 2, :].rearrange("p x o -> p (x o)"),
                        ps_t[:, u % 2, :]).then_inc(we_hi_set, 1)

            def stage_a(n, b, par):
                act.wait_ge(h2_t, n + 1)
                for k in range(KE):
                    nc.scalar.activation(h2[:, par, k, :], ps_t[:, par, k * P:(k + 1) * P], ACT.Identity,
                                         scale=modt[:, 3, k, b:b + 1], bias=modt[:, 2, k, b:b + 1]).then_inc(h2_set, 1)
                act.wait_ge(h2_set, n * KE + KE)
                act.wait_ge(moe_mm, (n + 1) * 4)
                keep_hi(h2_hi[par][:, :, :], h2[:, par, :, :]).then_inc(h2_hi_set, 1)
                act.wait_ge(gate_mm, n + 1)
                nc.scalar.activation(logits[:, par, :], ps_m[:, 0:EXPERTS], ACT.Copy).then_inc(logits_set, 1)
                act.wait_ge(gap_set, n + 1)
                nc.scalar.activation(egap[:, par, :], gap[:, par, :], ACT.Exp).then_inc(egap_set, 1)

            def mix_bias(n, par):
                act.wait_ge(coef_mm, n + 1)
                nc.scalar.activation(coef_t[:, par, :], ps_m[0:EXPERTS, 0:P], ACT.Copy).then_inc(coef_t_set, 1)
                act.wait_ge(yb_mm, n + 1)
                nc.scalar.activation(y_bias[:, par, :], ps_m[:, 0:O], ACT.Copy).then_inc(yb_set, 1)

            stage_a(0, 0, 0)
            mix_bias(0, 0)
            for b in range(B):
                n0 = b * NT
                with act.Fori(0, NT // 2 - 1) as it:
                    for par in (1, 0):
                        stage_a(it * 2 + (n0 + 2 - par), b, par)
                        mix_bias(it * 2 + (n0 + 2 - par), par)
                stage_a(n0 + NT - 1, b, 1)
                mix_bias(n0 + NT - 1, 1)
                if b + 1 < B:
                    stage_a(n0 + NT, b + 1, 0)
                    mix_bias(n0 + NT, 0)

        @block.vector
        def _(dve):
            dve.wait_ge(rows_t, 1)
            nc.vector.tensor_copy(qk_bias[:, :], ps_m[:, 0:HEADS + G]).then_inc(dve_step, 1)
            nc.vector.tensor_copy(gate_t[:, :, :].rearrange("p k e -> p (k e)"),
                                  ps_m[:, 64:64 + KE * EXPERTS]).then_inc(dve_step, 1)
            nc.vector.tensor_copy(silu_c[:, :, :].rearrange("p k b -> p (k b)"),
                                  ps_m[:, 32:32 + KE * B]).then_inc(rows_used, 1)
            dve.wait_ge(vb_mm, 1)
            nc.vector.tensor_copy(v_bias[:, :], ps_o[:, :]).then_inc(vb_set, 1)
            dve.wait_ge(sig_exp, 1)
            nc.vector.tensor_scalar(sig_tmp[:, 1, :], sig_tmp[:, 0, :], 1.0, None, ALU.add).then_inc(dve_step, 1)
            dve.wait_ge(dve_step, 3)
            nc.vector.reciprocal(sig_tmp[:, 2, :], sig_tmp[:, 1, :]).then_inc(dve_step, 1)
            dve.wait_ge(dve_step, 4)
            flat_c = silu_c[:, :, :].rearrange("p k b -> p (k b)")
            nc.vector.tensor_tensor(flat_c, flat_c, sig_tmp[:, 2, :], ALU.mult).then_inc(silu_set, 1)
            for i in range(B * NT):
                if i % 4 == 0:
                    dve.wait_ge(x_in[i // 4], 16)
                nc.vector.bn_stats(stats[:, i, :], xs[:, i, :]).then_inc(ln_step, 1)
            for i in range(B * NT):
                dve.wait_ge(ln_step, i + 1)
                nc.vector.bn_aggr(mv[:, i, :], stats[:, i, :]).then_inc(dve_step, 1)
            dve.wait_ge(dve_step, 4 + B * NT)
            nc.vector.tensor_scalar(var_eps[:, :], mv[:, :, 1], EPS, None, ALU.add).then_inc(var_set, 1)
            dve.wait_ge(modt_mm, 1)
            for i in range(4):
                cols = slice(i * KE * B, (i + 1) * KE * B)
                last = nc.vector.tensor_scalar(modt[:, i, :, :].rearrange("p k b -> p (k b)"), ps_m[:, cols],
                                               float(i % 2), None, ALU.add)
            last.then_inc(modt_set, 1)
            dve.wait_ge(rstd_set, 1)
            for i in range(B * NT):
                nc.vector.tensor_scalar(xs[:, i, :], xs[:, i, :], mv[:, i, 0:1], rstd[:, i:i + 1],
                                        ALU.subtract, ALU.mult).then_inc(xn_set, 1)
            dve.wait_ge(modt_set, 1)

            def hidden_lo(u):
                c, k = divmod(u, KE)
                part = slice(c * CH, (c + 1) * CH)
                dve.wait_ge(ht_hi, u + 1)
                nc.vector.tensor_tensor(h_lo[:, k, part], raw[:, u % 2, :], h_hi[:, k, part].bitcast(F32),
                                        ALU.subtract).then_inc(ht_lo, 1)

            for u in range(B * NC * KE):
                c, k = divmod(u, KE)
                b = c // NC
                dve.wait_ge(ht_mm, u + 1)
                if u >= 2:
                    dve.wait_ge(ht_lo, u - 1)
                nc.vector.tensor_scalar(raw[:, u % 2, :], ps_t[:, u % 2, :], modt[:, 1, k, b:b + 1],
                                        modt[:, 0, k, b:b + 1], ALU.mult, ALU.add).then_inc(ht_raw, 1)
                if u >= 1:
                    hidden_lo(u - 1)
            hidden_lo(B * NC * KE - 1)

            def kv_part(b, u):
                if u < G * NC:
                    g, c = divmod(u, NC)
                    return [t[:, g, c * CH:(c + 1) * CH] for t in (k_hi, k_lo)]
                return [t[:, u - G * NC, :, :].rearrange("p g d -> p (g d)") for t in (v_hi, v_lo)]

            def kv_cut(b, u):
                hi, lo = kv_part(b, u)
                dve.wait_ge(kv_hi, 16 * b + u + 1)
                nc.vector.tensor_tensor(lo, raw[:, u % 2, :], hi.bitcast(F32), ALU.subtract).then_inc(kv_lo, 1)

            def maxima(n, par, i):
                w = (i + 1) * P
                dve.wait_ge(s_mm, n * NT + (i + 1))
                col = score_offset(i)
                nc.vector.tensor_reduce(neg_max[:, par, i:i + 1], ps_s[:, i % 2, col:col + w], AXIS_X, ALU.max,
                                        negate=True).then_inc(max_set, 1)

            def probs_lo(n, q):
                c, j = STEPS[q]
                dve.wait_ge(pt_hi_set, n * NS + (q + 1))
                lo = (max(j, c * TPC) - c * TPC) * P
                hi_t, lo_t = [(z[:, P:2 * P] if q in LAST_STEP else t[:, q % PT, lo:CH])
                              for z, t in ((pz_hi, pt_hi), (pz_lo, pt_lo))]
                nc.vector.tensor_tensor(lo_t, ps_t[:, q % 2, lo:CH], hi_t.bitcast(F32),
                                        ALU.subtract).then_inc(pt_lo_set, 1)

            def output_lo(n, c):
                dve.wait_ge(o_hi_set, n * NC + (c + 1))
                nc.vector.tensor_tensor(o_lo[c][:, :], ps_o[:, :], o_hi[c][:, :].bitcast(F32),
                                        ALU.subtract).then_inc(o_lo_set, 1)

            def queries_raw(n, g, b, c, r, after_kv=False):
                head = r + g * QPG
                bias = qk_bias[:, head:head + 1] if isinstance(head, int) else qk_bias[:, bass.ds(head, 1)]
                if after_kv:
                    dve.wait_ge(kv_lo, 16 * (b + 1))
                else:
                    dve.wait_ge(q_lo_set, n * NC + (c - 1))
                dve.wait_ge(q_mm, n * NC + (c + 1))
                nc.vector.scalar_tensor_tensor(raw[:, c, :], ps_m[:, :], bias, pos[:, c * CH:(c + 1) * CH],
                                               ALU.add, ALU.add).then_inc(q_raw, 1)

            def queries_lo(n, par, c):
                part = slice(c * CH, (c + 1) * CH)
                dve.wait_ge(q_hi_set, n * NC + (c + 1))
                nc.vector.scalar_tensor_tensor(q_lo[par][:, part], raw[:, c, :], SCALE,
                                               q_hi[par][:, part].bitcast(F32), ALU.mult,
                                               ALU.subtract).then_inc(q_lo_set, 1)

            def sum_inverse(n, par, c):
                part = slice(c * TPC, (c + 1) * TPC)
                dve.wait_ge(exp_set, n * NT + (c + 1) * TPC)
                nc.vector.reciprocal(rsum[:, par, part], sums[:, par, part]).then_inc(rsum_set, 1)

            def add_projection(n, par, b, c, pair):
                dve.wait_ge(y_mm, n * 4 + (2 * c + pair + 1))
                if pair == 0:
                    dve.wait_ge(rsum_set, n * NC + (c + 1))
                for i in range(2):
                    tile = c * TPC + 2 * pair + i
                    row = acc[:, b * NT + tile, :]
                    last = nc.vector.scalar_tensor_tensor(row, ps_m[:, i * E:(i + 1) * E],
                                                          rsum[:, par, tile:tile + 1], row, ALU.mult, ALU.add)
                last.then_inc(y_add, 1)

            def frame(n, l, b, r):
                par, g = l % 2, l % G
                prev, nxt, nxt2 = l > 0, l + 1 < HEADS, l + 2 < HEADS
                for q in range(NS):
                    if q == 1 and nxt:
                        queries_lo(n + 1, 1 - par, 1)
                    if q == 11 and nxt2:
                        queries_lo(n + 2, par, 0)
                    probs_lo(n, q)
                    if q == LAG - 1 and prev:
                        output_lo(n - 1, 1)
                    if q == LAST_STEP[0] + LAG:
                        output_lo(n, 0)
                    if q == 2:
                        sum_inverse(n, par, 0)
                    if q == 6:
                        sum_inverse(n, par, 1)
                    if nxt and PIECES[q][3]:
                        maxima(n + 1, 1 - par, PIECES[q][0])
                    if q == 0 and nxt:
                        queries_raw(n + 1, (l + 1) % G, b, 1, r(1))
                    if q == 3 and prev:
                        add_projection(n - 1, 1 - par, b, 1, 0)
                    if q == 5 and prev:
                        add_projection(n - 1, 1 - par, b, 1, 1)
                    if q == 7:
                        add_projection(n, par, b, 0, 0)
                    if q == 9:
                        add_projection(n, par, b, 0, 1)
                    if q == 10 and nxt2:
                        queries_raw(n + 2, (l + 2) % G, b, 0, r(2))

            for b in range(B):
                n0 = b * HEADS
                if b == 0:
                    dve.wait_ge(pos_in, 16)
                    dve.wait_ge(vb_set, 1)
                for u in range(G * NC + NT):
                    if u >= 2:
                        dve.wait_ge(kv_lo, 16 * b + u - 1)
                    elif b == 0:
                        dve.wait_ge(ht_lo, B * NC * KE)
                    else:
                        dve.wait_ge(q_lo_set, n0 * NC)
                    dve.wait_ge(kv_mm, 16 * b + u + 1)
                    if u < G * NC:
                        g, c = divmod(u, NC)
                        last = nc.vector.scalar_tensor_tensor(raw[:, u % 2, :], kv_bank(u),
                                                              qk_bias[:, HEADS + g:HEADS + g + 1],
                                                              pos[:, c * CH:(c + 1) * CH], ALU.add, ALU.add)
                    else:
                        last = nc.vector.tensor_tensor(raw[:, u % 2, :], kv_bank(u), v_bias[:, :], ALU.add)
                    last.then_inc(kv_raw, 1)
                    if u >= 1:
                        kv_cut(b, u - 1)
                kv_cut(b, G * NC + NT - 1)
                queries_raw(n0, 0, b, 0, 0, after_kv=True)
                queries_raw(n0, 0, b, 1, 0, after_kv=True)
                queries_lo(n0, 0, 0)
                queries_raw(n0 + 1, 1, b, 0, 0)
                queries_lo(n0, 0, 1)
                queries_lo(n0 + 1, 1, 0)
                dve.wait_ge(wkv_lo_set, 4 * (b + 1))
                nc.vector.memset(acc[:, b * NT:(b + 1) * NT, :], 0.0).then_inc(acc_zero, 1)
                for i in range(NT):
                    maxima(n0, 0, i)
                dve.wait_ge(acc_zero, b + 1)
                frame(n0, 0, b, lambda d: d // G)
                with dve.Fori(0, (HEADS - 4) // G) as it:
                    for s in range(G):
                        frame(it * G + (n0 + 1 + s), 1 + s, b, lambda d, s=s, it=it: it + (1 + s + d) // G)
                for l in range(HEADS - 3, HEADS):
                    frame(n0 + l, l, b, lambda d, l=l: (l + d) // G)
                n = n0 + HEADS - 1
                output_lo(n, 1)
                add_projection(n, 1, b, 1, 0)
                add_projection(n, 1, b, 1, 1)

            for k in range(KE):
                for b in range(B):
                    last = nc.vector.memset(silu_b[:, k, b, :], 1.0)
            last.then_inc(dve_step, 1)
            dve.wait_ge(dve_step, 5 + B * NT)
            for k in range(KE):
                for b in range(B):
                    last = nc.vector.tensor_scalar(silu_b[:, k, b, :], silu_b[:, k, b, :], silu_c[:, k, b:b + 1],
                                                   None, ALU.mult)
            last.then_inc(silu_b_set, 1)
            for u in range(EXPERTS // 2 * KE):
                e2, k = divmod(u, KE)
                dve.wait_ge(we_hi_set, u + 1)
                hi, lo = [t[:, k, 2 * e2:2 * e2 + 2, :].rearrange("p x o -> p (x o)") for t in (we_hi, we_lo)]
                nc.vector.tensor_tensor(lo, ps_t[:, u % 2, :], hi.bitcast(F32), ALU.subtract).then_inc(we_lo_set, 1)
            flat = [t[:, :, :, :].rearrange("p b m e -> p (b m e)") for t in (g_sign, g_size, gmod)]
            dve.wait_ge(gmod_mm, 1)
            nc.vector.tensor_scalar(flat[0], ps_s[:, 0, :], 0.0, 2.0, ALU.is_ge, ALU.mult).then_inc(dve_step, 1)
            nc.vector.tensor_scalar(flat[1], ps_s[:, 0, :], 0.25, None, ALU.max).then_inc(dve_step, 1)
            nc.vector.tensor_scalar(flat[2], ps_s[:, 0, :], -1.0, 0.25, ALU.mult, ALU.max).then_inc(dve_step, 1)
            dve.wait_ge(dve_step, 8 + B * NT)
            nc.vector.tensor_tensor(flat[1], flat[1], flat[2], ALU.max).then_inc(dve_step, 1)
            dve.wait_ge(dve_step, 9 + B * NT)
            nc.vector.scalar_tensor_tensor(flat[2], flat[0], -1.0, flat[1], ALU.add, ALU.mult).then_inc(gmod_set, 1)

            def row(n):
                return acc[:, bass.ds(n, 1), :].rearrange("p n e -> p (n e)")

            def normalise(n, par):
                dve.wait_ge(x1_set, n + (FREE + 1))
                nc.vector.bn_stats(st2[:, par, :], row(n)).then_inc(ln_step, 1)
                dve.wait_ge(ln_step, n * 2 + (B * NT + 1))
                dve.sem_inc(seen, 1)
                nc.vector.bn_aggr(mv2[:, par, :], st2[:, par, :]).then_inc(ln_step, 1)
                dve.wait_ge(ln_step, n * 2 + (B * NT + 2))
                nc.vector.tensor_scalar(ve2[:, par, :], mv2[:, par, 1:2], EPS, None, ALU.add).then_inc(ve2_set, 1)
                dve.wait_ge(rs2_set, n + 1)
                nc.vector.tensor_scalar(xn2[:, par, :], row(n), mv2[:, par, 0:1], rs2[:, par, :],
                                        ALU.subtract, ALU.mult).then_inc(xn2_set, 1)
            def choose(n, par):
                dve.wait_ge(logits_set, n + 1)
                dve.sem_inc(seen, 1)
                nc.vector.max(top_v[:, par, :], logits[:, par, :]).then_inc(gate_step, 1)
                dve.wait_ge(gate_step, n * 7 + 1)
                nc.vector.tensor_scalar(gap[:, par, :], top_v[:, par, 1:2], top_v[:, par, 0:1], None,
                                        ALU.subtract).then_inc(gap_set, 1)
                nc.vector.max_index(top_i[:, par, :], top_v[:, par, :], logits[:, par, :]).then_inc(gate_step, 1)
                dve.wait_ge(gate_step, n * 7 + 2)
                nc.vector.tensor_copy(top_f[:, par, :], top_i[:, par, 0:2]).then_inc(gate_step, 1)
                dve.wait_ge(egap_set, n + 1)
                nc.vector.tensor_scalar(wsum[:, par, :], egap[:, par, :], 1.0, None, ALU.add).then_inc(gate_step, 1)
                dve.wait_ge(gate_step, n * 7 + 4)
                nc.vector.reciprocal(wtop[:, par, 0:1], wsum[:, par, :]).then_inc(gate_step, 1)
                dve.wait_ge(gate_step, n * 7 + 5)
                nc.vector.tensor_tensor(wtop[:, par, 1:2], egap[:, par, :], wtop[:, par, 0:1],
                                        ALU.mult).then_inc(gate_step, 1)
                nc.vector.tensor_scalar(coef1[:, par, :], iota8[:, :], top_f[:, par, 0:1], wtop[:, par, 0:1],
                                        ALU.is_equal, ALU.mult)
                dve.wait_ge(gate_step, n * 7 + 6)
                nc.vector.tensor_scalar(coef2[:, par, :], iota8[:, :], top_f[:, par, 1:2], wtop[:, par, 1:2],
                                        ALU.is_equal, ALU.mult).then_inc(gate_step, 1)
                dve.wait_ge(gate_step, n * 7 + 7)
                nc.vector.tensor_tensor(coef[:, par, :], coef1[:, par, :], coef2[:, par, :],
                                        ALU.add).then_inc(coef_set, 1)

            def mix(n, par, experts):
                for e in experts:
                    if e == 0:
                        dve.wait_ge(yb_set, n + 1)
                        dve.wait_ge(ysum_set, n + 1)
                    if e % 2 == 0:
                        dve.wait_ge(moe_mm, n * 4 + (4 * FREE + e // 2 + 1))
                    src = kv_bank(e // 2)[:, (e % 2) * O:(e % 2 + 1) * O]
                    y = (y_even, y_odd)[e % 2][:, par, :]
                    weight = coef[:, par, e:e + 1]
                    if e >= 2:
                        dve.wait_ge(mixed, n * EXPERTS + (EXPERTS + e - 1))
                    if e == 1:
                        last = nc.vector.tensor_scalar(y, src, weight, None, ALU.mult)
                    else:
                        last = nc.vector.scalar_tensor_tensor(y, src, weight, y_bias[:, par, :] if e == 0 else y,
                                                              ALU.mult, ALU.add)
                    last.then_inc(mixed, 1)

            def slot(n, par, more, more2):
                if more2:
                    normalise(n + 2, par)
                mix(n, par, range(0, 4))
                if more:
                    choose(n + 1, 1 - par)
                mix(n, par, range(4, EXPERTS))

            dve.sem_inc(mixed, EXPERTS)
            dve.wait_ge(gmod_set, 1)
            normalise(0, 0)
            normalise(1, 1)
            choose(0, 0)
            with dve.Fori(0, B * NT // 2 - 1) as it:
                slot(it * 2, 0, True, True)
                slot(it * 2 + 1, 1, True, True)
            slot(B * NT - 2, 0, True, False)
            slot(B * NT - 1, 1, False, False)


_INS = ['L0_attn_x', 'L0_attn_wq', 'L0_attn_bq', 'L0_attn_wkv', 'L0_attn_bkv', 'L0_attn_wo', 'L0_ffn_gate_w',
        'L0_ffn_expert_w', 'L0_ffn_expert_b', 'L0_c', 'L0_wmod']
_OUTS = [((B, T, E), 'float32')]


def kernel(**inputs):
    import numpy as _np
    import concourse.bacc as _bacc
    from concourse import mybir as _mybir
    from concourse.bass_utils import run_bass_kernel_spmd as _run

    nc = _bacc.Bacc("TRN2", target_bir_lowering=False, num_devices=1)
    arrays, args = {}, []
    for name in _INS:
        a = _np.ascontiguousarray(inputs[name])
        arrays[f"in_{name}_dram"] = a
        args.append(nc.dram_tensor(f"in_{name}_dram", a.shape, _mybir.dt.from_np(a.dtype), kind="ExternalInput").ap())
    for i, (shape, dtype) in enumerate(_OUTS):
        dt = _mybir.dt.from_np(_np.dtype(dtype))
        args.append(nc.dram_tensor(f"out_{i}_dram", shape, dt, kind="ExternalOutput").ap())
    adaln_block(nc, *args)
    r = _run(nc, [arrays], core_ids=[0])
    return r.results[0]["out_0_dram"]
```

```python
from contextlib import ExitStack

import numpy as np

import concourse.bass as bass
from concourse import mybir

F32 = mybir.dt.float32
F32R = mybir.dt.float32r
BF16 = mybir.dt.bfloat16
U32 = mybir.dt.uint32
ALU = mybir.AluOpType
ACT = mybir.ActivationFunctionType
AXIS_X = mybir.AxisListType.X

P = 128
B, T, E = 2, 1024, 256
G, QPG, D = 4, 4, 128
HEADS = G * QPG
KE = E // P
NT = T // P
CH = 512
NC = T // CH
TPC = CH // P
EXPERTS, O = 8, 256
EPS = 1e-5
SCALE = float(1.0 / np.sqrt(np.float32(D)))
MASKED = -3.0e38
FREE = 2
MIX = [0, 2, 1, 3, 4, 5, 6, 7]
BANK_READ = [max(MIX.index(2 * i), MIX.index(2 * i + 1)) + 1 for i in range(EXPERTS // 2)]
SA, CA, GA, SB, CB, GB = range(6)

STEPS = [(c, j) for c in range(NC) for j in range((c + 1) * TPC)]
NS = len(STEPS)
PT = 3
LAG = 2
LAST_STEP = [max(q for q in range(NS) if STEPS[q][0] == c) for c in range(NC)]
FIRST_TURN = NS - EXPERTS // 2 * KE
PIECES = []
for _i in range(NT):
    _w = (_i + 1) * P
    if _w <= CH:
        PIECES.append((_i, 0, max(_w, 2 * P), True))
    else:
        _a = CH if _w - CH >= 2 * P else _w - 2 * P
        PIECES += [(_i, 0, _a, False), (_i, _a, _w - _a, True)]
assert len(PIECES) == NS
FIRST_PIECE = [next(q for q in range(NS) if PIECES[q][0] == i) for i in range(NT)]


def score_offset(i):
    w = (i + 1) * P
    return CH - PIECES[FIRST_PIECE[i]][2] if w > CH else 0


def prob_offset(i):
    return P * i * (i + 1) // 2


PROBS = prob_offset(NT)


def position_table():
    f = np.float32
    pos = np.arange(T, dtype=f)[:, None]
    i = np.arange(0, D, 2, dtype=f)
    inv_freq = np.exp(-(np.log(f(10000.0)) * i / f(D))).astype(f)
    ang = (pos * inv_freq).astype(f)
    pe = np.zeros((T, D), f)
    pe[:, 0::2] = np.sin(ang)
    pe[:, 1::2] = np.cos(ang)
    return np.ascontiguousarray(pe.T)


def adaln_block(nc, x, wq, bq, wkv, bkv, wo, gate_w, expert_w, expert_b, c_in, wmod, out):
    ctx = ExitStack()
    with ctx:
        def sem(name):
            return ctx.enter_context(nc.semaphore(name))

        top = [-(-nc.sbuf_base // 64) * 64]

        def at(name, shape, dt, offset):
            return nc.alloc_sbuf_tensor_at(name, shape, dt, offset=offset)

        def sb(name, shape, dt=F32):
            size = int(np.prod(shape[1:])) * (2 if dt == BF16 else 4)
            offset = top[0]
            top[0] = -(-(offset + size) // 32) * 32
            assert top[0] <= nc.sbuf_usable_end, (name, top[0], nc.sbuf_usable_end)
            return at(name, shape, dt, offset)

        def here():
            return top[0]

        h_at = here()
        h_hi = sb("h_hi", [P, KE, B * T], F32R)
        h_lo = sb("h_lo", [P, KE, B * T], F32R)
        kv_at = here()
        k_hi = sb("k_hi", [P, G, T], F32R)
        k_lo = sb("k_lo", [P, G, T], F32R)
        v_hi = sb("v_hi", [P, NT, G, D], F32R)
        v_lo = sb("v_lo", [P, NT, G, D], F32R)
        acc_at = here()
        acc = sb("acc", [P, B * NT, E])
        p_at = here()
        probs = [sb(f"probs{i}", [P, PROBS]) for i in range(2)]
        pt_hi = sb("pt_hi", [P, PT, CH], F32R)
        pt_lo = sb("pt_lo", [P, PT, CH], F32R)
        pz_hi = sb("pz_hi", [P, 2 * P], F32R)
        pz_lo = sb("pz_lo", [P, 2 * P], F32R)
        q_at = here()
        q_hi = [sb(f"q_hi{i}", [P, T], F32R) for i in range(2)]
        q_lo = [sb(f"q_lo{i}", [P, T], F32R) for i in range(2)]
        raw = sb("raw", [P, 2, CH])
        o_hi = [sb(f"o_hi{c}", [P, CH], F32R) for c in range(NC)]
        o_lo = [sb(f"o_lo{c}", [P, CH], F32R) for c in range(NC)]
        wq_raw = sb("wq_raw", [P, KE, D])
        wq_hi = [sb(f"wq_hi{i}", [P, KE, D], F32R) for i in range(2)]
        wq_lo = [sb(f"wq_lo{i}", [P, KE, D], F32R) for i in range(2)]
        wo_raw = sb("wo_raw", [P, E])
        wo_hi = [sb(f"wo_hi{i}", [P, E], F32R) for i in range(2)]
        wo_lo = [sb(f"wo_lo{i}", [P, E], F32R) for i in range(2)]
        pos = sb("pos", [P, T])
        v_bias = sb("v_bias", [P, CH])
        ident = sb("ident", [P, P])
        ident_bf = sb("ident_bf", [P, P], BF16)
        mask_bf = sb("mask_bf", [P, P], BF16)
        qk_bias = sb("qk_bias", [P, HEADS + G])
        silu_c = sb("silu_c", [P, KE, B])
        modt = sb("modt", [P, 4, KE, B])
        gate_t = sb("gate_t", [P, KE, EXPERTS])
        neg_half = sb("neg_half", [P, B * NT])
        neg_max = sb("neg_max", [P, 2, NT])
        sums = sb("sums", [P, 2, NT])
        rsum = sb("rsum", [P, 2, NT])
        iota8 = sb("iota8", [P, EXPERTS])

        xs = acc
        wmod_sb = at("wmod_sb", [P, KE, 6 * E], F32, kv_at)
        bias_rows = at("bias_rows", [HEADS + G, D], F32, kv_at + 16384)
        c_rows = at("c_rows", [B, E], F32, kv_at + 17408)
        gate_rows = at("gate_rows", [EXPERTS, E], F32, kv_at + 18432)
        vb_row = at("vb_row", [1, CH], F32, kv_at + 20480)
        stats = at("stats", [P, B * NT, 6], F32, kv_at + 22528)
        mv = at("mv", [P, B * NT, 2], F32, kv_at + 23040)
        var_eps = at("var_eps", [P, B * NT], F32, kv_at + 23296)
        rstd = at("rstd", [P, B * NT], F32, kv_at + 23424)
        ones_row = at("ones_row", [1, P], F32, kv_at + 23616)
        sig_tmp = at("sig_tmp", [P, 3, KE * B], F32, kv_at + 23552)
        wkv_hi = at("wkv_hi", [P, KE, 2 * G * D], F32R, p_at)
        wkv_lo = at("wkv_lo", [P, KE, 2 * G * D], F32R, p_at + 8192)
        wkv_raw = [at("wkv_raw0", [P, KE, 2 * G * D], F32, p_at + 4 * PROBS),
                   at("wkv_raw1", [P, KE, 2 * G * D], F32, acc_at + 8192)]
        x_again = at("x_again", [P, B * NT, E], F32, h_at)
        we_raw = at("we_raw", [P, EXPERTS, KE, E], F32, h_at + 16384)
        we_hi = at("we_hi", [P, KE, EXPERTS, O], F32R, kv_at)
        we_lo = at("we_lo", [P, KE, EXPERTS, O], F32R, kv_at + 16384)
        gmod_w = at("gmod_w", [P, KE, 2, E], F32, q_at)
        gmod = at("gmod", [P, B, 2, E], F32, q_at + 4096)
        silu_b = at("silu_b", [P, KE, B, P], F32, q_at + 8192)
        ebias = at("ebias", [EXPERTS, O], F32, q_at + 8192 + 2048)
        moe_top = [p_at]

        def moe(name, shape, dt=F32):
            offset = moe_top[0]
            moe_top[0] += -(-int(np.prod(shape[1:])) * 4 // 32) * 32
            assert moe_top[0] <= p_at + 8 * PROBS
            return at(name, shape, dt, offset)

        g_sign = moe("g_sign", [P, B, 2, E])
        g_size = moe("g_size", [P, B, 2, E])
        xn2 = moe("xn2", [P, 2, E])
        h2 = moe("h2", [P, 2, KE, P])
        h2_hi = [moe(f"h2_hi{i}", [P, KE, P], F32R) for i in range(2)]
        h2_lo = [moe(f"h2_lo{i}", [P, KE, P], F32R) for i in range(2)]
        st2 = moe("st2", [P, 2, 6])
        mv2 = moe("mv2", [P, 2, 2])
        ve2 = moe("ve2", [P, 2, 1])
        rs2 = moe("rs2", [P, 2, 1])
        logits = moe("logits", [P, 2, EXPERTS])
        top_v = moe("top_v", [P, 2, 8])
        top_i = moe("top_i", [P, 2, 8], U32)
        top_f = moe("top_f", [P, 2, 2])
        gap = moe("gap", [P, 2, 1])
        egap = moe("egap", [P, 2, 1])
        wsum = moe("wsum", [P, 2, 1])
        wtop = moe("wtop", [P, 2, 2])
        coef1 = moe("coef1", [P, 2, EXPERTS])
        coef2 = moe("coef2", [P, 2, EXPERTS])
        coef = moe("coef", [P, 2, EXPERTS])
        assert moe_top[0] <= p_at + 4 * PROBS
        coef_t = moe("coef_t", [EXPERTS, 2, P])
        y_bias = moe("y_bias", [P, 2, O])
        y_even = moe("y_even", [P, 2, O])
        y_odd = moe("y_odd", [P, 2, O])
        y_sum = moe("y_sum", [P, 2, O])
        y_out = moe("y_out", [P, 2, O])

        ps_s = ctx.enter_context(nc.psum_tensor("ps_s", [P, 2, T], F32))
        ps_t = ctx.enter_context(nc.psum_tensor("ps_t", [P, 2, CH], F32))
        ps_o = ctx.enter_context(nc.psum_tensor("ps_o", [P, CH], F32))
        ps_m = ctx.enter_context(nc.psum_tensor("ps_m", [P, CH], F32))

        def kv_bank(u):
            return ps_s[:, (u % 4) // 2, (u % 2) * CH:(u % 2 + 1) * CH]

        x_in = [sem(f"x_in{i}") for i in range(4)]
        small_in, wmod_in, pos_in, wkv_in = sem("small_in"), sem("wmod_in"), sem("pos_in"), sem("wkv_in")
        const_set, pool_step, dve_step = sem("const_set"), sem("pool_step"), sem("dve_step")
        rows_t, rows_used, sig_exp, silu_set = sem("rows_t"), sem("rows_used"), sem("sig_exp"), sem("silu_set")
        modt_mm, modt_set, vb_mm, vb_set = sem("modt_mm"), sem("modt_set"), sem("vb_mm"), sem("vb_set")
        var_set, rstd_set, xn_set = sem("var_set"), sem("rstd_set"), sem("xn_set")
        ht_mm, ht_raw, ht_hi, ht_lo = sem("ht_mm"), sem("ht_raw"), sem("ht_hi"), sem("ht_lo")
        wkv_hi_set, wkv_lo_set = sem("wkv_hi_set"), sem("wkv_lo_set")
        kv_mm, kv_raw, kv_hi, kv_lo = sem("kv_mm"), sem("kv_raw"), sem("kv_hi"), sem("kv_lo")
        acc_zero = sem("acc_zero")
        wq_in, wo_in = sem("wq_in"), sem("wo_in")
        wq_cut, wo_cut, w_step = sem("wq_cut"), sem("wo_cut"), sem("w_step")
        q_mm, q_raw, q_hi_set, q_lo_set = sem("q_mm"), sem("q_raw"), sem("q_hi_set"), sem("q_lo_set")
        s_mm, max_set, exp_set = sem("s_mm"), sem("max_set"), sem("exp_set")
        t_mm, pt_hi_set, pt_lo_set, pv_mm = sem("t_mm"), sem("pt_hi_set"), sem("pt_lo_set"), sem("pv_mm")
        o_hi_set, o_lo_set = sem("o_hi_set"), sem("o_lo_set")
        rsum_set, y_mm, y_add = sem("rsum_set"), sem("y_mm"), sem("y_add")
        we_in, gmod_in = sem("we_in"), sem("gmod_in")
        gmod_step = sem("gmod_step")
        we_t, we_hi_set, we_lo_set = sem("we_t"), sem("we_hi_set"), sem("we_lo_set")
        silu_b_set, gmod_mm, gmod_set = sem("silu_b_set"), sem("gmod_mm"), sem("gmod_set")
        x_again_in = [sem(f"x_again_in{b}") for b in range(B)]
        xga_set, x1_set, ln_step, ve2_set, rs2_set = (sem("xga_set"), sem("x1_set"), sem("ln_step"),
                                                      sem("ve2_set"), sem("rs2_set"))
        xn2_set, h2_t, h2_set, h2_hi_set, h2_lo_set = (
            sem("xn2_set"), sem("h2_t"), sem("h2_set"), sem("h2_hi_set"), sem("h2_lo_set"))
        gate_mm, logits_set, gate_step, gap_set, egap_set = (
            sem("gate_mm"), sem("logits_set"), sem("gate_step"), sem("gap_set"), sem("egap_set"))
        coef_set, coef_mm, coef_t_set, yb_mm, yb_set = (
            sem("coef_set"), sem("coef_mm"), sem("coef_t_set"), sem("yb_mm"), sem("yb_set"))
        moe_mm, mixed, ysum_set, ysc_set, yout_set = (
            sem("moe_mm"), sem("mixed"), sem("ysum_set"), sem("ysc_set"), sem("yout_set"))
        seen, seen_pool = sem("seen"), sem("seen_pool")
        out_done = [sem(f"out_done{i}") for i in range(2)]

        pos_dram = nc.inline_tensor(position_table(), "position_table").ap()
        x_tiles = x.rearrange("b (n p) e -> p (b n) e", p=P)
        out_tiles = out.rearrange("b (n p) e -> p (b n) e", p=P)
        wq_h = wq.rearrange("(k p) (h d) -> p k h d", p=P, d=D)
        wo_h = wo.rearrange("(h d) e -> d h e", d=D)
        wkv_v = wkv.rearrange("(k p) n -> p k n", p=P)
        bkv_v = bkv.rearrange("(g two d) -> two g d", g=G, two=2)
        wmod_v = wmod.rearrange("(k p) (m e) -> p k m e", p=P, e=E)
        we_v = expert_w.rearrange("x (h p) d -> p x h d", p=P)

        block = ctx.enter_context(nc.Block())

        @block.sync
        def _(sp):
            for i in range(4):
                sp.dma_start(xs[:, 4 * i:4 * i + 4, :], x_tiles[:, 4 * i:4 * i + 4, :]).then_inc(x_in[i], 16)
            sp.dma_start(c_rows[:, :], c_in).then_inc(small_in, 16)
            sp.dma_start(bias_rows[0:HEADS, :], bq.rearrange("(h d) -> h d", d=D)).then_inc(small_in, 16)
            sp.dma_start(bias_rows[HEADS:HEADS + G, :], bkv_v[0, :, :]).then_inc(small_in, 16)
            sp.dma_start(vb_row[0:1, :].rearrange("o (g d) -> o g d", d=D), bkv_v[1:2, :, :]).then_inc(small_in, 16)
            sp.dma_start(gate_rows[:, :], gate_w).then_inc(small_in, 16)
            sp.dma_start(wmod_sb[:, :, :].rearrange("p k (m e) -> p k m e", e=E), wmod_v).then_inc(wmod_in, 16)
            sp.dma_start(wkv_raw[0][:, :, :], wkv_v).then_inc(wkv_in, 16)
            sp.dma_start(pos[:, :], pos_dram).then_inc(pos_in, 16)

            def load_head(n, r, g):
                if not (isinstance(n, int) and n == 0):
                    sp.wait_ge(wq_cut, n)
                sp.dma_start(wq_raw[:, :, :], wq_h[:, :, bass.ds(r + g * QPG, 1), :]
                             .rearrange("p k h d -> p k (h d)")).then_inc(wq_in, 16)
                if not (isinstance(n, int) and n == 0):
                    sp.wait_ge(wo_cut, n)
                sp.dma_start(wo_raw[:, :], wo_h[:, bass.ds(r + g * QPG, 1), :]
                             .rearrange("d h e -> d (h e)")).then_inc(wo_in, 16)

            for b in range(B):
                for g in range(G):
                    load_head(b * HEADS + g, 0, g)
                with sp.Fori(1, QPG) as r:
                    for g in range(G):
                        load_head(r * G + (b * HEADS + g), r, g)
                if b + 1 < B:
                    sp.wait_ge(ht_lo, B * NC * KE)
                    sp.dma_start(wkv_raw[1][:, :, :], wkv_v).then_inc(wkv_in, 16)

            sp.wait_ge(q_mm, NC * B * HEADS)
            sp.wait_ge(s_mm, NT * (B * HEADS - 1))
            for i, m in enumerate((GA, GB)):
                sp.dma_start(gmod_w[:, :, i, :], wmod_v[:, :, m, :]).then_inc(gmod_in, 16)
            sp.dma_start(ebias[:, :], expert_b).then_inc(gmod_in, 16)
            sp.dma_start(we_raw[:, :, :, :], we_v).then_inc(we_in, 16)
            for b in range(B):
                sp.dma_start(x_again[:, b * NT:(b + 1) * NT, :],
                             x_tiles[:, b * NT:(b + 1) * NT, :]).then_inc(x_again_in[b], 16)

            def store(n, par):
                sp.wait_ge(yout_set, n + 1)
                sp.dma_start(out_tiles[:, bass.ds(n, 1), :].rearrange("p n e -> p (n e)"),
                             y_out[:, par, :]).then_inc(out_done[par], 16)

            for i in range(2):
                sp.sem_inc(out_done[i], 16)
            with sp.Fori(0, B * NT // 2 - 1) as it:
                for par in range(2):
                    store(it * 2 + par, par)
            for par in range(2):
                store(B * NT - 2 + par, par)
            for i in range(2):
                sp.wait_ge(out_done[i], 16 * (B * NT // 2 + 1))

        @block.gpsimd
        def _(pool):
            pool.memset(ident[:, :], 0.0).then_inc(pool_step, 1)
            pool.memset(ident_bf[:, :], 0.0).then_inc(pool_step, 1)
            pool.memset(mask_bf[:, :], 0.0).then_inc(pool_step, 1)
            pool.wait_ge(pool_step, 3)
            pool.affine_select(out=ident[:, :], in_=ident[:, :], compare_op=ALU.not_equal, fill=1.0, base=0,
                               pattern=[[-1, P]], channel_multiplier=1).then_inc(const_set, 1)
            pool.affine_select(out=ident_bf[:, :], in_=ident_bf[:, :], compare_op=ALU.not_equal, fill=1.0, base=0,
                               pattern=[[-1, P]], channel_multiplier=1).then_inc(const_set, 1)
            pool.affine_select(out=mask_bf[:, :], in_=mask_bf[:, :], compare_op=ALU.is_ge, fill=MASKED, base=0,
                               pattern=[[-1, P]], channel_multiplier=1).then_inc(const_set, 1)
            pool.memset(ones_row[:, :], 1.0).then_inc(const_set, 1)
            pool.memset(neg_half[:, :], -0.5).then_inc(const_set, 1)
            pool.iota(iota8[:, :], pattern=[[1, EXPERTS]], base=0, channel_multiplier=0,
                      allow_small_or_imprecise_dtypes=True).then_inc(const_set, 1)
            for z in (pz_hi, pz_lo):
                pool.memset(z[:, :].bitcast(F32), 0.0).then_inc(const_set, 1)
            pool.wait_ge(const_set, 5)
            pool.wait_ge(var_set, 1)
            pool.tensor_tensor(rstd[:, :], var_eps[:, :], neg_half[:, :], ALU.pow).then_inc(rstd_set, 1)

            def cut_wkv(b):
                for k in range(KE):
                    for i in range(2 * G * D // CH):
                        part = slice(i * CH, (i + 1) * CH)
                        pool.wait_ge(wkv_hi_set, 4 * b + 2 * k + i + 1)
                        pool.tensor_tensor(wkv_lo[:, k, part], wkv_raw[b][:, k, part],
                                           wkv_hi[:, k, part].bitcast(F32), ALU.subtract).then_inc(wkv_lo_set, 1)

            def cut_head(n, par):
                pool.wait_ge(wq_in, (n + 1) * 16)
                if not (isinstance(n, int) and n < 2):
                    pool.wait_ge(q_mm, n * NC - 2)
                pool.sem_inc(seen_pool, 1)
                pool.tensor_scalar(wq_hi[par][:, :, :], wq_raw[:, :, :], 1.0, 1.0, ALU.mult, ALU.mult).then_inc(w_step, 1)
                pool.wait_ge(w_step, n * 2 + 1)
                pool.tensor_tensor(wq_lo[par][:, :, :], wq_raw[:, :, :], wq_hi[par][:, :, :].bitcast(F32),
                                   ALU.subtract).then_inc(wq_cut, 1)
                pool.wait_ge(wo_in, (n + 1) * 16)
                if not (isinstance(n, int) and n < 2):
                    pool.wait_ge(y_mm, n * 4 - 4)
                pool.sem_inc(seen_pool, 1)
                pool.tensor_scalar(wo_hi[par][:, :], wo_raw[:, :], 1.0, 1.0, ALU.mult, ALU.mult).then_inc(w_step, 1)
                pool.wait_ge(w_step, n * 2 + 2)
                pool.tensor_tensor(wo_lo[par][:, :], wo_raw[:, :], wo_hi[par][:, :].bitcast(F32),
                                   ALU.subtract).then_inc(wo_cut, 1)

            for b in range(B):
                cut_wkv(b)
                for g in range(G):
                    cut_head(b * HEADS + g, g % 2)
                with pool.Fori(1, QPG) as r:
                    for g in range(G):
                        cut_head(r * G + (b * HEADS + g), g % 2)

            def row(n):
                return acc[:, bass.ds(n, 1), :].rearrange("p n e -> p (n e)")

            def residual(n, b):
                pool.tensor_tensor(row(n), row(n), gmod[:, b, 0, :], ALU.mult).then_inc(xga_set, 1)
                pool.wait_ge(xga_set, n + 1)
                pool.sem_inc(seen_pool, 1)
                pool.tensor_tensor(row(n), row(n), x_again[:, bass.ds(n, 1), :].rearrange("p n e -> p (n e)"),
                                   ALU.add).then_inc(x1_set, 1)

            def inverse_deviation(n, par):
                pool.wait_ge(ve2_set, n + 1)
                pool.tensor_tensor(rs2[:, par, :], ve2[:, par, :], neg_half[:, 0:1], ALU.pow).then_inc(rs2_set, 1)

            def hidden_lo(n, par):
                pool.wait_ge(h2_hi_set, n + 1)
                pool.tensor_tensor(h2_lo[par][:, :, :], h2[:, par, :, :], h2_hi[par][:, :, :].bitcast(F32),
                                   ALU.subtract).then_inc(h2_lo_set, 1)

            def finish(n, b, par, use):
                pool.wait_ge(out_done[par], use * 16 + 16)
                pool.wait_ge(mixed, (n + 2) * EXPERTS)
                pool.tensor_tensor(y_sum[:, par, :], y_even[:, par, :], y_odd[:, par, :], ALU.add).then_inc(ysum_set, 1)
                pool.wait_ge(ysum_set, n + (FREE + 1))
                pool.tensor_tensor(y_sum[:, par, :], y_sum[:, par, :], gmod[:, b, 1, :], ALU.mult).then_inc(ysc_set, 1)
                pool.wait_ge(ysc_set, n + 1)
                pool.sem_inc(seen_pool, 1)
                pool.tensor_tensor(y_out[:, par, :], y_sum[:, par, :], row(n), ALU.add).then_inc(yout_set, 1)

            def slot(n, l, b, use):
                par = l % 2
                last = b + 1 == B
                if not (last and l + 2 >= NT):
                    inverse_deviation(n + 2, par)
                if not last:
                    residual(n + NT, b + 1)
                if not (last and l + 1 >= NT):
                    hidden_lo(n + 1, 1 - par)
                if l > 0:
                    finish(n - 1, b, 1 - par, use - 1 if par == 0 else use)
                elif b > 0:
                    finish(n - 1, b - 1, 1, use - 1)

            pool.sem_inc(ysum_set, FREE)
            pool.wait_ge(gmod_set, 1)
            pool.wait_ge(x_again_in[0], 16)
            for i in range(FREE + 1):
                residual(i, 0)
            for i in range(FREE):
                inverse_deviation(i, i)
            with pool.Fori(FREE + 1, NT) as n:
                residual(n, 0)
            hidden_lo(0, 0)
            pool.wait_ge(y_add, 4 * B * HEADS)
            pool.wait_ge(x_again_in[1], 16)
            for b in range(B):
                n0, u0 = b * NT, b * NT // 2
                slot(n0, 0, b, u0)
                slot(n0 + 1, 1, b, u0)
                with pool.Fori(1, NT // 2 - 1) as it:
                    slot(it * 2 + n0, 2, b, it + u0)
                    slot(it * 2 + (n0 + 1), 3, b, it + u0)
                slot(n0 + NT - 2, NT - 2, b, u0 + NT // 2 - 1)
                slot(n0 + NT - 1, NT - 1, b, u0 + NT // 2 - 1)
            finish(B * NT - 1, B - 1, 1, B * NT // 2 - 1)

        @block.tensor
        def _(pe):
            def product(out_ap, a, b, start, stop):
                nc.tensor.matmul(out_ap, a[1], b[0], start=start, stop=False)
                nc.tensor.matmul(out_ap, a[0], b[1], start=False, stop=False)
                return nc.tensor.matmul(out_ap, a[0], b[0], start=False, stop=stop)

            pe.wait_ge(const_set, 5)
            pe.wait_ge(small_in, 5 * 16)
            nb = HEADS + G
            pe.transpose(ps_m[:, 0:nb], bias_rows[:, :], ident[0:nb, 0:nb])
            for k in range(KE):
                pe.transpose(ps_m[:, 32 + B * k:32 + B * (k + 1)], c_rows[:, k * P:(k + 1) * P], ident[0:B, 0:B])
            for k in range(KE):
                last = pe.transpose(ps_m[:, 64 + EXPERTS * k:64 + EXPERTS * (k + 1)],
                                    gate_rows[:, k * P:(k + 1) * P], ident[0:EXPERTS, 0:EXPERTS])
            last.then_inc(rows_t, 1)
            pe.matmul(ps_o[:, :], ones_row[0:1, :], vb_row[0:1, :], start=True, stop=True).then_inc(vb_mm, 1)
            pe.wait_ge(silu_set, 1)
            pe.wait_ge(wmod_in, 16)
            pe.wait_ge(rows_used, 1)
            for i, m in enumerate((SA, CA, SB, CB)):
                for et in range(KE):
                    at_col = (i * KE + et) * B
                    for k in range(KE):
                        last = pe.matmul(ps_m[:, at_col:at_col + B],
                                         wmod_sb[:, k, m * E + et * P:m * E + (et + 1) * P], silu_c[:, k, :],
                                         start=k == 0, stop=k == KE - 1)
            last.then_inc(modt_mm, 1)
            for u in range(B * NC * KE):
                c, k = divmod(u, KE)
                pe.wait_ge(xn_set, TPC * (c + 1))
                if u >= 2:
                    pe.wait_ge(ht_raw, u - 1)
                for i in range(TPC):
                    last = pe.transpose(ps_t[:, u % 2, i * P:(i + 1) * P],
                                        xs[:, c * TPC + i, k * P:(k + 1) * P], ident[:, :])
                last.then_inc(ht_mm, 1)

            def queries(n, par, b, c):
                pe.wait_ge(wq_cut, n + 1)
                tokens = slice(b * T + c * CH, b * T + (c + 1) * CH)
                for k in range(KE):
                    last = product(ps_m[:, :], (wq_hi[par][:, k, :], wq_lo[par][:, k, :]),
                                   (h_hi[:, k, tokens], h_lo[:, k, tokens]), k == 0, k == KE - 1)
                last.then_inc(q_mm, 1)

            def score_piece(n, par, g, q, first):
                i, c0, w, ends = PIECES[q]
                if i % TPC == 0 and q == FIRST_PIECE[i]:
                    pe.wait_ge(q_lo_set, n * NC + (i // TPC + 1))
                if q == FIRST_PIECE[i] and not (first and i < 2):
                    pe.wait_ge(exp_set, n * NT + (i - 1))
                rows = slice(i * P, (i + 1) * P)
                col = score_offset(i) + c0
                keys = slice(c0, c0 + w)
                last = product(ps_s[:, i % 2, col:col + w], (q_hi[par][:, rows], q_lo[par][:, rows]),
                               (k_hi[:, g, keys], k_lo[:, g, keys]), True, not ends)
                if ends:
                    diag = score_offset(i) + i * P
                    pe.matmul(ps_s[:, i % 2, diag:diag + P], ident_bf[:, :], mask_bf[:, :],
                              start=False, stop=True).then_inc(s_mm, 1)

            def turn_probs(n, par, q, first):
                c, j = STEPS[q]
                if j == 0:
                    pe.wait_ge(exp_set, n * NT + (c + 1) * TPC)
                if not (first and q < 2):
                    pe.wait_ge(pt_lo_set, n * NS + (q - 1))
                for i in range(max(j, c * TPC), (c + 1) * TPC):
                    p0 = prob_offset(i) + j * P
                    col = (i - c * TPC) * P
                    last = pe.transpose(ps_t[:, q % 2, col:col + P], probs[par][:, p0:p0 + P], ident[:, :])
                last.then_inc(t_mm, 1)

            def weigh_values(n, g, q, first):
                c, j = STEPS[q]
                pe.wait_ge(pt_lo_set, n * NS + (q + 1))
                if j == 0 and not (first and c == 0):
                    pe.wait_ge(o_lo_set, n * NC + c)
                v = (v_hi[:, j, g, :], v_lo[:, j, g, :])
                if q in LAST_STEP:
                    last = product(ps_o[:, CH - 2 * P:CH], v, (pz_hi[:, :], pz_lo[:, :]), False, True)
                else:
                    lo = (max(j, c * TPC) - c * TPC) * P
                    last = product(ps_o[:, lo:CH], v, (pt_hi[:, q % PT, lo:CH], pt_lo[:, q % PT, lo:CH]),
                                   j == 0, False)
                last.then_inc(pv_mm, 1)

            def project(n, par, c, pair):
                if pair == 0:
                    pe.wait_ge(o_lo_set, n * NC + (c + 1))
                    if c == 0:
                        pe.wait_ge(wo_cut, n + 1)
                for i in range(2):
                    rows = slice((2 * pair + i) * P, (2 * pair + i + 1) * P)
                    last = product(ps_m[:, i * E:(i + 1) * E], (o_hi[c][:, rows], o_lo[c][:, rows]),
                                   (wo_hi[par][:, :], wo_lo[par][:, :]), True, True)
                last.then_inc(y_mm, 1)

            def turn_weights(u):
                e2, k = divmod(u, KE)
                if u == 0:
                    pe.wait_ge(we_in, 16)
                    pe.wait_ge(exp_set, NT * B * HEADS)
                if u >= 2:
                    pe.wait_ge(we_lo_set, u - 1)
                for i in range(2):
                    for h in range(KE):
                        col = (i * KE + h) * P
                        last = pe.transpose(kv_bank(2 + u % 2)[:, col:col + P],
                                            we_raw[:, 2 * e2 + i, h, k * P:(k + 1) * P], ident[:, :])
                last.then_inc(we_t, 1)

            def modulation_rows():
                pe.wait_ge(silu_b_set, 1)
                pe.wait_ge(gmod_in, 48)
                pe.wait_ge(exp_set, NT * B * HEADS - 1)
                for b in range(B):
                    for m in range(2):
                        for k in range(KE):
                            last = pe.matmul(ps_s[:, 0, (b * 2 + m) * E:(b * 2 + m + 1) * E], silu_b[:, k, b, :],
                                             gmod_w[:, k, m, :], start=k == 0, stop=k == KE - 1)
                last.then_inc(gmod_mm, 1)

            def frame(n, l, b):
                very_last = b + 1 == B and l + 1 == HEADS
                par, g = l % 2, l % G
                prev, nxt, nxt2 = l > 0, l + 1 < HEADS, l + 2 < HEADS
                first = isinstance(n, int) and n == 0
                for q in range(NS):
                    turn_probs(n, par, q, first)
                    if q == 0 and nxt:
                        pe.wait_ge(q_raw, n * NC + 3)
                        queries(n + 1, 1 - par, b, 1)
                    if q == 10 and nxt2:
                        pe.wait_ge(y_add, n * 4 + 2)
                        queries(n + 2, par, b, 0)
                    if nxt:
                        score_piece(n + 1, 1 - par, (l + 1) % G, q, False)
                    if q == 3 and prev:
                        if nxt:
                            pe.wait_ge(q_raw, n * NC + 4)
                        else:
                            pe.wait_ge(y_add, n * 4 - 2)
                        project(n - 1, 1 - par, 1, 0)
                    if q == 6 and prev:
                        pe.wait_ge(y_add, n * 4 - 1)
                        project(n - 1, 1 - par, 1, 1)
                    if q == 0 and prev:
                        for p in range(NS - LAG, NS):
                            weigh_values(n - 1, (l - 1) % G, p, False)
                    if q >= LAG:
                        weigh_values(n, g, q - LAG, first)
                    if q == 7:
                        if prev:
                            pe.wait_ge(y_add, n * 4)
                        else:
                            pe.wait_ge(q_raw, n * NC + 4)
                        project(n, par, 0, 0)
                    if q == 8:
                        pe.wait_ge(y_add, n * 4 + 1)
                        project(n, par, 0, 1)
                    if very_last and q == 1:
                        modulation_rows()
                    if very_last and q >= FIRST_TURN:
                        turn_weights(q - FIRST_TURN)

            def turn_hidden(n, par):
                pe.wait_ge(xn2_set, n + 1)
                for k in range(KE):
                    last = pe.transpose(ps_t[:, par, k * P:(k + 1) * P], xn2[:, par, k * P:(k + 1) * P], ident[:, :])
                last.then_inc(h2_t, 1)

            def gate(n, par):
                pe.wait_ge(h2_set, n * KE + KE)
                if isinstance(n, int) and n == 0:
                    pe.wait_ge(o_hi_set, NC * B * HEADS)
                else:
                    pe.wait_ge(logits_set, n)
                for k in range(KE):
                    last = pe.matmul(ps_o[:, 0:EXPERTS], h2[:, par, k, :], gate_t[:, k, :],
                                     start=k == 0, stop=k == KE - 1)
                last.then_inc(gate_mm, 1)

            for b in range(B):
                n0 = b * HEADS
                pe.wait_ge(wkv_lo_set, 4 * (b + 1))
                if b == 0:
                    pe.wait_ge(ht_lo, B * NC * KE)
                else:
                    pe.wait_ge(exp_set, n0 * NT)
                for u in range(G * NC + NT):
                    if u >= 4:
                        pe.wait_ge(kv_raw, 16 * b + u - 3)
                    for k in range(KE):
                        if u < G * NC:
                            g, c = divmod(u, NC)
                            wcols = slice(2 * g * D, (2 * g + 1) * D)
                            tokens = slice(b * T + c * CH, b * T + (c + 1) * CH)
                            last = product(kv_bank(u), (wkv_hi[:, k, wcols], wkv_lo[:, k, wcols]),
                                           (h_hi[:, k, tokens], h_lo[:, k, tokens]), k == 0, k == KE - 1)
                        else:
                            s = b * T + (u - G * NC) * P
                            wv = [w[:, k, :].rearrange("p (g two d) -> p g two d", g=G, two=2)[:, :, 1, :]
                                  for w in (wkv_hi, wkv_lo)]
                            last = product(kv_bank(u), (h_hi[:, k, s:s + P], h_lo[:, k, s:s + P]), wv,
                                           k == 0, k == KE - 1)
                    last.then_inc(kv_mm, 1)
                if b == 0:
                    pe.wait_ge(modt_set, 1)
                else:
                    pe.wait_ge(y_add, n0 * 4)
                queries(n0, 0, b, 0)
                pe.wait_ge(q_raw, n0 * NC + 1)
                queries(n0, 0, b, 1)
                pe.wait_ge(q_raw, n0 * NC + 2)
                queries(n0 + 1, 1, b, 0)
                pe.wait_ge(kv_lo, 16 * (b + 1))
                for q in range(NS):
                    score_piece(n0, 0, 0, q, b == 0)
                frame(n0, 0, b)
                with pe.Fori(0, (HEADS - 4) // G) as it:
                    for s in range(G):
                        frame(it * G + (n0 + 1 + s), 1 + s, b)
                for l in range(HEADS - 3, HEADS):
                    frame(n0 + l, l, b)
                n = n0 + HEADS - 1
                for q in range(NS - LAG, NS):
                    weigh_values(n, G - 1, q, False)
                for pair in range(2):
                    if b + 1 == B:
                        (turn_hidden, gate)[pair](0, 0)
                    pe.wait_ge(y_add, n * 4 + 2 + pair)
                    project(n, 1, 1, pair)

            def turn_coef(n, par):
                pe.wait_ge(coef_set, n + 1)
                pe.wait_ge(yb_set, n + 1)
                pe.transpose(ps_m[0:EXPERTS, 0:P], coef[:, par, :], ident[:, :]).then_inc(coef_mm, 1)

            def mix_bias(n, par):
                pe.wait_ge(coef_t_set, n + 1)
                pe.matmul(ps_m[:, 0:O], coef_t[:, par, :], ebias[:, :], start=True, stop=True).then_inc(yb_mm, 1)

            def experts(n, par, e2):
                if e2 == 0:
                    pe.wait_ge(h2_lo_set, n + 1)
                pe.wait_ge(mixed, n * EXPERTS + BANK_READ[e2])
                for k in range(KE):
                    w = [t[:, k, 2 * e2:2 * e2 + 2, :].rearrange("p x o -> p (x o)") for t in (we_hi, we_lo)]
                    last = product(kv_bank(e2), (h2_hi[par][:, k, :], h2_lo[par][:, k, :]), w, k == 0, k == KE - 1)
                last.then_inc(moe_mm, 1)

            def slot(n, par, more):
                turn_coef(n, par)
                experts(n, par, 0)
                mix_bias(n, par)
                if more:
                    turn_hidden(n + 1, 1 - par)
                experts(n, par, 1)
                if more:
                    gate(n + 1, 1 - par)
                experts(n, par, 2)
                experts(n, par, 3)

            pe.sem_inc(moe_mm, FREE * EXPERTS // 2)
            pe.wait_ge(we_lo_set, 8)
            pe.wait_ge(gmod_set, 1)
            pe.wait_ge(y_add, 4 * B * HEADS)
            with pe.Fori(0, B * NT // 2 - 1) as it:
                slot(it * 2, 0, True)
                slot(it * 2 + 1, 1, True)
            slot(B * NT - 2, 0, True)
            slot(B * NT - 1, 1, False)

        @block.scalar
        def _(act):
            def keep_hi(dst, src, scale=1.0):
                return nc.scalar.activation(dst, src, ACT.Copy, scale=scale)

            act.wait_ge(rows_used, 1)
            nc.scalar.activation(sig_tmp[:, 0, :], silu_c[:, :, :].rearrange("p k b -> p (k b)"), ACT.Exp,
                                 scale=-1.0).then_inc(sig_exp, 1)

            def cut_wkv(b):
                act.wait_ge(wkv_in, 16 * (b + 1))
                for k in range(KE):
                    for i in range(2 * G * D // CH):
                        part = slice(i * CH, (i + 1) * CH)
                        keep_hi(wkv_hi[:, k, part], wkv_raw[b][:, k, part]).then_inc(wkv_hi_set, 1)

            cut_wkv(0)
            for u in range(B * NC * KE):
                c, k = divmod(u, KE)
                act.wait_ge(ht_raw, u + 1)
                keep_hi(h_hi[:, k, c * CH:(c + 1) * CH], raw[:, u % 2, :]).then_inc(ht_hi, 1)

            def exponentials(n, par, i):
                w = (i + 1) * P
                act.wait_ge(max_set, n * NT + (i + 1))
                col = score_offset(i)
                nc.scalar.activation(probs[par][:, prob_offset(i):prob_offset(i) + w], ps_s[:, i % 2, col:col + w],
                                     ACT.Exp, bias=neg_max[:, par, i:i + 1],
                                     accum_out=sums[:, par, i:i + 1]).then_inc(exp_set, 1)

            def probs_hi(n, q, first):
                c, j = STEPS[q]
                act.wait_ge(t_mm, n * NS + (q + 1))
                if not (first and q < PT):
                    act.wait_ge(pv_mm, n * NS + (q - PT + 1))
                lo = (max(j, c * TPC) - c * TPC) * P
                dst = pz_hi[:, P:2 * P] if q in LAST_STEP else pt_hi[:, q % PT, lo:CH]
                keep_hi(dst, ps_t[:, q % 2, lo:CH]).then_inc(pt_hi_set, 1)

            def output_hi(n, c, first):
                act.wait_ge(pv_mm, n * NS + (LAST_STEP[c] + 1))
                if not first:
                    act.wait_ge(y_mm, n * 4 + (2 * c - 2))
                keep_hi(o_hi[c][:, :], ps_o[:, :]).then_inc(o_hi_set, 1)

            def queries_hi(n, par, c):
                act.wait_ge(q_raw, n * NC + (c + 1))
                keep_hi(q_hi[par][:, c * CH:(c + 1) * CH], raw[:, c, :], SCALE).then_inc(q_hi_set, 1)

            def frame(n, l, b):
                par = l % 2
                prev, nxt, nxt2 = l > 0, l + 1 < HEADS, l + 2 < HEADS
                first = isinstance(n, int) and n == 0
                for q in range(NS):
                    if q == 1 and prev:
                        output_hi(n - 1, 1, isinstance(n, int) and n == 1)
                    probs_hi(n, q, first)
                    if q == LAST_STEP[0] + LAG:
                        output_hi(n, 0, first)
                    if q == 0 and prev:
                        exponentials(n, par, NT - 1)
                    if q == 0 and nxt:
                        exponentials(n + 1, 1 - par, 0)
                    if q > 1 and nxt and PIECES[q - 1][3]:
                        exponentials(n + 1, 1 - par, PIECES[q - 1][0])
                    if q == 1 and nxt:
                        queries_hi(n + 1, 1 - par, 1)
                    if q == 11 and nxt2:
                        queries_hi(n + 2, par, 0)
                    if b + 1 == B and l + 1 == HEADS and q >= FIRST_TURN:
                        weights_hi(q - FIRST_TURN)

            def weights_hi(u):
                e2, k = divmod(u, KE)
                act.wait_ge(we_t, u + 1)
                keep_hi(we_hi[:, k, 2 * e2:2 * e2 + 2, :].rearrange("p x o -> p (x o)"),
                        kv_bank(2 + u % 2)).then_inc(we_hi_set, 1)

            for b in range(B):
                n0 = b * HEADS
                for u in range(G * NC + NT):
                    act.wait_ge(kv_raw, 16 * b + u + 1)
                    if u < G * NC:
                        g, c = divmod(u, NC)
                        dst = k_hi[:, g, c * CH:(c + 1) * CH]
                    else:
                        dst = v_hi[:, u - G * NC, :, :].rearrange("p g d -> p (g d)")
                    keep_hi(dst, raw[:, u % 2, :]).then_inc(kv_hi, 1)
                queries_hi(n0, 0, 0)
                queries_hi(n0, 0, 1)
                queries_hi(n0 + 1, 1, 0)
                for i in range(NT):
                    exponentials(n0, 0, i)
                frame(n0, 0, b)
                with act.Fori(0, (HEADS - 4) // G) as it:
                    for s in range(G):
                        frame(it * G + (n0 + 1 + s), 1 + s, b)
                for l in range(HEADS - 3, HEADS):
                    frame(n0 + l, l, b)
                if b + 1 < B:
                    act.wait_ge(t_mm, (n0 + HEADS - 1) * NS)
                    cut_wkv(1)
                output_hi(n0 + HEADS - 1, 1, False)

            def stage_a(n, b, par):
                act.wait_ge(h2_t, n + 1)
                for k in range(KE):
                    nc.scalar.activation(h2[:, par, k, :], ps_t[:, par, k * P:(k + 1) * P], ACT.Identity,
                                         scale=modt[:, 3, k, b:b + 1], bias=modt[:, 2, k, b:b + 1]).then_inc(h2_set, 1)
                act.wait_ge(h2_set, n * KE + KE)
                act.wait_ge(moe_mm, (n + 1) * 4)
                keep_hi(h2_hi[par][:, :, :], h2[:, par, :, :]).then_inc(h2_hi_set, 1)
                act.wait_ge(gate_mm, n + 1)
                nc.scalar.activation(logits[:, par, :], ps_o[:, 0:EXPERTS], ACT.Copy).then_inc(logits_set, 1)
                act.wait_ge(gap_set, n + 1)
                nc.scalar.activation(egap[:, par, :], gap[:, par, :], ACT.Exp).then_inc(egap_set, 1)

            def mix_bias(n, par):
                act.wait_ge(coef_mm, n + 1)
                nc.scalar.activation(coef_t[:, par, :], ps_m[0:EXPERTS, 0:P], ACT.Copy).then_inc(coef_t_set, 1)
                act.wait_ge(yb_mm, n + 1)
                nc.scalar.activation(y_bias[:, par, :], ps_m[:, 0:O], ACT.Copy).then_inc(yb_set, 1)

            def slot(n, l, b):
                mix_bias(n, l % 2)
                if l + 1 < NT:
                    stage_a(n + 1, b, (l + 1) % 2)
                elif b + 1 < B:
                    stage_a(n + 1, b + 1, 0)

            act.sem_inc(yb_set, 1)
            stage_a(0, 0, 0)
            for b in range(B):
                n0 = b * NT
                with act.Fori(0, NT // 2 - 1) as it:
                    for par in range(2):
                        slot(it * 2 + (n0 + par), par, b)
                for l in range(NT - 2, NT):
                    slot(n0 + l, l, b)

        @block.vector
        def _(dve):
            dve.wait_ge(rows_t, 1)
            nc.vector.tensor_copy(qk_bias[:, :], ps_m[:, 0:HEADS + G]).then_inc(dve_step, 1)
            nc.vector.tensor_copy(gate_t[:, :, :].rearrange("p k e -> p (k e)"),
                                  ps_m[:, 64:64 + KE * EXPERTS]).then_inc(dve_step, 1)
            nc.vector.tensor_copy(silu_c[:, :, :].rearrange("p k b -> p (k b)"),
                                  ps_m[:, 32:32 + KE * B]).then_inc(rows_used, 1)
            dve.wait_ge(vb_mm, 1)
            nc.vector.tensor_copy(v_bias[:, :], ps_o[:, :]).then_inc(vb_set, 1)
            dve.wait_ge(sig_exp, 1)
            nc.vector.tensor_scalar(sig_tmp[:, 1, :], sig_tmp[:, 0, :], 1.0, None, ALU.add).then_inc(dve_step, 1)
            dve.wait_ge(dve_step, 3)
            nc.vector.reciprocal(sig_tmp[:, 2, :], sig_tmp[:, 1, :]).then_inc(dve_step, 1)
            dve.wait_ge(dve_step, 4)
            flat_c = silu_c[:, :, :].rearrange("p k b -> p (k b)")
            nc.vector.tensor_tensor(flat_c, flat_c, sig_tmp[:, 2, :], ALU.mult).then_inc(silu_set, 1)
            for i in range(B * NT):
                if i % 4 == 0:
                    dve.wait_ge(x_in[i // 4], 16)
                nc.vector.bn_stats(stats[:, i, :], xs[:, i, :]).then_inc(ln_step, 1)
            for i in range(B * NT):
                dve.wait_ge(ln_step, i + 1)
                nc.vector.bn_aggr(mv[:, i, :], stats[:, i, :]).then_inc(dve_step, 1)
            dve.wait_ge(dve_step, 4 + B * NT)
            nc.vector.tensor_scalar(var_eps[:, :], mv[:, :, 1], EPS, None, ALU.add).then_inc(var_set, 1)
            dve.wait_ge(modt_mm, 1)
            for i in range(4):
                cols = slice(i * KE * B, (i + 1) * KE * B)
                last = nc.vector.tensor_scalar(modt[:, i, :, :].rearrange("p k b -> p (k b)"), ps_m[:, cols],
                                               float(i % 2), None, ALU.add)
            last.then_inc(modt_set, 1)
            dve.wait_ge(rstd_set, 1)
            for i in range(B * NT):
                nc.vector.tensor_scalar(xs[:, i, :], xs[:, i, :], mv[:, i, 0:1], rstd[:, i:i + 1],
                                        ALU.subtract, ALU.mult).then_inc(xn_set, 1)
            dve.wait_ge(modt_set, 1)

            def hidden_lo(u):
                c, k = divmod(u, KE)
                part = slice(c * CH, (c + 1) * CH)
                dve.wait_ge(ht_hi, u + 1)
                nc.vector.tensor_tensor(h_lo[:, k, part], raw[:, u % 2, :], h_hi[:, k, part].bitcast(F32),
                                        ALU.subtract).then_inc(ht_lo, 1)

            for u in range(B * NC * KE):
                c, k = divmod(u, KE)
                b = c // NC
                dve.wait_ge(ht_mm, u + 1)
                if u >= 2:
                    dve.wait_ge(ht_lo, u - 1)
                nc.vector.tensor_scalar(raw[:, u % 2, :], ps_t[:, u % 2, :], modt[:, 1, k, b:b + 1],
                                        modt[:, 0, k, b:b + 1], ALU.mult, ALU.add).then_inc(ht_raw, 1)
                if u >= 1:
                    hidden_lo(u - 1)
            hidden_lo(B * NC * KE - 1)

            def kv_part(b, u):
                if u < G * NC:
                    g, c = divmod(u, NC)
                    return [t[:, g, c * CH:(c + 1) * CH] for t in (k_hi, k_lo)]
                return [t[:, u - G * NC, :, :].rearrange("p g d -> p (g d)") for t in (v_hi, v_lo)]

            def kv_cut(b, u):
                hi, lo = kv_part(b, u)
                dve.wait_ge(kv_hi, 16 * b + u + 1)
                nc.vector.tensor_tensor(lo, raw[:, u % 2, :], hi.bitcast(F32), ALU.subtract).then_inc(kv_lo, 1)

            def maxima(n, par, i):
                w = (i + 1) * P
                dve.wait_ge(s_mm, n * NT + (i + 1))
                col = score_offset(i)
                nc.vector.tensor_reduce(neg_max[:, par, i:i + 1], ps_s[:, i % 2, col:col + w], AXIS_X, ALU.max,
                                        negate=True).then_inc(max_set, 1)

            def probs_lo(n, q):
                c, j = STEPS[q]
                dve.wait_ge(pt_hi_set, n * NS + (q + 1))
                lo = (max(j, c * TPC) - c * TPC) * P
                hi_t, lo_t = [(z[:, P:2 * P] if q in LAST_STEP else t[:, q % PT, lo:CH])
                              for z, t in ((pz_hi, pt_hi), (pz_lo, pt_lo))]
                nc.vector.tensor_tensor(lo_t, ps_t[:, q % 2, lo:CH], hi_t.bitcast(F32),
                                        ALU.subtract).then_inc(pt_lo_set, 1)

            def output_lo(n, c):
                dve.wait_ge(o_hi_set, n * NC + (c + 1))
                nc.vector.tensor_tensor(o_lo[c][:, :], ps_o[:, :], o_hi[c][:, :].bitcast(F32),
                                        ALU.subtract).then_inc(o_lo_set, 1)

            def queries_raw(n, g, b, c, r, after_kv=False):
                head = r + g * QPG
                bias = qk_bias[:, head:head + 1] if isinstance(head, int) else qk_bias[:, bass.ds(head, 1)]
                if after_kv:
                    dve.wait_ge(kv_lo, 16 * (b + 1))
                else:
                    dve.wait_ge(q_lo_set, n * NC + (c - 1))
                dve.wait_ge(q_mm, n * NC + (c + 1))
                nc.vector.scalar_tensor_tensor(raw[:, c, :], ps_m[:, :], bias, pos[:, c * CH:(c + 1) * CH],
                                               ALU.add, ALU.add).then_inc(q_raw, 1)

            def queries_lo(n, par, c):
                part = slice(c * CH, (c + 1) * CH)
                dve.wait_ge(q_hi_set, n * NC + (c + 1))
                nc.vector.scalar_tensor_tensor(q_lo[par][:, part], raw[:, c, :], SCALE,
                                               q_hi[par][:, part].bitcast(F32), ALU.mult,
                                               ALU.subtract).then_inc(q_lo_set, 1)

            def sum_inverse(n, par, c):
                part = slice(c * TPC, (c + 1) * TPC)
                dve.wait_ge(exp_set, n * NT + (c + 1) * TPC)
                nc.vector.reciprocal(rsum[:, par, part], sums[:, par, part]).then_inc(rsum_set, 1)

            def add_projection(n, par, b, c, pair):
                dve.wait_ge(y_mm, n * 4 + (2 * c + pair + 1))
                if pair == 0:
                    dve.wait_ge(rsum_set, n * NC + (c + 1))
                for i in range(2):
                    tile = c * TPC + 2 * pair + i
                    row = acc[:, b * NT + tile, :]
                    last = nc.vector.scalar_tensor_tensor(row, ps_m[:, i * E:(i + 1) * E],
                                                          rsum[:, par, tile:tile + 1], row, ALU.mult, ALU.add)
                last.then_inc(y_add, 1)

            def frame(n, l, b, r):
                par, g = l % 2, l % G
                prev, nxt, nxt2 = l > 0, l + 1 < HEADS, l + 2 < HEADS
                for q in range(NS):
                    if q == 1 and prev:
                        output_lo(n - 1, 1)
                    if q == 1 and nxt:
                        maxima(n + 1, 1 - par, 1)
                    probs_lo(n, q)
                    if q == LAST_STEP[0] + LAG:
                        output_lo(n, 0)
                    if q == 10 and nxt2:
                        queries_raw(n + 2, (l + 2) % G, b, 0, r(2))
                    if q != 1 and nxt and PIECES[q][3]:
                        maxima(n + 1, 1 - par, PIECES[q][0])
                    if q == 11 and nxt2:
                        queries_lo(n + 2, par, 0)
                    if q == 2:
                        sum_inverse(n, par, 0)
                    if q == 6:
                        sum_inverse(n, par, 1)
                    if q == 0 and nxt:
                        queries_raw(n + 1, (l + 1) % G, b, 1, r(1))
                    if q == 2 and nxt:
                        queries_lo(n + 1, 1 - par, 1)
                    if q == 3 and prev:
                        add_projection(n - 1, 1 - par, b, 1, 0)
                    if q == 6 and prev:
                        add_projection(n - 1, 1 - par, b, 1, 1)
                    if q == 7:
                        add_projection(n, par, b, 0, 0)
                    if q == 8:
                        add_projection(n, par, b, 0, 1)
                    if b + 1 == B and l + 1 == HEADS:
                        if q == 0:
                            repeat_silu()
                        if 2 <= q < 6:
                            modulation_part(q - 2)
                        if q >= FIRST_TURN:
                            weights_lo(q - FIRST_TURN)
                        if q >= NS - FREE:
                            statistics(q - NS + FREE, q - NS + FREE)

            def repeat_silu():
                for k in range(KE):
                    for b in range(B):
                        last = nc.vector.tensor_scalar(silu_b[:, k, b, :], ident[:, :], 0.0, silu_c[:, k, b:b + 1],
                                                       ALU.mult, ALU.add)
                last.then_inc(silu_b_set, 1)

            def weights_lo(u):
                e2, k = divmod(u, KE)
                dve.wait_ge(we_hi_set, u + 1)
                hi, lo = [t[:, k, 2 * e2:2 * e2 + 2, :].rearrange("p x o -> p (x o)") for t in (we_hi, we_lo)]
                nc.vector.tensor_tensor(lo, kv_bank(2 + u % 2), hi.bitcast(F32), ALU.subtract).then_inc(we_lo_set, 1)

            def modulation_part(i):
                g = ps_s[:, 0, :]
                sign, size, both = [t[:, :, :, :].rearrange("p b m e -> p (b m e)") for t in (g_sign, g_size, gmod)]
                if i == 0:
                    dve.wait_ge(gmod_mm, 1)
                    nc.vector.tensor_scalar(sign, g, 0.0, 2.0, ALU.is_ge, ALU.mult).then_inc(gmod_step, 1)
                elif i == 1:
                    nc.vector.tensor_scalar(size, g, -1.0, 0.25, ALU.mult, ALU.max).then_inc(gmod_step, 1)
                elif i == 2:
                    dve.wait_ge(gmod_step, 2)
                    nc.vector.tensor_tensor(size, g, size, ALU.max).then_inc(gmod_step, 1)
                else:
                    dve.wait_ge(gmod_step, 3)
                    nc.vector.scalar_tensor_tensor(both, sign, -1.0, size, ALU.add, ALU.mult).then_inc(gmod_set, 1)

            def row(n):
                return acc[:, bass.ds(n, 1), :].rearrange("p n e -> p (n e)")

            def statistics(n, par):
                if not (isinstance(n, int) and n < 2):
                    dve.wait_ge(xn2_set, n - 1)
                dve.wait_ge(x1_set, n + 1)
                nc.vector.bn_stats(st2[:, par, :], row(n)).then_inc(ln_step, 1)
                dve.wait_ge(ln_step, n * 2 + (B * NT + 1))
                dve.sem_inc(seen, 1)
                nc.vector.bn_aggr(mv2[:, par, :], st2[:, par, :]).then_inc(ln_step, 1)
                dve.wait_ge(ln_step, n * 2 + (B * NT + 2))
                nc.vector.tensor_scalar(ve2[:, par, :], mv2[:, par, 1:2], EPS, None, ALU.add).then_inc(ve2_set, 1)

            def normalise(n, par):
                if not (isinstance(n, int) and n < 2):
                    dve.wait_ge(h2_t, n - 1)
                dve.wait_ge(rs2_set, n + 1)
                nc.vector.tensor_scalar(xn2[:, par, :], row(n), mv2[:, par, 0:1], rs2[:, par, :],
                                        ALU.subtract, ALU.mult).then_inc(xn2_set, 1)

            for b in range(B):
                n0 = b * HEADS
                if b == 0:
                    dve.wait_ge(pos_in, 16)
                    dve.wait_ge(vb_set, 1)
                for u in range(G * NC + NT):
                    if u >= 2:
                        dve.wait_ge(kv_lo, 16 * b + u - 1)
                    elif b == 0:
                        dve.wait_ge(ht_lo, B * NC * KE)
                    else:
                        dve.wait_ge(q_lo_set, n0 * NC)
                    dve.wait_ge(kv_mm, 16 * b + u + 1)
                    if u < G * NC:
                        g, c = divmod(u, NC)
                        last = nc.vector.scalar_tensor_tensor(raw[:, u % 2, :], kv_bank(u),
                                                              qk_bias[:, HEADS + g:HEADS + g + 1],
                                                              pos[:, c * CH:(c + 1) * CH], ALU.add, ALU.add)
                    else:
                        last = nc.vector.tensor_tensor(raw[:, u % 2, :], kv_bank(u), v_bias[:, :], ALU.add)
                    last.then_inc(kv_raw, 1)
                    if u >= 1:
                        kv_cut(b, u - 1)
                kv_cut(b, G * NC + NT - 1)
                queries_raw(n0, 0, b, 0, 0, after_kv=True)
                queries_raw(n0, 0, b, 1, 0, after_kv=True)
                queries_lo(n0, 0, 0)
                queries_raw(n0 + 1, 1, b, 0, 0)
                queries_lo(n0, 0, 1)
                queries_lo(n0 + 1, 1, 0)
                dve.wait_ge(wkv_lo_set, 4 * (b + 1))
                nc.vector.memset(acc[:, b * NT:(b + 1) * NT, :], 0.0).then_inc(acc_zero, 1)
                for i in range(NT):
                    maxima(n0, 0, i)
                dve.wait_ge(acc_zero, b + 1)
                frame(n0, 0, b, lambda d: d // G)
                with dve.Fori(0, (HEADS - 4) // G) as it:
                    for s in range(G):
                        frame(it * G + (n0 + 1 + s), 1 + s, b, lambda d, s=s, it=it: it + (1 + s + d) // G)
                for l in range(HEADS - 3, HEADS):
                    frame(n0 + l, l, b, lambda d, l=l: (l + d) // G)
                n = n0 + HEADS - 1
                if b + 1 == B:
                    normalise(0, 0)
                output_lo(n, 1)
                if b + 1 == B:
                    normalise(1, 1)
                add_projection(n, 1, b, 1, 0)
                add_projection(n, 1, b, 1, 1)
            statistics(FREE, 0)

            def choose(n, par):
                dve.wait_ge(logits_set, n + 1)
                dve.sem_inc(seen, 1)
                nc.vector.max(top_v[:, par, :], logits[:, par, :]).then_inc(gate_step, 1)
                dve.wait_ge(gate_step, n * 7 + 1)
                nc.vector.tensor_scalar(gap[:, par, :], top_v[:, par, 1:2], top_v[:, par, 0:1], None,
                                        ALU.subtract).then_inc(gap_set, 1)
                nc.vector.max_index(top_i[:, par, :], top_v[:, par, :], logits[:, par, :]).then_inc(gate_step, 1)
                dve.wait_ge(gate_step, n * 7 + 2)
                nc.vector.tensor_copy(top_f[:, par, :], top_i[:, par, 0:2]).then_inc(gate_step, 1)
                dve.wait_ge(egap_set, n + 1)
                nc.vector.tensor_scalar(wsum[:, par, :], egap[:, par, :], 1.0, None, ALU.add).then_inc(gate_step, 1)
                dve.wait_ge(gate_step, n * 7 + 4)
                nc.vector.reciprocal(wtop[:, par, 0:1], wsum[:, par, :]).then_inc(gate_step, 1)
                dve.wait_ge(gate_step, n * 7 + 5)
                nc.vector.tensor_tensor(wtop[:, par, 1:2], egap[:, par, :], wtop[:, par, 0:1],
                                        ALU.mult).then_inc(gate_step, 1)
                nc.vector.tensor_scalar(coef1[:, par, :], iota8[:, :], top_f[:, par, 0:1], wtop[:, par, 0:1],
                                        ALU.is_equal, ALU.mult)
                dve.wait_ge(gate_step, n * 7 + 6)
                nc.vector.tensor_scalar(coef2[:, par, :], iota8[:, :], top_f[:, par, 1:2], wtop[:, par, 1:2],
                                        ALU.is_equal, ALU.mult).then_inc(gate_step, 1)
                dve.wait_ge(gate_step, n * 7 + 7)
                nc.vector.tensor_tensor(coef[:, par, :], coef1[:, par, :], coef2[:, par, :],
                                        ALU.add).then_inc(coef_set, 1)

            def mix(n, par, places):
                for place in places:
                    e = MIX[place]
                    if e == 0:
                        dve.wait_ge(ysum_set, n + 1)
                    if e == 1:
                        dve.wait_ge(yb_set, n + 2)
                    if e % 2 == 0:
                        dve.wait_ge(moe_mm, n * 4 + (4 * FREE + e // 2 + 1))
                    src = kv_bank(e // 2)[:, (e % 2) * O:(e % 2 + 1) * O]
                    y = (y_even, y_odd)[e % 2][:, par, :]
                    weight = coef[:, par, e:e + 1]
                    if e >= 2:
                        dve.wait_ge(mixed, n * EXPERTS + (EXPERTS + MIX.index(e - 2) + 1))
                    if e == 0:
                        last = nc.vector.tensor_scalar(y, src, weight, None, ALU.mult)
                    else:
                        last = nc.vector.scalar_tensor_tensor(y, src, weight, y_bias[:, par, :] if e == 1 else y,
                                                              ALU.mult, ALU.add)
                    last.then_inc(mixed, 1)

            def slot(n, par, ahead):
                mix(n, par, range(0, 4))
                if ahead >= 1:
                    choose(n + 1, 1 - par)
                mix(n, par, range(4, EXPERTS))
                if ahead >= 2:
                    normalise(n + 2, par)
                if ahead >= 3:
                    statistics(n + 3, 1 - par)

            dve.sem_inc(mixed, EXPERTS)
            choose(0, 0)
            with dve.Fori(0, B * NT // 2 - 2) as it:
                slot(it * 2, 0, 3)
                slot(it * 2 + 1, 1, 3)
            for ahead in range(3, -1, -1):
                n = B * NT - 1 - ahead
                slot(n, n % 2, ahead)


_INS = ['L0_attn_x', 'L0_attn_wq', 'L0_attn_bq', 'L0_attn_wkv', 'L0_attn_bkv', 'L0_attn_wo', 'L0_ffn_gate_w',
        'L0_ffn_expert_w', 'L0_ffn_expert_b', 'L0_c', 'L0_wmod']
_OUTS = [((B, T, E), 'float32')]


def kernel(**inputs):
    import numpy as _np
    import concourse.bacc as _bacc
    from concourse import mybir as _mybir
    from concourse.bass_utils import run_bass_kernel_spmd as _run

    nc = _bacc.Bacc("TRN2", target_bir_lowering=False, num_devices=1)
    arrays, args = {}, []
    for name in _INS:
        a = _np.ascontiguousarray(inputs[name])
        arrays[f"in_{name}_dram"] = a
        args.append(nc.dram_tensor(f"in_{name}_dram", a.shape, _mybir.dt.from_np(a.dtype), kind="ExternalInput").ap())
    for i, (shape, dtype) in enumerate(_OUTS):
        dt = _mybir.dt.from_np(_np.dtype(dtype))
        args.append(nc.dram_tensor(f"out_{i}_dram", shape, dt, kind="ExternalOutput").ap())
    adaln_block(nc, *args)
    r = _run(nc, [arrays], core_ids=[0])
    return r.results[0]["out_0_dram"]
```

```python
from contextlib import ExitStack

import numpy as np

import concourse.bass as bass
from concourse import mybir

F32 = mybir.dt.float32
F32R = mybir.dt.float32r
BF16 = mybir.dt.bfloat16
U32 = mybir.dt.uint32
ALU = mybir.AluOpType
ACT = mybir.ActivationFunctionType
AXIS_X = mybir.AxisListType.X

P = 128
B, T, E = 2, 1024, 256
G, QPG, D = 4, 4, 128
HEADS = G * QPG
KE = E // P
NT = T // P
CH = 512
NC = T // CH
TPC = CH // P
EXPERTS, O = 8, 256
EPS = 1e-5
SCALE = float(1.0 / np.sqrt(np.float32(D)))
MASKED = -3.0e38
FREE = 2
MIX = [0, 2, 1, 3, 4, 5, 6, 7]
BANK_READ = [max(MIX.index(2 * i), MIX.index(2 * i + 1)) + 1 for i in range(EXPERTS // 2)]
SA, CA, GA, SB, CB, GB = range(6)

STEPS = [(c, j) for c in range(NC) for j in range((c + 1) * TPC)]
NS = len(STEPS)
PT = 3
LAG = 2
LAST_STEP = [max(q for q in range(NS) if STEPS[q][0] == c) for c in range(NC)]
CUTS = NS - NC
KEYS_POOL = 4
SECOND_HIDDEN = [2, 5, 6, 7]
FIRST_KEYS = 3
SECOND_MODULATION = [1, 2, 6, 7]
FIRST_TURN = 2
PIECES = []
for _i in range(NT):
    _w = (_i + 1) * P
    if _w <= CH:
        PIECES.append((_i, 0, max(_w, 2 * P), True))
    else:
        _a = CH if _w - CH >= 2 * P else _w - 2 * P
        PIECES += [(_i, 0, _a, False), (_i, _a, _w - _a, True)]
assert len(PIECES) == NS
FIRST_PIECE = [next(q for q in range(NS) if PIECES[q][0] == i) for i in range(NT)]


def score_offset(i):
    w = (i + 1) * P
    return CH - PIECES[FIRST_PIECE[i]][2] if w > CH else 0


def prob_offset(i):
    return P * i * (i + 1) // 2


PROBS = prob_offset(NT)


def cuts_before(q):
    return q - sum(s < q for s in LAST_STEP)



def position_table():
    f = np.float32
    pos = np.arange(T, dtype=f)[:, None]
    i = np.arange(0, D, 2, dtype=f)
    inv_freq = np.exp(-(np.log(f(10000.0)) * i / f(D))).astype(f)
    ang = (pos * inv_freq).astype(f)
    pe = np.zeros((T, D), f)
    pe[:, 0::2] = np.sin(ang)
    pe[:, 1::2] = np.cos(ang)
    return np.ascontiguousarray(pe.T)


def adaln_block(nc, x, wq, bq, wkv, bkv, wo, gate_w, expert_w, expert_b, c_in, wmod, out):
    ctx = ExitStack()
    with ctx:
        def sem(name):
            return ctx.enter_context(nc.semaphore(name))

        top = [-(-nc.sbuf_base // 64) * 64]

        def at(name, shape, dt, offset):
            return nc.alloc_sbuf_tensor_at(name, shape, dt, offset=offset)

        def sb(name, shape, dt=F32):
            size = int(np.prod(shape[1:])) * (2 if dt == BF16 else 4)
            offset = top[0]
            top[0] = -(-(offset + size) // 32) * 32
            assert top[0] <= nc.sbuf_usable_end, (name, top[0], nc.sbuf_usable_end)
            return at(name, shape, dt, offset)

        def here():
            return top[0]

        h_at = here()
        h_hi = sb("h_hi", [P, KE, B * T], F32R)
        h_lo = sb("h_lo", [P, KE, B * T], F32R)
        kv_at = here()
        k_hi = sb("k_hi", [P, G, T], F32R)
        k_lo = sb("k_lo", [P, G, T], F32R)
        v_hi = sb("v_hi", [P, NT - 1, G, D], F32R)
        v_lo = sb("v_lo", [P, NT - 1, G, D], F32R)
        v_whole = sb("v_whole", [P, NC, G, D])
        acc_at = here()
        acc = sb("acc", [P, B * NT, E])
        p_at = here()
        probs = [sb(f"probs{i}", [P, PROBS]) for i in range(2)]
        pt_at = here()
        pt_hi = sb("pt_hi", [P, PT, CH], F32R)
        pt_lo = sb("pt_lo", [P, PT, CH], F32R)
        pt_whole = sb("pt_whole", [P, P])
        q_at = here()
        q_hi, q_lo = zip(*[(sb(f"q_hi{i}", [P, T], F32R), sb(f"q_lo{i}", [P, T], F32R)) for i in range(2)])
        raw = sb("raw", [P, 2, CH])
        o_at = here()
        o_hi, o_lo = zip(*[(sb(f"o_hi{c}", [P, CH], F32R), sb(f"o_lo{c}", [P, CH], F32R)) for c in range(NC)])
        wq_raw = sb("wq_raw", [P, KE, D])
        wq_at = here()
        wq_hi = [sb(f"wq_hi{i}", [P, KE, D], F32R) for i in range(2)]
        wq_lo = [sb(f"wq_lo{i}", [P, KE, D], F32R) for i in range(2)]
        wo_raw = sb("wo_raw", [P, E])
        wo_hi = [sb(f"wo_hi{i}", [P, E], F32R) for i in range(2)]
        wo_lo = [sb(f"wo_lo{i}", [P, E], F32R) for i in range(2)]
        pos = sb("pos", [P, T])
        v_bias = sb("v_bias", [P, CH])
        ident = sb("ident", [P, P])
        k_whole = sb("k_whole", [P, G, P])
        mask = sb("mask", [P, P], BF16)
        qk_bias = sb("qk_bias", [P, HEADS + G])
        silu_c = sb("silu_c", [P, KE, B])
        modt = sb("modt", [P, 4, KE, B])
        gate_t = sb("gate_t", [P, KE, EXPERTS])
        neg_half = sb("neg_half", [P, NT])
        neg_max = sb("neg_max", [P, 2, NT])
        sums = sb("sums", [P, 2, NT])
        rsum = sb("rsum", [P, 2, NT])
        iota8 = sb("iota8", [P, EXPERTS])

        stats = at("stats", [P, NT, 6], F32, pt_at)
        mv = at("mv", [P, NT, 2], F32, pt_at + 4 * NT * 6)
        var_eps = sb("var_eps", [P, NT])
        rstd = sb("rstd", [P, NT])

        xs = acc
        v_at = kv_at + 32768
        wmod_sb = at("wmod_sb", [P, KE, 6 * E], F32, v_at)
        bias_rows = at("bias_rows", [HEADS + G, D], F32, v_at + 16384)
        c_rows = at("c_rows", [B, E], F32, v_at + 17408)
        gate_rows = at("gate_rows", [EXPERTS, E], F32, v_at + 18432)
        vb_row = at("vb_row", [1, CH], F32, v_at + 20480)
        ones_row = at("ones_row", [1, P], F32, v_at + 22528)
        sig_tmp = at("sig_tmp", [P, 3, KE * B], F32, v_at + 23552)
        h1_raw = at("h1_raw", [P, 2, CH], F32, o_at + 4096)
        wkv_raw = at("wkv_raw", [P, KE, G, 2, D], F32, q_at)
        wv_hi = at("wv_hi", [P, KE, G, D], F32R, q_at + 8192)
        wv_lo = at("wv_lo", [P, KE, G, D], F32R, q_at + 12288)
        wk_hi = at("wk_hi", [P, KE, G, D], F32R, p_at)
        wk_lo = at("wk_lo", [P, KE, G, D], F32R, p_at + 4096)
        x_again = at("x_again", [P, B * NT, E], F32, h_at)
        we_raw = at("we_raw", [P, EXPERTS, KE, E], F32, h_at + 16384)
        we_hi = at("we_hi", [P, KE, EXPERTS, O], F32R, kv_at)
        we_lo = at("we_lo", [P, KE, EXPERTS, O], F32R, kv_at + 16384)
        gmod_w = at("gmod_w", [P, KE, 2, E], F32, q_at)
        gmod = at("gmod", [P, B, 2, E], F32, wq_at)
        g_sign = at("g_sign", [P, 2, E], F32, h_at + 8192)
        g_size = at("g_size", [P, 2, E], F32, h_at + 8192 + 2048)
        silu_b = at("silu_b", [P, KE, B, P], F32, q_at + 4096)
        ebias = at("ebias", [EXPERTS, O], F32, q_at + 4096 + 2048)
        moe_top = [p_at]

        def moe(name, shape, dt=F32):
            offset = moe_top[0]
            moe_top[0] += -(-int(np.prod(shape[1:])) * 4 // 32) * 32
            assert moe_top[0] <= p_at + 8 * PROBS
            return at(name, shape, dt, offset)

        xn2 = moe("xn2", [P, 2, E])
        h2 = moe("h2", [P, 2, KE, P])
        h2_hi = [moe(f"h2_hi{i}", [P, KE, P], F32R) for i in range(2)]
        h2_lo = [moe(f"h2_lo{i}", [P, KE, P], F32R) for i in range(2)]
        st2 = moe("st2", [P, 2, 6])
        mv2 = moe("mv2", [P, 2, 2])
        ve2 = moe("ve2", [P, 2, 1])
        rs2 = moe("rs2", [P, 2, 1])
        logits = moe("logits", [P, 2, EXPERTS])
        top_v = moe("top_v", [P, 2, 8])
        top_i = moe("top_i", [P, 2, 8], U32)
        top_f = moe("top_f", [P, 2, 2])
        gap = moe("gap", [P, 2, 1])
        egap = moe("egap", [P, 2, 1])
        wsum = moe("wsum", [P, 2, 1])
        wtop = moe("wtop", [P, 2, 2])
        coef1 = moe("coef1", [P, 2, EXPERTS])
        coef2 = moe("coef2", [P, 2, EXPERTS])
        coef = moe("coef", [P, 2, EXPERTS])
        assert moe_top[0] <= p_at + 4 * PROBS
        coef_t = moe("coef_t", [EXPERTS, 2, P])
        y_bias = moe("y_bias", [P, 2, O])
        y_even = moe("y_even", [P, 2, O])
        y_odd = moe("y_odd", [P, 2, O])
        y_sum = moe("y_sum", [P, 2, O])
        y_out = moe("y_out", [P, 2, O])

        ps_s = ctx.enter_context(nc.psum_tensor("ps_s", [P, 2, T], F32))
        ps_t = ctx.enter_context(nc.psum_tensor("ps_t", [P, 2, CH], F32))
        ps_o = ctx.enter_context(nc.psum_tensor("ps_o", [P, CH], F32))
        ps_m = ctx.enter_context(nc.psum_tensor("ps_m", [P, CH], F32))

        def kv_bank(u):
            return ps_s[:, (u % 4) // 2, (u % 2) * CH:(u % 2 + 1) * CH]

        def raw_of(u):
            return raw[:, u % 2, :]

        x_in = [sem(f"x_in{i}") for i in range(NC + B - 1)]
        c_in_set, small_in, pos_in, wkv_in = sem("c_in_set"), sem("small_in"), sem("pos_in"), sem("wkv_in")
        wmod_in = [sem(f"wmod_in{i}") for i in range(2)]
        c_t, agg_step, xn1_set = sem("c_t"), sem("agg_step"), sem("xn1_set")
        const_set, pool_step, dve_step = sem("const_set"), sem("pool_step"), sem("dve_step")
        rows_t, rows_used, rows_set = sem("rows_t"), sem("rows_used"), sem("rows_set")
        sig_exp, silu_set = sem("sig_exp"), sem("silu_set")
        modt_mm, modt_set, vb_mm, vb_set = sem("modt_mm"), sem("modt_set"), sem("vb_mm"), sem("vb_set")
        var_set, rstd_set, xn_set = sem("var_set"), sem("rstd_set"), sem("xn_set")
        ht_mm, ht_raw, ht_hi, ht_lo = [[sem(f"{name}{b}") for b in range(B)]
                                       for name in ("ht_mm", "ht_raw", "ht_hi", "ht_lo")]
        wkv_hi_set, wkv_lo_set = sem("wkv_hi_set"), sem("wkv_lo_set")
        kv_mm, kv_raw, kv_hi, k_cut, v_cut = sem("kv_mm"), sem("kv_raw"), sem("kv_hi"), sem("k_cut"), sem("v_cut")
        shift_set, k_scaled = sem("shift_set"), sem("k_scaled")
        acc_zero = sem("acc_zero")
        wq_in, wo_in = sem("wq_in"), sem("wo_in")
        wq_cut, wo_cut, wq_hi_set, wo_hi_set = sem("wq_cut"), sem("wo_cut"), sem("wq_hi_set"), sem("wo_hi_set")
        q_mm, q_raw, q_hi_set, q_lo_set = sem("q_mm"), sem("q_raw"), sem("q_hi_set"), sem("q_lo_set")
        masked = sem("masked")
        s_mm, max_set, exp_set = sem("s_mm"), sem("max_set"), sem("exp_set")
        t_mm, pt_hi_set, pt_lo_set, pv_mm = sem("t_mm"), sem("pt_hi_set"), sem("pt_lo_set"), sem("pv_mm")
        o_hi_set, o_lo_set = sem("o_hi_set"), sem("o_lo_set")
        rsum_set, y_mm, y_add = sem("rsum_set"), sem("y_mm"), sem("y_add")
        we_in, gmod_in = sem("we_in"), sem("gmod_in")
        gmod_step = sem("gmod_step")
        we_t, we_hi_set, we_lo_set = sem("we_t"), sem("we_hi_set"), sem("we_lo_set")
        silu_b_set, gmod_mm, gmod_set = sem("silu_b_set"), sem("gmod_mm"), sem("gmod_set")
        x_again_in = [sem(f"x_again_in{b}") for b in range(B)]
        xga_set, x1_set, ln_step, ve2_set, rs2_set = (sem("xga_set"), sem("x1_set"), sem("ln_step"),
                                                      sem("ve2_set"), sem("rs2_set"))
        xn2_set, h2_t, h2_set, h2_hi_set, h2_lo_set = (
            sem("xn2_set"), sem("h2_t"), sem("h2_set"), sem("h2_hi_set"), sem("h2_lo_set"))
        gate_mm, logits_set, gate_step, gap_set, egap_set = (
            sem("gate_mm"), sem("logits_set"), sem("gate_step"), sem("gap_set"), sem("egap_set"))
        coef_set, coef_mm, coef_t_set, yb_mm, yb_set = (
            sem("coef_set"), sem("coef_mm"), sem("coef_t_set"), sem("yb_mm"), sem("yb_set"))
        moe_mm, mixed, ysum_set, ysc_set, yout_set = (
            sem("moe_mm"), sem("mixed"), sem("ysum_set"), sem("ysc_set"), sem("yout_set"))
        seen, seen_pool = sem("seen"), sem("seen_pool")
        out_done = [sem(f"out_done{i}") for i in range(2)]

        pos_dram = nc.inline_tensor(position_table(), "position_table").ap()
        x_tiles = x.rearrange("b (n p) e -> p (b n) e", p=P)
        out_tiles = out.rearrange("b (n p) e -> p (b n) e", p=P)
        wq_h = wq.rearrange("(k p) (h d) -> p k h d", p=P, d=D)
        wo_h = wo.rearrange("(h d) e -> d h e", d=D)
        wkv_v = wkv.rearrange("(k p) n -> p k n", p=P)
        bkv_v = bkv.rearrange("(g two d) -> two g d", g=G, two=2)
        wmod_v = wmod.rearrange("(k p) (m e) -> p k m e", p=P, e=E)
        we_v = expert_w.rearrange("x (h p) d -> p x h d", p=P)

        block = ctx.enter_context(nc.Block())

        @block.sync
        def _(sp):
            sp.dma_start(c_rows[:, :], c_in).then_inc(c_in_set, 16)
            for c in range(NC):
                tiles = slice(c * TPC, (c + 1) * TPC)
                sp.dma_start(xs[:, tiles, :], x_tiles[:, tiles, :]).then_inc(x_in[c], 16)
            sp.dma_start(wmod_sb[:, :, 0:2 * E].rearrange("p k (m e) -> p k m e", e=E),
                         wmod_v[:, :, SA:CA + 1, :]).then_inc(wmod_in[0], 16)
            sp.dma_start(wkv_raw[:, :, :, :, :].rearrange("p k g two d -> p k (g two d)"), wkv_v).then_inc(wkv_in, 16)
            sp.dma_start(pos[:, :], pos_dram).then_inc(pos_in, 16)
            sp.dma_start(wmod_sb[:, :, 3 * E:5 * E].rearrange("p k (m e) -> p k m e", e=E),
                         wmod_v[:, :, SB:CB + 1, :]).then_inc(wmod_in[1], 16)
            for b in range(1, B):
                tiles = slice(b * NT, (b + 1) * NT)
                sp.dma_start(xs[:, tiles, :], x_tiles[:, tiles, :]).then_inc(x_in[NC + b - 1], 16)

            def load_head(n, r, g):
                if not (isinstance(n, int) and n == 0):
                    sp.wait_ge(wq_cut, n)
                sp.dma_start(wq_raw[:, :, :], wq_h[:, :, bass.ds(r + g * QPG, 1), :]
                             .rearrange("p k h d -> p k (h d)")).then_inc(wq_in, 16)
                if not (isinstance(n, int) and n == 0):
                    sp.wait_ge(wo_cut, n)
                sp.dma_start(wo_raw[:, :], wo_h[:, bass.ds(r + g * QPG, 1), :]
                             .rearrange("d h e -> d (h e)")).then_inc(wo_in, 16)

            for b in range(B):
                for g in range(G):
                    load_head(b * HEADS + g, 0, g)
                with sp.Fori(1, QPG) as r:
                    for g in range(G):
                        load_head(r * G + (b * HEADS + g), r, g)
                if b + 1 < B:
                    sp.wait_ge(s_mm, NT * (HEADS - 1))
                    sp.dma_start(wkv_raw[:, :, :, :, :].rearrange("p k g two d -> p k (g two d)"),
                                 wkv_v).then_inc(wkv_in, 16)

            sp.wait_ge(q_mm, NC * B * HEADS)
            sp.wait_ge(s_mm, NT * (B * HEADS - 1))
            for i, m in enumerate((GA, GB)):
                sp.dma_start(gmod_w[:, :, i, :], wmod_v[:, :, m, :]).then_inc(gmod_in, 16)
            sp.dma_start(ebias[:, :], expert_b).then_inc(gmod_in, 16)
            sp.dma_start(we_raw[:, :, :, :], we_v).then_inc(we_in, 16)
            for b in range(B):
                if b == 1:
                    sp.wait_ge(gmod_set, B)
                sp.dma_start(x_again[:, b * NT:(b + 1) * NT, :],
                             x_tiles[:, b * NT:(b + 1) * NT, :]).then_inc(x_again_in[b], 16)

            def store(n, par):
                sp.wait_ge(yout_set, n + 1)
                sp.dma_start(out_tiles[:, bass.ds(n, 1), :].rearrange("p n e -> p (n e)"),
                             y_out[:, par, :]).then_inc(out_done[par], 16)

            for i in range(2):
                sp.sem_inc(out_done[i], 16)
            with sp.Fori(0, B * NT // 2 - 1) as it:
                for par in range(2):
                    store(it * 2 + par, par)
            for par in range(2):
                store(B * NT - 2 + par, par)
            for i in range(2):
                sp.wait_ge(out_done[i], 16 * (B * NT // 2 + 1))

        @block.gpsimd
        def _(pool):
            pool.memset(ident[:, :], 0.0).then_inc(pool_step, 1)
            pool.memset(mask[:, :], 0.0).then_inc(pool_step, 1)
            pool.wait_ge(pool_step, 2)
            pool.affine_select(out=ident[:, :], in_=ident[:, :], compare_op=ALU.not_equal, fill=1.0, base=0,
                               pattern=[[-1, P]], channel_multiplier=1).then_inc(const_set, 1)
            pool.affine_select(out=mask[:, :], in_=mask[:, :], compare_op=ALU.is_ge, fill=MASKED, base=0,
                               pattern=[[-1, P]], channel_multiplier=1).then_inc(const_set, 1)
            pool.memset(ones_row[:, :], 1.0).then_inc(const_set, 1)
            pool.memset(neg_half[:, :], -0.5).then_inc(const_set, 1)
            pool.iota(iota8[:, :], pattern=[[1, EXPERTS]], base=0, channel_multiplier=0,
                      allow_small_or_imprecise_dtypes=True).then_inc(const_set, 1)
            pool.wait_ge(const_set, 4)

            def inverse_deviations(lo, hi, count):
                pool.wait_ge(var_set, count)
                pool.tensor_tensor(rstd[:, lo:hi], var_eps[:, lo:hi], neg_half[:, lo:hi],
                                   ALU.pow).then_inc(rstd_set, 1)

            for c in range(NC):
                inverse_deviations(c * TPC, (c + 1) * TPC, c + 1)

            def cut_wkv(b):
                for i, (hi, lo) in enumerate(((wk_hi, wk_lo), (wv_hi, wv_lo))):
                    for k in range(KE):
                        pool.wait_ge(wkv_hi_set, 4 * b + 2 * i + k + 1)
                        pool.tensor_tensor(lo[:, k, :, :], wkv_raw[:, k, :, i, :], hi[:, k, :, :].bitcast(F32),
                                           ALU.subtract).then_inc(wkv_lo_set, 1)

            def clear_sums(b):
                pool.wait_ge(ht_mm[b], NC * KE)
                pool.memset(acc[:, b * NT:(b + 1) * NT, :], 0.0).then_inc(acc_zero, 1)

            def keys_lo():
                for u in range(KEYS_POOL):
                    c, g = divmod(u, G)
                    part = slice(c * CH, (c + 1) * CH)
                    pool.wait_ge(kv_hi, u + 1)
                    pool.tensor_tensor(k_lo[:, g, part], raw_of(u), k_hi[:, g, part].bitcast(F32),
                                       ALU.subtract).then_inc(k_cut, 1)
                pool.wait_ge(xn_set, NT)
                inverse_deviations(0, NT, NC + 1)

            def values_lo(b):
                for j in range(NT):
                    pool.wait_ge(kv_hi, 16 * b + G * NC + j + 1)
                    if j + 1 == NT:
                        pool.sem_inc(v_cut, 1)
                        continue
                    pool.tensor_tensor(v_lo[:, j, :, :].rearrange("p g d -> p (g d)"), raw_of(G * NC + j),
                                       v_hi[:, j, :, :].rearrange("p g d -> p (g d)").bitcast(F32),
                                       ALU.subtract).then_inc(v_cut, 1)

            def second_hidden_lo():
                for u in range(NC * KE):
                    c, k = divmod(u, KE)
                    part = slice(T + c * CH, T + (c + 1) * CH)
                    pool.wait_ge(ht_hi[1], u + 1)
                    pool.tensor_tensor(h_lo[:, k, part], h1_raw[:, u % 2, :], h_hi[:, k, part].bitcast(F32),
                                       ALU.subtract).then_inc(ht_lo[1], 1)

            def cut_wq(n, par):
                pool.wait_ge(wq_in, (n + 1) * 16)
                if not (isinstance(n, int) and n < 2):
                    pool.wait_ge(q_mm, n * NC - 2)
                pool.sem_inc(seen_pool, 1)
                pool.tensor_scalar(wq_hi[par][:, :, :], wq_raw[:, :, :], 1.0, 1.0, ALU.mult,
                                   ALU.mult).then_inc(wq_hi_set, 1)
                pool.wait_ge(wq_hi_set, n + 1)
                pool.tensor_tensor(wq_lo[par][:, :, :], wq_raw[:, :, :], wq_hi[par][:, :, :].bitcast(F32),
                                   ALU.subtract).then_inc(wq_cut, 1)

            def cut_wo(n, par):
                pool.wait_ge(wo_in, (n + 1) * 16)
                if not (isinstance(n, int) and n < 2):
                    pool.wait_ge(y_mm, n * 4 - 4)
                pool.sem_inc(seen_pool, 1)
                pool.tensor_scalar(wo_hi[par][:, :], wo_raw[:, :], 1.0, 1.0, ALU.mult,
                                   ALU.mult).then_inc(wo_hi_set, 1)
                pool.wait_ge(wo_hi_set, n + 1)
                pool.tensor_tensor(wo_lo[par][:, :], wo_raw[:, :], wo_hi[par][:, :].bitcast(F32),
                                   ALU.subtract).then_inc(wo_cut, 1)

            def queries_lo(n, par, c):
                part = slice(c * CH, (c + 1) * CH)
                pool.wait_ge(q_hi_set, n * NC + (c + 1))
                pool.tensor_tensor(q_lo[par][:, part], raw[:, c, :], q_hi[par][:, part].bitcast(F32),
                                   ALU.subtract).then_inc(q_lo_set, 1)

            def frame(n, l):
                par = l % 2
                nxt, nxt2 = l + 1 < HEADS, l + 2 < HEADS
                if nxt:
                    queries_lo(n + 1, 1 - par, 1)
                if isinstance(n, int) and n == 0:
                    second_hidden_lo()
                if nxt2:
                    cut_wq(n + 2, par)
                if nxt:
                    cut_wo(n + 1, 1 - par)
                if nxt2:
                    queries_lo(n + 2, par, 0)

            for b in range(B):
                n0 = b * HEADS
                cut_wkv(b)
                cut_wq(n0, 0)
                if b == 0:
                    keys_lo()
                cut_wq(n0 + 1, 1)
                values_lo(b)
                queries_lo(n0 + 1, 1, 0)
                cut_wo(n0, 0)
                clear_sums(b)
                frame(n0, 0)
                with pool.Fori(0, (HEADS - 4) // G) as it:
                    for s in range(G):
                        frame(it * G + (n0 + 1 + s), 1 + s)
                for l in range(HEADS - 3, HEADS):
                    frame(n0 + l, l)

            def row(n):
                return acc[:, bass.ds(n, 1), :].rearrange("p n e -> p (n e)")

            def residual(n, b):
                pool.tensor_tensor(row(n), row(n), gmod[:, b, 0, :], ALU.mult).then_inc(xga_set, 1)
                pool.wait_ge(xga_set, n + 1)
                pool.sem_inc(seen_pool, 1)
                pool.tensor_tensor(row(n), row(n), x_again[:, bass.ds(n, 1), :].rearrange("p n e -> p (n e)"),
                                   ALU.add).then_inc(x1_set, 1)

            def inverse_deviation(n, par):
                pool.wait_ge(ve2_set, n + 1)
                pool.tensor_tensor(rs2[:, par, :], ve2[:, par, :], neg_half[:, 0:1], ALU.pow).then_inc(rs2_set, 1)

            def hidden_lo(n, par):
                pool.wait_ge(h2_hi_set, n + 1)
                pool.tensor_tensor(h2_lo[par][:, :, :], h2[:, par, :, :], h2_hi[par][:, :, :].bitcast(F32),
                                   ALU.subtract).then_inc(h2_lo_set, 1)

            def finish(n, b, par, use):
                pool.wait_ge(out_done[par], use * 16 + 16)
                pool.wait_ge(mixed, (n + 2) * EXPERTS)
                pool.tensor_tensor(y_sum[:, par, :], y_even[:, par, :], y_odd[:, par, :], ALU.add).then_inc(ysum_set, 1)
                pool.wait_ge(ysum_set, n + (FREE + 1))
                pool.tensor_tensor(y_sum[:, par, :], y_sum[:, par, :], gmod[:, b, 1, :], ALU.mult).then_inc(ysc_set, 1)
                pool.wait_ge(ysc_set, n + 1)
                pool.sem_inc(seen_pool, 1)
                pool.tensor_tensor(y_out[:, par, :], y_sum[:, par, :], row(n), ALU.add).then_inc(yout_set, 1)

            def slot(n, l, b, use):
                par = l % 2
                last = b + 1 == B
                if not (last and l + 2 >= NT):
                    inverse_deviation(n + 2, par)
                if not last:
                    residual(n + NT, b + 1)
                if not (last and l + 1 >= NT):
                    hidden_lo(n + 1, 1 - par)
                if l > 0:
                    finish(n - 1, b, 1 - par, use - 1 if par == 0 else use)
                elif b > 0:
                    finish(n - 1, b - 1, 1, use - 1)

            pool.sem_inc(ysum_set, FREE)
            pool.wait_ge(gmod_set, 1)
            pool.wait_ge(x_again_in[0], 16)
            with pool.Fori(0, NT) as n:
                residual(n, 0)
            for i in range(FREE):
                inverse_deviation(i, i)
            hidden_lo(0, 0)
            pool.wait_ge(y_add, 4 * B * HEADS)
            pool.wait_ge(x_again_in[1], 16)
            pool.wait_ge(gmod_set, B)
            for b in range(B):
                n0, u0 = b * NT, b * NT // 2
                slot(n0, 0, b, u0)
                slot(n0 + 1, 1, b, u0)
                with pool.Fori(1, NT // 2 - 1) as it:
                    slot(it * 2 + n0, 2, b, it + u0)
                    slot(it * 2 + (n0 + 1), 3, b, it + u0)
                slot(n0 + NT - 2, NT - 2, b, u0 + NT // 2 - 1)
                slot(n0 + NT - 1, NT - 1, b, u0 + NT // 2 - 1)
            finish(B * NT - 1, B - 1, 1, B * NT // 2 - 1)

        @block.tensor
        def _(pe):
            def product(out_ap, a, b, start, stop):
                nc.tensor.matmul(out_ap, a[1], b[0], start=start, stop=False)
                nc.tensor.matmul(out_ap, a[0], b[1], start=False, stop=False)
                return nc.tensor.matmul(out_ap, a[0], b[0], start=False, stop=stop)

            pe.wait_ge(const_set, 4)
            pe.wait_ge(c_in_set, 16)
            nb = HEADS + G
            for k in range(KE):
                last = pe.transpose(kv_bank(0)[:, B * k:B * (k + 1)], c_rows[:, k * P:(k + 1) * P],
                                    ident[0:B, 0:B])
            last.then_inc(c_t, 1)

            def modulate(pair):
                pe.wait_ge(wmod_in[pair], 16)
                for i, m in enumerate(((SA, CA), (SB, CB))[pair]):
                    for et in range(KE):
                        at_col = (i * KE + et) * B
                        for k in range(KE):
                            last = pe.matmul((kv_bank(2), ps_m)[pair][:, at_col:at_col + B],
                                             wmod_sb[:, k, m * E + et * P:m * E + (et + 1) * P], silu_c[:, k, :],
                                             start=k == 0, stop=k == KE - 1)
                last.then_inc(modt_mm, 1)

            def turn_normalised(u):
                c, k = divmod(u, KE)
                pe.wait_ge(xn_set, TPC * (c + 1))
                if u >= 2:
                    pe.wait_ge(ht_raw[0], u - 1)
                for i in range(TPC):
                    last = pe.transpose(ps_t[:, u % 2, i * P:(i + 1) * P],
                                        xs[:, c * TPC + i, k * P:(k + 1) * P], ident[:, :])
                last.then_inc(ht_mm[0], 1)

            def turn_second(u):
                c, k = divmod(u, KE)
                pe.wait_ge(xn1_set, TPC * (c + 1))
                if u == 0:
                    pe.wait_ge(q_raw, 4)
                else:
                    pe.wait_ge(ht_raw[1], u)
                if SECOND_HIDDEN[u] > 8:
                    pe.wait_ge(y_add, 1)
                for i in range(TPC):
                    last = pe.transpose(ps_m[:, i * P:(i + 1) * P],
                                        xs[:, NT + c * TPC + i, k * P:(k + 1) * P], ident[:, :])
                last.then_inc(ht_mm[1], 1)

            pe.wait_ge(silu_set, 1)
            modulate(0)
            for u in range(NC * KE):
                turn_normalised(u)
            pe.wait_ge(small_in, 4 * 16)
            pe.transpose(ps_o[:, 0:nb], bias_rows[:, :], ident[0:nb, 0:nb])
            for k in range(KE):
                last = pe.transpose(ps_o[:, 64 + EXPERTS * k:64 + EXPERTS * (k + 1)],
                                    gate_rows[:, k * P:(k + 1) * P], ident[0:EXPERTS, 0:EXPERTS])
            last.then_inc(rows_t, 1)

            def queries(n, par, b, c, bank=ps_m):
                pe.wait_ge(wq_cut, n + 1)
                tokens = slice(b * T + c * CH, b * T + (c + 1) * CH)
                for k in range(KE):
                    last = product(bank[:, :], (wq_hi[par][:, k, :], wq_lo[par][:, k, :]),
                                   (h_hi[:, k, tokens], h_lo[:, k, tokens]), k == 0, k == KE - 1)
                last.then_inc(q_mm, 1)

            def score_piece(n, par, g, q, first, at_start=False):
                i, c0, w, ends = PIECES[q]
                whole = i == 0 and not at_start
                if i in ((0, TPC) if at_start else (1, TPC)) and q == FIRST_PIECE[i]:
                    pe.wait_ge(q_lo_set, n * NC + (i // TPC + 1))
                if q == FIRST_PIECE[i] and not (first and i < 2):
                    pe.wait_ge(exp_set, n * NT + (i - 1))
                rows = slice(i * P, (i + 1) * P)
                col = score_offset(i) + c0
                keys = slice(c0, c0 + w)
                if whole:
                    last = nc.tensor.matmul(ps_s[:, 0, 0:P], raw[:, 0, 0:P], k_whole[:, g, :], start=True, stop=True)
                else:
                    last = product(ps_s[:, i % 2, col:col + w], (q_hi[par][:, rows], q_lo[par][:, rows]),
                                   (k_hi[:, g, keys], k_lo[:, g, keys]), True, True)
                if ends:
                    last.then_inc(s_mm, 1)

            def turn_probs(n, par, q, first):
                c, j = STEPS[q]
                if j == 0:
                    pe.wait_ge(exp_set, n * NT + (c + 1) * TPC)
                if (q - 2) % NS in LAST_STEP and not (first and q < 2):
                    pe.wait_ge(pt_hi_set, n * NS + (q - 1))
                elif not (first and q < 2):
                    pe.wait_ge(pt_lo_set, n * CUTS + cuts_before(max(q - 1, 0)))
                for i in range(max(j, c * TPC), (c + 1) * TPC):
                    p0 = prob_offset(i) + j * P
                    col = (i - c * TPC) * P
                    last = pe.transpose(ps_t[:, q % 2, col:col + P], probs[par][:, p0:p0 + P], ident[:, :])
                last.then_inc(t_mm, 1)

            def weigh_values(n, g, q, first):
                c, j = STEPS[q]
                if j == 0 and not (first and c == 0):
                    pe.wait_ge(o_lo_set, n * NC + c)
                if q in LAST_STEP:
                    pe.wait_ge(pt_hi_set, n * NS + (q + 1))
                    last = nc.tensor.matmul(ps_o[:, CH - P:CH], v_whole[:, c, g, :], pt_whole[:, :],
                                            start=False, stop=True)
                else:
                    pe.wait_ge(pt_lo_set, n * CUTS + cuts_before(q + 1))
                    lo = (max(j, c * TPC) - c * TPC) * P
                    last = product(ps_o[:, lo:CH], (v_hi[:, j, g, :], v_lo[:, j, g, :]),
                                   (pt_hi[:, q % PT, lo:CH], pt_lo[:, q % PT, lo:CH]), j == 0, False)
                last.then_inc(pv_mm, 1)

            def project(n, par, c, pair):
                if pair == 0:
                    pe.wait_ge(o_lo_set, n * NC + (c + 1))
                    if c == 0:
                        pe.wait_ge(wo_cut, n + 1)
                for i in range(2):
                    rows = slice((2 * pair + i) * P, (2 * pair + i + 1) * P)
                    last = product(ps_m[:, i * E:(i + 1) * E], (o_hi[c][:, rows], o_lo[c][:, rows]),
                                   (wo_hi[par][:, :], wo_lo[par][:, :]), True, True)
                last.then_inc(y_mm, 1)

            def turn_weights(u):
                e2, k = divmod(u, KE)
                if u == 0:
                    pe.wait_ge(we_in, 16)
                    pe.wait_ge(exp_set, NT * B * HEADS)
                if u >= 2:
                    pe.wait_ge(we_lo_set, u - 1)
                for i in range(2):
                    for h in range(KE):
                        col = (i * KE + h) * P
                        last = pe.transpose(kv_bank(2 + u % 2)[:, col:col + P],
                                            we_raw[:, 2 * e2 + i, h, k * P:(k + 1) * P], ident[:, :])
                last.then_inc(we_t, 1)

            def modulation_rows(b, bank):
                pe.wait_ge(silu_b_set, 1)
                pe.wait_ge(gmod_in, 48)
                for m in range(2):
                    for k in range(KE):
                        last = pe.matmul(bank[:, m * E:(m + 1) * E], silu_b[:, k, b, :],
                                         gmod_w[:, k, m, :], start=k == 0, stop=k == KE - 1)
                last.then_inc(gmod_mm, 1)

            def turn_hidden(n, par, bank=None):
                if bank is None:
                    bank = ps_t[:, par, :]
                pe.wait_ge(xn2_set, n + 1)
                for k in range(KE):
                    last = pe.transpose(bank[:, k * P:(k + 1) * P], xn2[:, par, k * P:(k + 1) * P], ident[:, :])
                last.then_inc(h2_t, 1)

            def gate(n, par, bank=ps_o):
                pe.wait_ge(h2_set, n * KE + KE)
                if not (isinstance(n, int) and n < 2):
                    pe.wait_ge(logits_set, n)
                for k in range(KE):
                    last = pe.matmul(bank[:, 0:EXPERTS], h2[:, par, k, :], gate_t[:, k, :],
                                     start=k == 0, stop=k == KE - 1)
                last.then_inc(gate_mm, 1)

            def frame(n, l, b):
                very_last = b + 1 == B and l + 1 == HEADS
                before_last = b + 1 == B and l + 2 == HEADS
                par, g = l % 2, l % G
                prev, nxt, nxt2 = l > 0, l + 1 < HEADS, l + 2 < HEADS
                first = isinstance(n, int) and n == 0
                for q in range(NS):
                    turn_probs(n, par, q, first)
                    if q == 0 and nxt:
                        pe.wait_ge(q_raw, n * NC + 3)
                        queries(n + 1, 1 - par, b, 1)
                    if q == 10 and nxt2:
                        pe.wait_ge(y_add, n * 4 + 1)
                        if first:
                            pe.wait_ge(ht_raw[1], NC * KE)
                        queries(n + 2, par, b, 0)
                    if nxt:
                        score_piece(n + 1, 1 - par, (l + 1) % G, q, False)
                    if q == 2 and prev:
                        if nxt:
                            pe.wait_ge(q_raw, n * NC + 4)
                        else:
                            pe.wait_ge(y_add, n * 4 - 3)
                        if very_last:
                            pe.wait_ge(gmod_set, 1)
                        project(n - 1, 1 - par, 0, 1)
                    if q == 4 and prev:
                        pe.wait_ge(y_add, n * 4 - 2)
                        project(n - 1, 1 - par, 1, 0)
                    if q == 6 and prev:
                        pe.wait_ge(y_add, n * 4 - 1)
                        project(n - 1, 1 - par, 1, 1)
                    if q == 0 and prev:
                        for p in range(NS - LAG, NS):
                            weigh_values(n - 1, (l - 1) % G, p, False)
                    if q >= LAG:
                        weigh_values(n, g, q - LAG, first)
                    if first and q in SECOND_HIDDEN:
                        turn_second(SECOND_HIDDEN.index(q))
                    if b == 0 and l + 1 == HEADS and FIRST_KEYS <= q < FIRST_KEYS + G * NC:
                        keys(1, q - FIRST_KEYS)
                    if q == 8:
                        if prev:
                            pe.wait_ge(y_add, n * 4)
                        elif first:
                            pe.wait_ge(ht_raw[1], sum(s <= q for s in SECOND_HIDDEN))
                        else:
                            pe.wait_ge(q_raw, n * NC + 4)
                        project(n, par, 0, 0)
                    if q == 10 and not nxt:
                        pe.wait_ge(y_add, n * 4 + 1)
                        project(n, par, 0, 1)
                    if before_last and q == 9:
                        pe.wait_ge(y_add, n * 4 + 1)
                        modulation_rows(0, ps_m)
                    if very_last and q == 0:
                        pe.wait_ge(exp_set, NT * B * HEADS - 1)
                        modulation_rows(1, kv_bank(0))
                    if very_last and FIRST_TURN <= q < FIRST_TURN + EXPERTS // 2 * KE:
                        turn_weights(q - FIRST_TURN)
                    if very_last and q == 10:
                        turn_hidden(0, 0, kv_bank(1))
                    if very_last and q == 11:
                        pe.wait_ge(gmod_set, B)
                        gate(0, 0, kv_bank(0))

            def keys(b, u):
                c, g = divmod(u, G)
                if u == 0:
                    pe.wait_ge(wkv_lo_set, 4 * b + 2)
                if b > 0 and u in (0, 2):
                    pe.wait_ge(exp_set, NT * b * HEADS - 1 + u // 2)
                if g == 0:
                    pe.wait_ge(ht_lo[b], KE * (c + 1))
                if u >= 4:
                    pe.wait_ge(kv_raw, 16 * b + u - 3)
                tokens = slice(b * T + c * CH, b * T + (c + 1) * CH)
                for k in range(KE):
                    last = product(kv_bank(u), (wk_hi[:, k, g, :], wk_lo[:, k, g, :]),
                                   (h_hi[:, k, tokens], h_lo[:, k, tokens]), k == 0, k == KE - 1)
                last.then_inc(kv_mm, 1)

            def values(b, j):
                if j == 0:
                    pe.wait_ge(wkv_lo_set, 4 * (b + 1))
                if j >= 2:
                    pe.wait_ge(kv_raw, 16 * b + G * NC + j - 1)
                elif b == 0:
                    pe.wait_ge(ht_raw[0], NC * KE)
                else:
                    pe.wait_ge(pt_lo_set, CUTS * b * HEADS)
                    pe.wait_ge(pt_hi_set, NS * b * HEADS)
                s = b * T + j * P
                for k in range(KE):
                    w = [t[:, k, :, :].rearrange("p g d -> p (g d)") for t in (wv_hi, wv_lo)]
                    last = product(ps_t[:, j % 2, :], (h_hi[:, k, s:s + P], h_lo[:, k, s:s + P]), w,
                                   k == 0, k == KE - 1)
                last.then_inc(kv_mm, 1)

            for b in range(B):
                n0 = b * HEADS
                if b == 0:
                    for u in range(G * NC):
                        keys(0, u)
                        if u == 2:
                            pe.matmul(ps_m[:, :], ones_row[0:1, :], vb_row[0:1, :], start=True,
                                      stop=True).then_inc(vb_mm, 1)
                        if u == 4:
                            pe.wait_ge(vb_set, 1)
                            modulate(1)
                    pe.wait_ge(modt_set, 2)
                else:
                    for q in range(NS - LAG, NS):
                        weigh_values(n0 - 1, G - 1, q, False)
                    pe.wait_ge(y_add, n0 * 4 - 2)
                queries(n0, 0, b, 0)
                values(b, 0)
                if b > 0:
                    pe.wait_ge(o_lo_set, n0 * NC)
                queries(n0, 0, b, 1, ps_o)
                pe.wait_ge(q_raw, n0 * NC + 1)
                if b > 0:
                    project(n0 - 1, 1, 1, 0)
                values(b, 1)
                if b > 0:
                    pe.wait_ge(y_add, n0 * 4 - 1)
                    project(n0 - 1, 1, 1, 1)
                values(b, 2)
                pe.wait_ge(k_cut, G * NC * (b + 1))
                for q in range(NS):
                    score_piece(n0, 0, 0, q, b == 0, True)
                    i = PIECES[q][0]
                    if PIECES[q][3] and i + 3 < NT:
                        values(b, i + 3)
                    if PIECES[q][3] and i == 5:
                        if b > 0:
                            pe.wait_ge(y_add, n0 * 4)
                        queries(n0 + 1, 1, b, 0)
                pe.wait_ge(v_cut, NT * (b + 1))
                pe.wait_ge(q_raw, n0 * NC + 2)
                frame(n0, 0, b)
                with pe.Fori(0, (HEADS - 4) // G) as it:
                    for s in range(G):
                        frame(it * G + (n0 + 1 + s), 1 + s, b)
                for l in range(HEADS - 3, HEADS):
                    frame(n0 + l, l, b)
            def turn_coef(n, par):
                pe.wait_ge(coef_set, n + 1)
                pe.wait_ge(yb_set, n + 1)
                pe.transpose(ps_m[0:EXPERTS, 0:P], coef[:, par, :], ident[:, :]).then_inc(coef_mm, 1)

            def mix_bias(n, par):
                pe.wait_ge(coef_t_set, n + 1)
                pe.matmul(ps_m[:, 0:O], coef_t[:, par, :], ebias[:, :], start=True, stop=True).then_inc(yb_mm, 1)

            def experts(n, par, e2):
                if e2 == 0:
                    pe.wait_ge(h2_lo_set, n + 1)
                pe.wait_ge(mixed, n * EXPERTS + BANK_READ[e2])
                for k in range(KE):
                    w = [t[:, k, 2 * e2:2 * e2 + 2, :].rearrange("p x o -> p (x o)") for t in (we_hi, we_lo)]
                    last = product(kv_bank(e2), (h2_hi[par][:, k, :], h2_lo[par][:, k, :]), w, k == 0, k == KE - 1)
                last.then_inc(moe_mm, 1)

            def slot(n, par, more):
                experts(n, par, 0)
                turn_coef(n, par)
                if more:
                    turn_hidden(n + 1, 1 - par)
                experts(n, par, 1)
                mix_bias(n, par)
                if more:
                    gate(n + 1, 1 - par)
                experts(n, par, 2)
                experts(n, par, 3)

            pe.sem_inc(moe_mm, FREE * EXPERTS // 2)
            n = B * HEADS - 1
            for q in range(NS - LAG, NS):
                weigh_values(n, G - 1, q, False)
            pe.wait_ge(we_lo_set, EXPERTS // 2 * KE)
            pe.wait_ge(logits_set, 1)
            experts(0, 0, 0)
            pe.wait_ge(y_add, n * 4 + 2)
            project(n, 1, 1, 0)
            experts(0, 0, 1)
            pe.wait_ge(y_add, n * 4 + 3)
            project(n, 1, 1, 1)
            turn_hidden(1, 1)
            experts(0, 0, 2)
            pe.wait_ge(y_add, n * 4 + 4)
            turn_coef(0, 0)
            gate(1, 1)
            mix_bias(0, 0)
            experts(0, 0, 3)
            with pe.Fori(0, B * NT // 4 - 1) as it:
                for i in range(4):
                    slot(it * 4 + (i + 1), (i + 1) % 2, True)
            for n in range(B * NT - 3, B * NT):
                slot(n, n % 2, n + 1 < B * NT)

        @block.scalar
        def _(act):
            def keep_hi(dst, src, scale=1.0):
                return nc.scalar.activation(dst, src, ACT.Copy, scale=scale)

            act.wait_ge(rows_used, 1)
            nc.scalar.activation(sig_tmp[:, 0, :], silu_c[:, :, :].rearrange("p k b -> p (k b)"), ACT.Exp,
                                 scale=-1.0).then_inc(sig_exp, 1)

            act.dma_start(bias_rows[0:HEADS, :], bq.rearrange("(h d) -> h d", d=D)).then_inc(small_in, 16)
            act.dma_start(bias_rows[HEADS:HEADS + G, :], bkv_v[0, :, :]).then_inc(small_in, 16)
            act.dma_start(vb_row[0:1, :].rearrange("o (g d) -> o g d", d=D), bkv_v[1:2, :, :]).then_inc(small_in, 16)
            act.dma_start(gate_rows[:, :], gate_w).then_inc(small_in, 16)

            def cut_weights(b, i, halves=range(KE)):
                act.wait_ge(wkv_in, 16 * (b + 1))
                for k in halves:
                    keep_hi((wk_hi, wv_hi)[i][:, k, :, :], wkv_raw[:, k, :, i, :]).then_inc(wkv_hi_set, 1)

            def hidden(b, u):
                c, k = divmod(u, KE)
                src = ps_t[:, u % 2, :] if b == 0 else ps_m[:, :]
                mid = (raw, h1_raw)[b][:, u % 2, :]
                act.wait_ge(ht_mm[b], u + 1)
                if u >= 2:
                    act.wait_ge(ht_lo[b], u - 1)
                nc.scalar.activation(mid, src, ACT.Identity, scale=modt[:, 1, k, b:b + 1],
                                     bias=modt[:, 0, k, b:b + 1]).then_inc(ht_raw[b], 1)
                act.wait_ge(ht_raw[b], u + 1)
                keep_hi(h_hi[:, k, b * T + c * CH:b * T + (c + 1) * CH], mid).then_inc(ht_hi[b], 1)

            def normalise_second(first_tile):
                act.wait_ge(shift_set, 1)
                for i in range(first_tile, first_tile + 2):
                    row = xs[:, NT + i, :]
                    nc.scalar.activation(row, row, ACT.Identity, scale=rstd[:, i:i + 1],
                                         bias=var_eps[:, i:i + 1]).then_inc(xn1_set, 1)

            cut_weights(0, 0)
            act.wait_ge(modt_set, 1)
            for u in range(NC * KE):
                hidden(0, u)
            cut_weights(0, 1)

            def exponentials(n, par, i):
                w = (i + 1) * P
                act.wait_ge(max_set, n * NT + (i + 1))
                col = score_offset(i)
                nc.scalar.activation(probs[par][:, prob_offset(i):prob_offset(i) + w], ps_s[:, i % 2, col:col + w],
                                     ACT.Exp, bias=neg_max[:, par, i:i + 1],
                                     accum_out=sums[:, par, i:i + 1]).then_inc(exp_set, 1)

            def probs_hi(n, q, first):
                c, j = STEPS[q]
                act.wait_ge(t_mm, n * NS + (q + 1))
                if not (first and q < PT):
                    act.wait_ge(pv_mm, n * NS + (q - PT + 1))
                lo = (max(j, c * TPC) - c * TPC) * P
                dst = pt_whole[:, :] if q in LAST_STEP else pt_hi[:, q % PT, lo:CH]
                keep_hi(dst, ps_t[:, q % 2, lo:CH]).then_inc(pt_hi_set, 1)

            def output_hi(n, c, first):
                act.wait_ge(pv_mm, n * NS + (LAST_STEP[c] + 1))
                if not first:
                    act.wait_ge(y_mm, n * 4 + (2 * c - 2))
                keep_hi(o_hi[c][:, :], ps_o[:, :]).then_inc(o_hi_set, 1)

            def queries_hi(n, par, c):
                act.wait_ge(q_raw, n * NC + (c + 1))
                keep_hi(q_hi[par][:, c * CH:(c + 1) * CH], raw[:, c, :]).then_inc(q_hi_set, 1)

            def frame(n, l, b):
                par = l % 2
                prev, nxt, nxt2 = l > 0, l + 1 < HEADS, l + 2 < HEADS
                first = isinstance(n, int) and n == 0
                turning = b + 1 < B and l + 1 == HEADS
                for q in range(NS):
                    if turning and q == 0:
                        act.wait_ge(t_mm, n * NS)
                        cut_weights(1, 0, (0,))
                    if q == 1 and prev:
                        output_hi(n - 1, 1, isinstance(n, int) and n == 1)
                    probs_hi(n, q, first)
                    if q == LAST_STEP[0] + LAG:
                        output_hi(n, 0, first)
                    if q == (1 if turning else 0):
                        if turning:
                            cut_weights(1, 0, (1,))
                        exponentials(n, par, NT - 1)
                    if q == 0 and nxt:
                        exponentials(n + 1, 1 - par, 0)
                    if q > 1 and nxt and PIECES[q - 1][3]:
                        exponentials(n + 1, 1 - par, PIECES[q - 1][0])
                    if q == 1 and nxt:
                        queries_hi(n + 1, 1 - par, 1)
                    if q == 11 and nxt2:
                        queries_hi(n + 2, par, 0)
                    if b + 1 == B and l + 1 == HEADS:
                        if FIRST_TURN <= q < FIRST_TURN + EXPERTS // 2 * KE:
                            weights_hi(q - FIRST_TURN)
                        if q == 10:
                            hidden2(0, 0, 0, kv_bank(1))
                    if first and q in SECOND_HIDDEN:
                        hidden(1, SECOND_HIDDEN.index(q))
                    if first and q + 1 == NS:
                        act.wait_ge(ht_lo[1], NC * KE)
                    if turning:
                        if q == 2:
                            cut_weights(1, 1)
                        if FIRST_KEYS < q <= FIRST_KEYS + G * NC:
                            upper(1, q - FIRST_KEYS - 1)

            def upper(b, u):
                act.wait_ge(kv_raw, 16 * b + u + 1)
                if u < G * NC:
                    c, g = divmod(u, G)
                    scale = SCALE
                    if b == 0 and u < KEYS_POOL:
                        keep_hi(raw_of(u), raw_of(u), SCALE).then_inc(k_scaled, 1)
                        act.wait_ge(k_scaled, u + 1)
                        scale = 1.0
                    if c == 0:
                        keep_hi(k_whole[:, g, :], raw_of(u)[:, 0:P], scale)
                    keep_hi(k_hi[:, g, c * CH:(c + 1) * CH], raw_of(u), scale).then_inc(kv_hi, 1)
                else:
                    j = u - G * NC
                    if j + 1 < NT:
                        last = keep_hi(v_hi[:, j, :, :].rearrange("p g d -> p (g d)"), raw_of(u))
                    if j % TPC + 1 == TPC:
                        last = keep_hi(v_whole[:, j // TPC, :, :].rearrange("p g d -> p (g d)"), raw_of(u))
                    last.then_inc(kv_hi, 1)

            def hidden2(n, b, par, bank=None):
                if bank is None:
                    bank = ps_t[:, par, :]
                act.wait_ge(h2_t, n + 1)
                for k in range(KE):
                    nc.scalar.activation(h2[:, par, k, :], bank[:, k * P:(k + 1) * P], ACT.Identity,
                                         scale=modt[:, 3, k, b:b + 1], bias=modt[:, 2, k, b:b + 1]).then_inc(h2_set, 1)
                act.wait_ge(h2_set, n * KE + KE)
                act.wait_ge(moe_mm, (n + 1) * 4)
                keep_hi(h2_hi[par][:, :, :], h2[:, par, :, :]).then_inc(h2_hi_set, 1)

            def read_logits(n, par, bank=ps_o):
                act.wait_ge(gate_mm, n + 1)
                nc.scalar.activation(logits[:, par, :], bank[:, 0:EXPERTS], ACT.Copy).then_inc(logits_set, 1)

            def gap_exponential(n, par):
                act.wait_ge(gap_set, n + 1)
                nc.scalar.activation(egap[:, par, :], gap[:, par, :], ACT.Exp).then_inc(egap_set, 1)

            def turned_coef(n, par):
                act.wait_ge(coef_mm, n + 1)
                nc.scalar.activation(coef_t[:, par, :], ps_m[0:EXPERTS, 0:P], ACT.Copy).then_inc(coef_t_set, 1)

            def mix_bias(n, par):
                act.wait_ge(yb_mm, n + 1)
                nc.scalar.activation(y_bias[:, par, :], ps_m[:, 0:O], ACT.Copy).then_inc(yb_set, 1)

            def weights_hi(u):
                e2, k = divmod(u, KE)
                act.wait_ge(we_t, u + 1)
                keep_hi(we_hi[:, k, 2 * e2:2 * e2 + 2, :].rearrange("p x o -> p (x o)"),
                        kv_bank(2 + u % 2)).then_inc(we_hi_set, 1)

            for b in range(B):
                n0 = b * HEADS
                if b == 0:
                    for u in range(G * NC):
                        upper(0, u)
                        if u >= 6:
                            normalise_second((u - 6) * 2)
                else:
                    output_hi(n0 - 1, 1, False)
                act.wait_ge(wkv_lo_set, 4 * (b + 1))
                for i in range(NC):
                    queries_hi(n0, 0, i)
                    upper(b, G * NC + i)
                upper(b, G * NC + 2)
                for i in range(NT - 1):
                    exponentials(n0, 0, i)
                    if i + 3 < NT:
                        upper(b, G * NC + i + 3)
                    elif i + 3 == NT:
                        queries_hi(n0 + 1, 1, 0)
                    if b == 0 and 1 <= i < 3:
                        normalise_second(2 * i + 2)
                frame(n0, 0, b)
                with act.Fori(0, (HEADS - 4) // G) as it:
                    for s in range(G):
                        frame(it * G + (n0 + 1 + s), 1 + s, b)
                for l in range(HEADS - 3, HEADS):
                    frame(n0 + l, l, b)
            def slot(n, l, b):
                more = l + 1 < NT or b + 1 < B
                turned_coef(n, l % 2)
                if more:
                    hidden2(n + 1, b if l + 1 < NT else b + 1, (l + 1) % 2)
                mix_bias(n, l % 2)
                if more:
                    read_logits(n + 1, (l + 1) % 2)
                    gap_exponential(n + 1, (l + 1) % 2)

            read_logits(0, 0, kv_bank(0))
            output_hi(B * HEADS - 1, 1, False)
            gap_exponential(0, 0)
            act.sem_inc(yb_set, 1)
            hidden2(1, 0, 1)
            turned_coef(0, 0)
            mix_bias(0, 0)
            read_logits(1, 1)
            gap_exponential(1, 1)
            for b in range(B):
                n0 = b * NT
                first_slot = 1 if b == 0 else 0
                with act.Fori(0, NT // 2 - 1) as it:
                    for i in range(2):
                        slot(it * 2 + (n0 + first_slot + i), first_slot + i, b)
                for l in range(NT - 2 + first_slot, NT):
                    slot(n0 + l, l, b)

        @block.vector
        def _(dve):
            dve.wait_ge(c_t, 1)
            flat_c = silu_c[:, :, :].rearrange("p k b -> p (k b)")
            nc.vector.tensor_copy(flat_c, kv_bank(0)[:, 0:KE * B]).then_inc(rows_used, 1)
            dve.wait_ge(sig_exp, 1)
            nc.vector.tensor_scalar(sig_tmp[:, 1, :], sig_tmp[:, 0, :], 1.0, None, ALU.add).then_inc(dve_step, 1)
            dve.wait_ge(dve_step, 1)
            nc.vector.reciprocal(sig_tmp[:, 2, :], sig_tmp[:, 1, :]).then_inc(dve_step, 1)
            dve.wait_ge(dve_step, 2)
            nc.vector.tensor_tensor(flat_c, flat_c, sig_tmp[:, 2, :], ALU.mult).then_inc(silu_set, 1)

            def row_stats(b, lo, hi):
                for i in range(lo, hi):
                    nc.vector.bn_stats(stats[:, i, :], xs[:, b * NT + i, :]).then_inc(ln_step, 1)

            def deviations(b, lo, hi):
                for i in range(lo, hi):
                    dve.wait_ge(ln_step, b * NT + i + 1)
                    nc.vector.bn_aggr(mv[:, i, :], stats[:, i, :]).then_inc(agg_step, 1)
                dve.wait_ge(agg_step, b * NT + hi)
                nc.vector.tensor_scalar(var_eps[:, lo:hi], mv[:, lo:hi, 1], EPS, None, ALU.add).then_inc(var_set, 1)

            def modulation_columns(pair):
                dve.wait_ge(modt_mm, pair + 1)
                for i in range(2):
                    cols = slice(i * KE * B, (i + 1) * KE * B)
                    last = nc.vector.tensor_scalar(modt[:, 2 * pair + i, :, :].rearrange("p k b -> p (k b)"),
                                                   (kv_bank(2), ps_m)[pair][:, cols], float(i), None, ALU.add)
                last.then_inc(modt_set, 1)

            def normalise_first(c):
                dve.wait_ge(rstd_set, c + 1)
                for i in range(c * TPC, (c + 1) * TPC):
                    nc.vector.tensor_scalar(xs[:, i, :], xs[:, i, :], mv[:, i, 0:1], rstd[:, i:i + 1],
                                            ALU.subtract, ALU.mult).then_inc(xn_set, 1)

            for c in range(NC):
                dve.wait_ge(x_in[c], 16)
                row_stats(0, c * TPC, (c + 1) * TPC)
                if c > 0:
                    normalise_first(c - 1)
                deviations(0, c * TPC, (c + 1) * TPC)
            modulation_columns(0)
            normalise_first(NC - 1)
            for u in range(NC * KE):
                c, k = divmod(u, KE)
                part = slice(c * CH, (c + 1) * CH)
                dve.wait_ge(ht_hi[0], u + 1)
                nc.vector.tensor_tensor(h_lo[:, k, part], raw[:, u % 2, :], h_hi[:, k, part].bitcast(F32),
                                        ALU.subtract).then_inc(ht_lo[0], 1)
            dve.wait_ge(rows_t, 1)
            nc.vector.tensor_copy(qk_bias[:, :], ps_o[:, 0:HEADS + G])
            nc.vector.tensor_copy(gate_t[:, :, :].rearrange("p k e -> p (k e)"),
                                  ps_o[:, 64:64 + KE * EXPERTS]).then_inc(rows_set, 1)

            def kv_raw_part(b, u):
                if 2 <= u < G * NC:
                    dve.wait_ge(k_cut, G * NC * b + u - 1)
                elif G * NC <= u < G * NC + NC:
                    dve.wait_ge(q_lo_set, b * HEADS * NC + (u - G * NC + 1))
                elif u >= G * NC + NC:
                    dve.wait_ge(v_cut, NT * b + u - G * NC - 1)
                elif b == 0:
                    dve.wait_ge(ht_lo[0], NC * KE)
                else:
                    dve.wait_ge(q_lo_set, b * HEADS * NC)
                dve.wait_ge(kv_mm, 16 * b + u + 1)
                if u < G * NC:
                    c, g = divmod(u, G)
                    last = nc.vector.scalar_tensor_tensor(raw_of(u), kv_bank(u),
                                                          qk_bias[:, HEADS + g:HEADS + g + 1],
                                                          pos[:, c * CH:(c + 1) * CH], ALU.add, ALU.add)
                else:
                    last = nc.vector.tensor_tensor(raw_of(u), ps_t[:, u % 2, :], v_bias[:, :], ALU.add)
                last.then_inc(kv_raw, 1)

            def second_shift():
                dve.wait_ge(rstd_set, NC + 1)
                nc.vector.scalar_tensor_tensor(var_eps[:, :], mv[:, :, 0], -1.0, rstd[:, :], ALU.mult,
                                               ALU.mult).then_inc(shift_set, 1)

            def keys_lo(b, u):
                c, g = divmod(u, G)
                part = slice(c * CH, (c + 1) * CH)
                if b == 0 and u == KEYS_POOL:
                    dve.wait_ge(k_cut, KEYS_POOL)
                dve.wait_ge(kv_hi, 16 * b + u + 1)
                nc.vector.scalar_tensor_tensor(k_lo[:, g, part], raw_of(u), SCALE, k_hi[:, g, part].bitcast(F32),
                                               ALU.mult, ALU.subtract).then_inc(k_cut, 1)

            def mask_tile(n, i):
                col = score_offset(i) + i * P
                own = ps_s[:, i % 2, col:col + P]
                dve.wait_ge(s_mm, n * NT + (i + 1))
                nc.vector.tensor_tensor(own, own, mask[:, :], ALU.add).then_inc(masked, 1)

            def maxima(n, par, i):
                w = (i + 1) * P
                col = score_offset(i)
                dve.wait_ge(masked, n * NT + (i + 1))
                nc.vector.tensor_reduce(neg_max[:, par, i:i + 1], ps_s[:, i % 2, col:col + w], AXIS_X, ALU.max,
                                        negate=True).then_inc(max_set, 1)

            def probs_lo(n, q):
                c, j = STEPS[q]
                if q in LAST_STEP:
                    return
                dve.wait_ge(pt_hi_set, n * NS + (q + 1))
                lo = (max(j, c * TPC) - c * TPC) * P
                nc.vector.tensor_tensor(pt_lo[:, q % PT, lo:CH], ps_t[:, q % 2, lo:CH],
                                        pt_hi[:, q % PT, lo:CH].bitcast(F32), ALU.subtract).then_inc(pt_lo_set, 1)

            def output_lo(n, c):
                dve.wait_ge(o_hi_set, n * NC + (c + 1))
                nc.vector.tensor_tensor(o_lo[c][:, :], ps_o[:, :], o_hi[c][:, :].bitcast(F32),
                                        ALU.subtract).then_inc(o_lo_set, 1)

            def queries_raw(n, g, b, c, r, after=None, bank=ps_m):
                head = r + g * QPG
                bias = qk_bias[:, head:head + 1] if isinstance(head, int) else qk_bias[:, bass.ds(head, 1)]
                if after:
                    dve.wait_ge(*after)
                else:
                    dve.wait_ge(q_lo_set, n * NC + (c - 1))
                dve.wait_ge(q_mm, n * NC + (c + 1))
                nc.vector.scalar_tensor_tensor(raw[:, c, :], bank[:, :], bias, pos[:, c * CH:(c + 1) * CH],
                                               ALU.add, ALU.add).then_inc(q_raw, 1)

            def queries_lo(n, par, c):
                part = slice(c * CH, (c + 1) * CH)
                dve.wait_ge(q_hi_set, n * NC + (c + 1))
                nc.vector.tensor_tensor(q_lo[par][:, part], raw[:, c, :], q_hi[par][:, part].bitcast(F32),
                                        ALU.subtract).then_inc(q_lo_set, 1)

            def sum_inverse(n, par, c):
                part = slice(c * TPC, (c + 1) * TPC)
                dve.wait_ge(exp_set, n * NT + (c + 1) * TPC)
                nc.vector.reciprocal(rsum[:, par, part], sums[:, par, part]).then_inc(rsum_set, 1)

            def add_projection(n, par, b, c, pair):
                dve.wait_ge(y_mm, n * 4 + (2 * c + pair + 1))
                if pair == 0:
                    dve.wait_ge(rsum_set, n * NC + (c + 1))
                for i in range(2):
                    tile = c * TPC + 2 * pair + i
                    row = acc[:, b * NT + tile, :]
                    last = nc.vector.scalar_tensor_tensor(row, ps_m[:, i * E:(i + 1) * E],
                                                          rsum[:, par, tile:tile + 1], row, ALU.mult, ALU.add)
                last.then_inc(y_add, 1)

            def frame(n, l, b, r):
                par, g = l % 2, l % G
                prev, nxt, nxt2 = l > 0, l + 1 < HEADS, l + 2 < HEADS
                turning = b + 1 < B and l + 1 == HEADS
                for q in range(NS):
                    unit = None
                    if turning and FIRST_KEYS < q <= FIRST_KEYS + G * NC:
                        unit = q - FIRST_KEYS - 1
                        if q + 1 < NS:
                            kv_raw_part(1, unit)
                    tile = PIECES[q][0] if nxt and PIECES[q][3] else None
                    if tile is not None and 0 < q < 11:
                        mask_tile(n + 1, tile)
                    if q == 1 and prev:
                        output_lo(n - 1, 1)
                    if tile == 1:
                        maxima(n + 1, 1 - par, tile)
                    probs_lo(n, q)
                    if turning and q == 1:
                        maxima(n, par, NT - 1)
                    if unit is not None and q + 1 == NS:
                        kv_raw_part(1, unit)
                    if tile is not None and q in (0, 11):
                        mask_tile(n + 1, tile)
                    if q == LAST_STEP[0] + LAG:
                        output_lo(n, 0)
                    if q == 10 and nxt2:
                        queries_raw(n + 2, (l + 2) % G, b, 0, r(2))
                    if tile is not None and tile != 1 and not (b + 1 < B and l + 2 == HEADS and q + 1 == NS):
                        maxima(n + 1, 1 - par, tile)
                    if q == 7:
                        sum_inverse(n, par, 0)
                    if q == 9:
                        sum_inverse(n, par, 1)
                    if q == 0 and nxt:
                        queries_raw(n + 1, (l + 1) % G, b, 1, r(1))
                    if q == 2 and prev:
                        add_projection(n - 1, 1 - par, b, 0, 1)
                    if q == 4 and prev:
                        add_projection(n - 1, 1 - par, b, 1, 0)
                    if q == 6 and prev:
                        add_projection(n - 1, 1 - par, b, 1, 1)
                    if q == 8:
                        if l == 0:
                            dve.wait_ge(acc_zero, b + 1)
                        add_projection(n, par, b, 0, 0)
                    if q == 11 and not nxt:
                        add_projection(n, par, b, 0, 1)
                    if unit is not None:
                        keys_lo(1, unit)
                    if b + 1 == B and l + 2 == HEADS:
                        if q == 1:
                            repeat_silu()
                        if q == 10:
                            modulation_part(0, 0)
                            modulation_part(0, 1)
                        if q == 11:
                            modulation_part(0, 2)
                            modulation_part(0, 3)
                    if b + 1 == B and l + 1 == HEADS:
                        if q in SECOND_MODULATION:
                            modulation_part(1, SECOND_MODULATION.index(q))
                        if FIRST_TURN <= q < FIRST_TURN + EXPERTS // 2 * KE:
                            weights_lo(q - FIRST_TURN)
                        if 6 <= q < 8:
                            statistics(q - 6, q - 6)
                        if 8 <= q < 10:
                            normalise(q - 8, q - 8)
                        if q == 10:
                            statistics(2, 0)

            def repeat_silu():
                for k in range(KE):
                    for b in range(B):
                        last = nc.vector.tensor_scalar(silu_b[:, k, b, :], ident[:, :], 0.0, silu_c[:, k, b:b + 1],
                                                       ALU.mult, ALU.add)
                last.then_inc(silu_b_set, 1)

            def weights_lo(u):
                e2, k = divmod(u, KE)
                dve.wait_ge(we_hi_set, u + 1)
                hi, lo = [t[:, k, 2 * e2:2 * e2 + 2, :].rearrange("p x o -> p (x o)") for t in (we_hi, we_lo)]
                nc.vector.tensor_tensor(lo, kv_bank(2 + u % 2), hi.bitcast(F32), ALU.subtract).then_inc(we_lo_set, 1)

            def modulation_part(b, i):
                g = (ps_m[:, :], kv_bank(0))[b]
                sign, size = [t[:, :, :].rearrange("p m e -> p (m e)") for t in (g_sign, g_size)]
                if i == 0:
                    dve.wait_ge(gmod_mm, b + 1)
                    if b > 0:
                        dve.wait_ge(gmod_set, b)
                    nc.vector.tensor_scalar(sign, g, 0.0, 2.0, ALU.is_ge, ALU.mult).then_inc(gmod_step, 1)
                elif i == 1:
                    nc.vector.tensor_scalar(size, g, -1.0, 0.25, ALU.mult, ALU.max).then_inc(gmod_step, 1)
                elif i == 2:
                    dve.wait_ge(gmod_step, 3 * b + 2)
                    nc.vector.tensor_tensor(size, g, size, ALU.max).then_inc(gmod_step, 1)
                else:
                    dve.wait_ge(gmod_step, 3 * b + 3)
                    nc.vector.scalar_tensor_tensor(gmod[:, b, :, :].rearrange("p m e -> p (m e)"), sign, -1.0, size,
                                                   ALU.add, ALU.mult).then_inc(gmod_set, 1)

            def row(n):
                return acc[:, bass.ds(n, 1), :].rearrange("p n e -> p (n e)")

            def statistics(n, par):
                if not (isinstance(n, int) and n < 2):
                    dve.wait_ge(xn2_set, n - 1)
                dve.wait_ge(x1_set, n + 1)
                nc.vector.bn_stats(st2[:, par, :], row(n)).then_inc(ln_step, 1)
                dve.wait_ge(ln_step, n * 2 + (B * NT + 1))
                dve.sem_inc(seen, 1)
                nc.vector.bn_aggr(mv2[:, par, :], st2[:, par, :]).then_inc(ln_step, 1)
                dve.wait_ge(ln_step, n * 2 + (B * NT + 2))
                nc.vector.tensor_scalar(ve2[:, par, :], mv2[:, par, 1:2], EPS, None, ALU.add).then_inc(ve2_set, 1)

            def normalise(n, par):
                if not (isinstance(n, int) and n < 2):
                    dve.wait_ge(h2_t, n - 1)
                dve.wait_ge(rs2_set, n + 1)
                nc.vector.tensor_scalar(xn2[:, par, :], row(n), mv2[:, par, 0:1], rs2[:, par, :],
                                        ALU.subtract, ALU.mult).then_inc(xn2_set, 1)

            for b in range(B):
                n0 = b * HEADS
                nk = G * NC
                if b == 0:
                    dve.wait_ge(pos_in, 16)
                    dve.wait_ge(rows_set, 1)
                    for u in range(nk):
                        kv_raw_part(0, u)
                        if u == 0:
                            dve.wait_ge(x_in[NC], 16)
                            dve.wait_ge(xn_set, NT)
                        if u < 2:
                            row_stats(1, u * TPC, (u + 1) * TPC)
                        if u == 2:
                            deviations(1, 0, NT)
                        if u == 3:
                            dve.wait_ge(vb_mm, 1)
                            nc.vector.tensor_copy(v_bias[:, :], ps_m[:, :]).then_inc(vb_set, 1)
                        if u == 5:
                            modulation_columns(1)
                        if u == 6:
                            second_shift()
                        if u > KEYS_POOL:
                            keys_lo(0, u - 1)
                    keys_lo(0, nk - 1)
                    dve.wait_ge(vb_set, 1)
                else:
                    output_lo(n0 - 1, 1)
                queries_raw(n0, 0, b, 0, 0, after=(k_cut, nk * (b + 1)))
                queries_lo(n0, 0, 0)
                kv_raw_part(b, nk)
                queries_raw(n0, 0, b, 1, 0, after=(k_cut, nk * (b + 1)), bank=ps_o)
                if b > 0:
                    add_projection(n0 - 1, 1, b - 1, 1, 0)
                queries_lo(n0, 0, 1)
                kv_raw_part(b, nk + 1)
                if b > 0:
                    add_projection(n0 - 1, 1, b - 1, 1, 1)
                kv_raw_part(b, nk + 2)
                for i in range(NT):
                    mask_tile(n0, i)
                    maxima(n0, 0, i)
                    if i + 3 < NT:
                        kv_raw_part(b, nk + i + 3)
                    elif i + 3 == NT:
                        queries_raw(n0 + 1, 1, b, 0, 0, after=(v_cut, NT * (b + 1)))
                frame(n0, 0, b, lambda d: d // G)
                with dve.Fori(0, (HEADS - 4) // G) as it:
                    for s in range(G):
                        frame(it * G + (n0 + 1 + s), 1 + s, b, lambda d, s=s, it=it: it + (1 + s + d) // G)
                for l in range(HEADS - 3, HEADS):
                    frame(n0 + l, l, b, lambda d, l=l: (l + d) // G)
            def choose(n, par):
                dve.wait_ge(logits_set, n + 1)
                dve.sem_inc(seen, 1)
                nc.vector.max(top_v[:, par, :], logits[:, par, :]).then_inc(gate_step, 1)
                dve.wait_ge(gate_step, n * 7 + 1)
                nc.vector.tensor_scalar(gap[:, par, :], top_v[:, par, 1:2], top_v[:, par, 0:1], None,
                                        ALU.subtract).then_inc(gap_set, 1)
                nc.vector.max_index(top_i[:, par, :], top_v[:, par, :], logits[:, par, :]).then_inc(gate_step, 1)
                dve.wait_ge(gate_step, n * 7 + 2)
                nc.vector.tensor_copy(top_f[:, par, :], top_i[:, par, 0:2]).then_inc(gate_step, 1)
                dve.wait_ge(egap_set, n + 1)
                nc.vector.tensor_scalar(wsum[:, par, :], egap[:, par, :], 1.0, None, ALU.add).then_inc(gate_step, 1)
                dve.wait_ge(gate_step, n * 7 + 4)
                nc.vector.reciprocal(wtop[:, par, 0:1], wsum[:, par, :]).then_inc(gate_step, 1)
                dve.wait_ge(gate_step, n * 7 + 5)
                nc.vector.tensor_tensor(wtop[:, par, 1:2], egap[:, par, :], wtop[:, par, 0:1],
                                        ALU.mult).then_inc(gate_step, 1)
                nc.vector.tensor_scalar(coef1[:, par, :], iota8[:, :], top_f[:, par, 0:1], wtop[:, par, 0:1],
                                        ALU.is_equal, ALU.mult)
                dve.wait_ge(gate_step, n * 7 + 6)
                nc.vector.tensor_scalar(coef2[:, par, :], iota8[:, :], top_f[:, par, 1:2], wtop[:, par, 1:2],
                                        ALU.is_equal, ALU.mult).then_inc(gate_step, 1)
                dve.wait_ge(gate_step, n * 7 + 7)
                nc.vector.tensor_tensor(coef[:, par, :], coef1[:, par, :], coef2[:, par, :],
                                        ALU.add).then_inc(coef_set, 1)

            def mix(n, par, places):
                for place in places:
                    e = MIX[place]
                    if e == 0:
                        dve.wait_ge(ysum_set, n + 1)
                    if e == 1:
                        dve.wait_ge(yb_set, n + 2)
                    if e % 2 == 0:
                        dve.wait_ge(moe_mm, n * 4 + (4 * FREE + e // 2 + 1))
                    src = kv_bank(e // 2)[:, (e % 2) * O:(e % 2 + 1) * O]
                    y = (y_even, y_odd)[e % 2][:, par, :]
                    weight = coef[:, par, e:e + 1]
                    if e >= 2:
                        dve.wait_ge(mixed, n * EXPERTS + (EXPERTS + MIX.index(e - 2) + 1))
                    if e == 0:
                        last = nc.vector.tensor_scalar(y, src, weight, None, ALU.mult)
                    else:
                        last = nc.vector.scalar_tensor_tensor(y, src, weight, y_bias[:, par, :] if e == 1 else y,
                                                              ALU.mult, ALU.add)
                    last.then_inc(mixed, 1)

            def slot(n, par, ahead):
                if ahead >= 2:
                    normalise(n + 2, par)
                if ahead >= 3:
                    statistics(n + 3, 1 - par)
                mix(n, par, range(0, 4))
                if ahead >= 1:
                    choose(n + 1, 1 - par)
                mix(n, par, range(4, EXPERTS))

            dve.sem_inc(mixed, EXPERTS)
            n = B * HEADS - 1
            output_lo(n, 1)
            choose(0, 0)
            add_projection(n, 1, B - 1, 1, 0)
            add_projection(n, 1, B - 1, 1, 1)
            with dve.Fori(0, B * NT // 4 - 1) as it:
                for i in range(4):
                    slot(it * 4 + i, i % 2, 3)
            for ahead in range(3, -1, -1):
                n = B * NT - 1 - ahead
                slot(n, n % 2, ahead)


_INS = ['L0_attn_x', 'L0_attn_wq', 'L0_attn_bq', 'L0_attn_wkv', 'L0_attn_bkv', 'L0_attn_wo', 'L0_ffn_gate_w',
        'L0_ffn_expert_w', 'L0_ffn_expert_b', 'L0_c', 'L0_wmod']
_OUTS = [((B, T, E), 'float32')]


def kernel(**inputs):
    import numpy as _np
    import concourse.bacc as _bacc
    from concourse import mybir as _mybir
    from concourse.bass_utils import run_bass_kernel_spmd as _run

    nc = _bacc.Bacc("TRN2", target_bir_lowering=False, num_devices=1)
    arrays, args = {}, []
    for name in _INS:
        a = _np.ascontiguousarray(inputs[name])
        arrays[f"in_{name}_dram"] = a
        args.append(nc.dram_tensor(f"in_{name}_dram", a.shape, _mybir.dt.from_np(a.dtype), kind="ExternalInput").ap())
    for i, (shape, dtype) in enumerate(_OUTS):
        dt = _mybir.dt.from_np(_np.dtype(dtype))
        args.append(nc.dram_tensor(f"out_{i}_dram", shape, dt, kind="ExternalOutput").ap())
    adaln_block(nc, *args)
    r = _run(nc, [arrays], core_ids=[0])
    return r.results[0]["out_0_dram"]
```
